# Optimizing a Trainium2 kernel written in Bass

```python
import numpy as np
import jax
import jax.numpy as jnp

def _softmax(x, axis=-1):
    return jax.nn.softmax(x, axis=axis)
def _gelu(x):
    return jax.nn.gelu(x, approximate=True)
def _silu(x):
    return jax.nn.silu(x)
def _sigmoid(x):
    return jax.nn.sigmoid(x)
def _layernorm(x, axis=-1, eps=1e-5):
    m = jnp.mean(x, axis=axis, keepdims=True)
    v = jnp.var(x, axis=axis, keepdims=True)
    return (x - m) / jnp.sqrt(v + eps)
def _scatter_add(tgt, idx, src, axis=0):
    return tgt.at[idx].add(src)
def _segment_sum(src, seg, n):
    return jax.ops.segment_sum(src, seg, n)

kernel_name = 'mk_conv_attn_hybrid_d2_conv_nchw128_3eaeef'

def setup_inputs(seed: int = 0):
    np.random.seed(seed)
    _w = jnp.asarray
    def _rec_inputs():
        import jax
        import jax.numpy as jnp
        _gk = jax.random.key(seed)
        x = -0.000929 + 1 * jax.random.normal(jax.random.fold_in(_gk, 1), (2, 128, 64, 64), jnp.float32)
        return x
    x = _rec_inputs()
    def _L0_conv_setup():
        import jax, jax.numpy as jnp
        import numpy as np
        B, DIM, H, W = (2, 128, 64, 64)
        DH, HEADS, K = (32, 4, 7)

        def _ln(x, g, b):
            mu = jnp.mean(x, -1, keepdims=True)
            var = jnp.mean((x - mu) ** 2, -1, keepdims=True)
            return (x - mu) * jax.lax.rsqrt(var + 1e-05) * g + b

        def _na2d(x, qkv_w, qkv_b, rpb, proj_w, proj_b):
            Bb, Hh, Ww, C = x.shape
            k = K
            qkv = (x @ qkv_w.T + qkv_b).reshape(Bb, Hh, Ww, 3, HEADS, DH).transpose(3, 0, 4, 1, 2, 5)
            q = qkv[0] * DH ** (-0.5)
            kt, vt = (qkv[1], qkv[2])

            def starts(n):
                return jnp.clip(jnp.arange(n) - k // 2, 0, n - k)
            nh = starts(Hh)[:, None] + jnp.arange(k)
            nw = starts(Ww)[:, None] + jnp.arange(k)
            ih = nh[:, None, :, None]
            iw = nw[None, :, None, :]
            Kw = kt[:, :, ih, iw, :]
            Vw = vt[:, :, ih, iw, :]
            attn = jnp.einsum('bnhwd,bnhwijd->bnhwij', q, Kw)
            bih = (nh - jnp.arange(Hh)[:, None] + (k - 1))[:, None, :, None]
            biw = (nw - jnp.arange(Ww)[:, None] + (k - 1))[None, :, None, :]
            attn = attn + rpb[:, bih, biw][None]
            attn = jax.nn.softmax(attn.reshape(Bb, HEADS, Hh, Ww, k * k), -1).reshape(Bb, HEADS, Hh, Ww, k, k)
            out = jnp.einsum('bnhwij,bnhwijd->bnhwd', attn, Vw)
            out = out.transpose(0, 2, 3, 1, 4).reshape(Bb, Hh, Ww, C)
            return out @ proj_w.T + proj_b
        key = jax.random.key(seed)
        ks = jax.random.split(key, 8)
        d = DIM
        w = lambda k_, sh: jax.random.normal(k_, sh, jnp.float32) * 0.02
        inp = {'x': jax.random.normal(ks[0], (B, DIM, H, W), jnp.float32)}
        inp.update(g1=jnp.ones(d), be1=jnp.zeros(d), g2=jnp.ones(d), be2=jnp.zeros(d), g3=jnp.ones(d), be3=jnp.zeros(d), g4=jnp.ones(d), be4=jnp.zeros(d))
        inp['qkv_w'] = w(ks[1], (3 * d, d))
        inp['qkv_b'] = jnp.zeros(3 * d)
        inp['rpb'] = w(ks[2], (HEADS, 2 * K - 1, 2 * K - 1))
        inp['proj_w'] = w(ks[3], (d, d))
        inp['proj_b'] = jnp.zeros(d)
        inp['w1'] = w(ks[4], (d, d))
        inp['bl1'] = jnp.zeros(d)
        inp['w2'] = w(ks[5], (d, d))
        inp['bl2'] = jnp.zeros(d)
        inp['w3'] = w(ks[6], (d, d))
        inp['bl3'] = jnp.zeros(d)
        return inp
    _L0_conv_all = _L0_conv_setup()
    _L0_conv_in = {k: v for k, v in _L0_conv_all.items() if k in ('g1', 'be1', 'g2', 'be2', 'g3', 'be3', 'g4', 'be4', 'qkv_w', 'qkv_b', 'rpb', 'proj_w', 'proj_b', 'w1', 'bl1', 'w2', 'bl2', 'w3', 'bl3', )}
    del _L0_conv_all

    def _L1_attn_setup():
        import jax, jax.numpy as jnp
        import numpy as np
        B, T, D = (4, 2048, 128)
        key = jax.random.key(seed)
        k1, k2, k3 = jax.random.split(key, 3)
        x = jax.random.normal(k1, (B, T, D), dtype=jnp.float32)
        lim = 1.0 / np.sqrt(D)
        W = jax.random.uniform(k2, (3 * D, D), dtype=jnp.float32, minval=-lim, maxval=lim)
        b = jax.random.uniform(k3, (3 * D,), dtype=jnp.float32, minval=-lim, maxval=lim)
        return {'x': x, 'W': W, 'b': b}
    _L1_attn_all = _L1_attn_setup()
    _L1_attn_in = {k: v for k, v in _L1_attn_all.items() if k in ('W', 'b', )}
    del _L1_attn_all

    def _L1_ffn_setup():
        import jax, jax.numpy as jnp
        import numpy as np
        B, N, D, C, E, K = (8, 8192, 128, 128, 8, 2)
        key = jax.random.key(seed)
        k0, k1, k2 = jax.random.split(key, 3)
        x = jax.random.normal(k0, (B, N, D), dtype=jnp.float32)
        router_w = jax.random.normal(k1, (D, E), dtype=jnp.float32) * 0.05
        router_b = jnp.zeros((E,), dtype=jnp.float32)
        expert_w = jax.random.normal(k2, (E, D, C), dtype=jnp.float32) * (1.0 / np.sqrt(D))
        expert_b = jnp.zeros((E, C), dtype=jnp.float32)
        return {'x': x, 'router_w': router_w, 'router_b': router_b, 'expert_w': expert_w, 'expert_b': expert_b}
    _L1_ffn_all = _L1_ffn_setup()
    _L1_ffn_in = {k: v for k, v in _L1_ffn_all.items() if k in ('router_w', 'router_b', 'expert_w', 'expert_b', )}
    del _L1_ffn_all

    return {
        "x": x,
        "L0_conv_g1": _L0_conv_in["g1"],
        "L0_conv_be1": _L0_conv_in["be1"],
        "L0_conv_g2": _L0_conv_in["g2"],
        "L0_conv_be2": _L0_conv_in["be2"],
        "L0_conv_g3": _L0_conv_in["g3"],
        "L0_conv_be3": _L0_conv_in["be3"],
        "L0_conv_g4": _L0_conv_in["g4"],
        "L0_conv_be4": _L0_conv_in["be4"],
        "L0_conv_qkv_w": _L0_conv_in["qkv_w"],
        "L0_conv_qkv_b": _L0_conv_in["qkv_b"],
        "L0_conv_rpb": _L0_conv_in["rpb"],
        "L0_conv_proj_w": _L0_conv_in["proj_w"],
        "L0_conv_proj_b": _L0_conv_in["proj_b"],
        "L0_conv_w1": _L0_conv_in["w1"],
        "L0_conv_bl1": _L0_conv_in["bl1"],
        "L0_conv_w2": _L0_conv_in["w2"],
        "L0_conv_bl2": _L0_conv_in["bl2"],
        "L0_conv_w3": _L0_conv_in["w3"],
        "L0_conv_bl3": _L0_conv_in["bl3"],
        "L1_attn_W": _L1_attn_in["W"],
        "L1_attn_b": _L1_attn_in["b"],
        "L1_ffn_router_w": _L1_ffn_in["router_w"],
        "L1_ffn_router_b": _L1_ffn_in["router_b"],
        "L1_ffn_expert_w": _L1_ffn_in["expert_w"],
        "L1_ffn_expert_b": _L1_ffn_in["expert_b"],
    }

def reference(x, L0_conv_g1, L0_conv_be1, L0_conv_g2, L0_conv_be2, L0_conv_g3, L0_conv_be3, L0_conv_g4, L0_conv_be4, L0_conv_qkv_w, L0_conv_qkv_b, L0_conv_rpb, L0_conv_proj_w, L0_conv_proj_b, L0_conv_w1, L0_conv_bl1, L0_conv_w2, L0_conv_bl2, L0_conv_w3, L0_conv_bl3, L1_attn_W, L1_attn_b, L1_ffn_router_w, L1_ffn_router_b, L1_ffn_expert_w, L1_ffn_expert_b):
    import jax
    import jax.numpy as jnp
    def _L0_conv_ref(x, g1, be1, g2, be2, g3, be3, g4, be4, qkv_w, qkv_b, rpb, proj_w, proj_b, w1, bl1, w2, bl2, w3, bl3):
        import jax, jax.numpy as jnp
        import numpy as np
        B, DIM, H, W = (2, 128, 64, 64)
        DH, HEADS, K = (32, 4, 7)

        def _ln(x, g, b):
            mu = jnp.mean(x, -1, keepdims=True)
            var = jnp.mean((x - mu) ** 2, -1, keepdims=True)
            return (x - mu) * jax.lax.rsqrt(var + 1e-05) * g + b

        def _na2d(x, qkv_w, qkv_b, rpb, proj_w, proj_b):
            Bb, Hh, Ww, C = x.shape
            k = K
            qkv = (x @ qkv_w.T + qkv_b).reshape(Bb, Hh, Ww, 3, HEADS, DH).transpose(3, 0, 4, 1, 2, 5)
            q = qkv[0] * DH ** (-0.5)
            kt, vt = (qkv[1], qkv[2])

            def starts(n):
                return jnp.clip(jnp.arange(n) - k // 2, 0, n - k)
            nh = starts(Hh)[:, None] + jnp.arange(k)
            nw = starts(Ww)[:, None] + jnp.arange(k)
            ih = nh[:, None, :, None]
            iw = nw[None, :, None, :]
            Kw = kt[:, :, ih, iw, :]
            Vw = vt[:, :, ih, iw, :]
            attn = jnp.einsum('bnhwd,bnhwijd->bnhwij', q, Kw)
            bih = (nh - jnp.arange(Hh)[:, None] + (k - 1))[:, None, :, None]
            biw = (nw - jnp.arange(Ww)[:, None] + (k - 1))[None, :, None, :]
            attn = attn + rpb[:, bih, biw][None]
            attn = jax.nn.softmax(attn.reshape(Bb, HEADS, Hh, Ww, k * k), -1).reshape(Bb, HEADS, Hh, Ww, k, k)
            out = jnp.einsum('bnhwij,bnhwijd->bnhwd', attn, Vw)
            out = out.transpose(0, 2, 3, 1, 4).reshape(Bb, Hh, Ww, C)
            return out @ proj_w.T + proj_b
        x = x.transpose(0, 2, 3, 1)
        r = x
        y = _ln(x, g1, be1)
        y = _na2d(y, qkv_w, qkv_b, rpb, proj_w, proj_b)
        y = _ln(y, g2, be2)
        y = y @ w1.T + bl1
        x = y + r
        r = x
        y = _ln(x, g3, be3)
        y = y @ w2.T + bl2
        y = jax.nn.relu(y)
        y = _ln(y, g4, be4)
        y = y @ w3.T + bl3
        x = y + r
        return x.transpose(0, 3, 1, 2)

    def _L1_attn_ref(x, W, b):
        import jax, jax.numpy as jnp
        import numpy as np
        B, T, D = (4, 2048, 128)
        Bx, Tx, Dx = x.shape
        qkv = (x @ W.T + b).reshape(Bx, Tx, 3, Dx)
        q, k, v = (qkv[:, :, 0], qkv[:, :, 1], qkv[:, :, 2])
        q = jax.nn.elu(q) + 1.0
        k = jax.nn.elu(k) + 1.0
        kv = jnp.einsum('bti,btj->btij', k, v)
        kv_cum = jnp.cumsum(kv, axis=1)
        k_cum = jnp.cumsum(k, axis=1)
        num = jnp.einsum('bti,btij->btj', q, kv_cum)
        den = jnp.einsum('bti,bti->bt', q, k_cum)[..., None] + 1e-06
        return num / den

    def _L1_ffn_ref(x, router_w, router_b, expert_w, expert_b):
        import jax, jax.numpy as jnp
        import numpy as np
        B, N, D, C, E, K = (8, 8192, 128, 128, 8, 2)
        router_probs = jax.nn.softmax(x @ router_w + router_b, axis=-1)
        top_p, top_i = jax.lax.top_k(router_probs, K)
        top_p = top_p / jnp.sum(top_p, axis=-1, keepdims=True)
        expert_out = jnp.einsum('bnd,edc->bnec', x, expert_w) + expert_b
        gathered = jnp.take_along_axis(expert_out, top_i[..., None], axis=2)
        return jnp.einsum('bnk,bnkc->bnc', top_p, gathered)

    def _gn(v, G=32, eps=1e-5):
        B_, C_, H_, W_ = v.shape
        g = v.reshape(B_, G, C_ // G, H_, W_)
        m = jnp.mean(g, axis=(2, 3, 4), keepdims=True)
        s = jnp.var(g, axis=(2, 3, 4), keepdims=True)
        return ((g - m) / jnp.sqrt(s + eps)).reshape(v.shape)

    def _ln_c(v, eps=1e-6):
        m = jnp.mean(v, axis=1, keepdims=True)
        s = jnp.var(v, axis=1, keepdims=True)
        return (v - m) / jnp.sqrt(s + eps)

    def _ln_t(v, eps=1e-5):
        m = jnp.mean(v, axis=-1, keepdims=True)
        s = jnp.var(v, axis=-1, keepdims=True)
        return (v - m) / jnp.sqrt(s + eps)

    def _to_tokens(v):
        B_, C_, H_, W_ = v.shape
        return v.reshape(B_, C_, H_ * W_).transpose(0, 2, 1)
    def _from_tokens(t, like):
        B_, C_, H_, W_ = like.shape
        return t.transpose(0, 2, 1).reshape(B_, C_, H_, W_)

    x = x + _L0_conv_ref(_gn(x), L0_conv_g1, L0_conv_be1, L0_conv_g2, L0_conv_be2, L0_conv_g3, L0_conv_be3, L0_conv_g4, L0_conv_be4, L0_conv_qkv_w, L0_conv_qkv_b, L0_conv_rpb, L0_conv_proj_w, L0_conv_proj_b, L0_conv_w1, L0_conv_bl1, L0_conv_w2, L0_conv_bl2, L0_conv_w3, L0_conv_bl3)
    t = _to_tokens(x)
    t = t + _L1_attn_ref(_ln_t(t), L1_attn_W, L1_attn_b)
    t = t + _L1_ffn_ref(_ln_t(t), L1_ffn_router_w, L1_ffn_router_b, L1_ffn_expert_w, L1_ffn_expert_b)
    x = _from_tokens(t, x)
    return x


_drawn_inputs = setup_inputs


def setup_inputs(seed=0):
    import zlib

    import numpy as np

    out = dict(_drawn_inputs(seed))
    spreads = {'L0_conv_g1': (1.0, 0.6),
     'L0_conv_be1': (0.0, 0.339),
     'L0_conv_g2': (1.0, 0.2),
     'L0_conv_be2': (0.0, 0.1),
     'L0_conv_g3': (1.0, 0.2),
     'L0_conv_be3': (0.0, 0.1),
     'L0_conv_g4': (1.0, 0.2),
     'L0_conv_be4': (0.0, 0.1),
     'L0_conv_qkv_b': (0.0, 0.1),
     'L0_conv_proj_b': (0.0, 0.1),
     'L0_conv_bl1': (0.0, 0.1),
     'L0_conv_bl2': (0.0, 0.1),
     'L0_conv_bl3': (0.0, 0.1),
     'L1_ffn_router_b': (0.0, 0.1),
     'L1_ffn_expert_b': (0.0, 0.1)}
    factors = {'L0_conv_rpb': 37.475}
    for name, (base, spread) in spreads.items():
        noise = np.random.default_rng([zlib.crc32(name.encode()), seed]).standard_normal(out[name].shape)
        drawn = base * np.exp(spread * noise) if base else spread * noise
        out[name] = jnp.asarray(drawn.astype(out[name].dtype))
    for name, factor in factors.items():
        out[name] = (out[name] * factor).astype(out[name].dtype)
    return out
```

```python
from contextlib import ExitStack

import numpy as np

import concourse.bass as bass
from concourse import mybir

F32 = mybir.dt.float32
BF16 = mybir.dt.bfloat16
ALU = mybir.AluOpType
ACT = mybir.ActivationFunctionType
AX_X = mybir.AxisListType.X

B, C, H, W = 2, 128, 64, 64
TOK = H * W
HEADS, DH, K = 4, 32, 7
GROUPS = 32
NE = 8
P = 128

R = K // 2
QR, QC = 4, 8
KR, KC = QR + 2 * R, QC + 2 * R
NK = KR * KC
PW = W + 2 * R
PADT = 4
YH = H + 2 * PADT
KH = H + 2 * R
CHR = 8
CHK = CHR * KC
NCH = YH // CHR
STRIPS = W // QC
NSTRIP = B * STRIPS
TILES = H // QR
PAIRS = TILES // 2
NQ = QR * QC
BLK = 512
BROWS = BLK // W
NBLK = B * TOK // BLK
T = BLK // P
FAR = -1.0e30

VEC = ["g1", "be1", "g2", "be2", "g3", "be3", "g4", "be4", "bq", "bk", "bv", "bp", "bl1", "bl3", "lbq", "lbk"]
VI = {n: i for i, n in enumerate(VEC)}
ROWS = ["bp", "bl2", "lbv"]
BIAS = ["p", "z1", "z2", "v"]


def shift(i, d):
    return i + d // 2, d % 2


def exists(j):
    return not isinstance(j, int) or 0 <= j < NBLK // 2


def wait(eng, sem, value):
    if isinstance(value, int) and value <= 0:
        return
    eng.wait_ge(sem, value)


def settle(eng, passed):
    eng.sem_inc(passed, 1)


def build(nc, x, wqkvT, wp, wpT, w123T, vecs, rows, rpb, laT, expw, rw, rb, expb, consts, out):
    ctx = ExitStack()
    with ctx:
        names = {}

        def sb(stack, name, shape, dt=F32):
            return stack.enter_context(nc.sbuf_tensor(name, shape, dt))

        def ps(stack, name, shape=(P, 512), dt=F32):
            return stack.enter_context(nc.psum_tensor(name, list(shape), dt))

        def sem(name):
            assert name not in names
            names[name] = ctx.enter_context(nc.semaphore(name))
            return names[name]

        passed = {n: sem(f"passed_{n}") for n in ("dve", "pool")}

        X = sb(ctx, "X", [P, B, TOK])
        cst = sb(ctx, "cst", [P, 4 * P])
        ident, groupavg, center, causal = (cst[:, k * P:(k + 1) * P] for k in range(4))
        halfneg = sb(ctx, "halfneg", [P, 4])
        vec = sb(ctx, "vec", [P, len(VEC)])
        row = sb(ctx, "row", [1, len(ROWS), P])
        gn_scale = sb(ctx, "gn_scale", [P, B])
        gn_bias = sb(ctx, "gn_bias", [P, B])
        res_bias = sb(ctx, "res_bias", [P, B])
        b3 = sb(ctx, "b3", [P, 1])
        WP = sb(ctx, "WP", [P, P])
        WPZ = sb(ctx, "WPZ", [P, P])
        W2 = sb(ctx, "W2", [P, P])
        W3 = sb(ctx, "W3", [P, P])
        bias3 = sb(ctx, "bias3", [96, len(BIAS), T, P], BF16)
        ones3 = sb(ctx, "ones3", [96, P], BF16)
        Y = sb(ctx, "Y", [P, B, YH, PW])

        attn_mem = ctx.enter_context(ExitStack())
        KEY = sb(attn_mem, "KEY", [P, B, KH, PW])
        WQ = sb(attn_mem, "WQ", [P, P])
        WK = sb(attn_mem, "WK", [P, P])
        WV = sb(attn_mem, "WV", [P, P])
        bq = sb(attn_mem, "bq", [P, 1])
        bk = sb(attn_mem, "bk", [P, 1])
        tab = sb(attn_mem, "tab", [P, 3, 3, NK])

        with ExitStack() as mem:
            wqkv_in = sb(mem, "wqkv_in", [P, 3, P])
            wp_in = sb(mem, "wp_in", [P, P])
            w123_in = sb(mem, "w123_in", [P, 3, P])
            w1g = sb(mem, "w1g", [P, P])
            w1c = sb(mem, "w1c", [P, P])
            w3g = sb(mem, "w3g", [P, P])
            far = sb(mem, "far", [P, 3 * NK])
            bvc = sb(mem, "bvc", [P, 1])
            bpc = sb(mem, "bpc", [P, 1])
            brow = sb(mem, "brow", [1, len(BIAS), P])
            bhi = sb(mem, "bhi", [1, 3, len(BIAS), P], BF16)
            bres = sb(mem, "bres", [1, 2, len(BIAS), P])
            stat = sb(mem, "stat", [P, B, 8, 6])
            mv = sb(mem, "mv", [P, B, 2])
            mom = sb(mem, "mom", [P, B, 2])
            gmom = sb(mem, "gmom", [P, B, 2])
            gvar = sb(mem, "gvar", [P, B])
            gsq = sb(mem, "gsq", [P, B])
            rslot = sb(mem, "rslot", [P, B, BLK])
            tstat = sb(mem, "tstat", [P, B, T, 6])
            tmv = sb(mem, "tmv", [P, B, T, 2])
            tve = sb(mem, "tve", [P, B, T])
            trs = sb(mem, "trs", [P, B, T])
            yn = sb(mem, "yn", [P, B, BLK])
            TA = [ps(mem, f"TA{i}") for i in range(B)]
            TB = [ps(mem, f"TB{i}") for i in range(B)]
            KP = [ps(mem, f"KP{i}") for i in range(B)]
            PREP = [ps(mem, f"PREP{i}") for i in range(2)]
            wq_be, wk_be, wv_be, w1_be, w3_be, wp_bv = (PREP[0][:, a:a + 1] for a in range(6))
            gsum = KP[0][:, 0:2 * B]
            w1c_ps, w3c_ps, wpz_ps = (PREP[1][:, k * P:(k + 1) * P] for k in range(3))
            row_ps = PREP[0][0:1, P:4 * P]
            cdram = nc.dram_tensor("column_bias", [3, HEADS, QC, 2 * K - 1, KC], F32, kind="Internal").ap()
            tdram = nc.dram_tensor("bias_table", [3, 3, HEADS, QR, QC, NK], F32, kind="Internal").ap()

            x_in = [sem(f"x_in{i}") for i in range(B)]
            const_in, wqkv_sem, wrest_sem = sem("const_in"), sem("wqkv_sem"), sem("wrest_sem")
            far_set, far_out = sem("far_set"), sem("far_out")
            columns_out, table_out, table_in = sem("columns_out"), sem("table_out"), sem("table_in")
            table_neg, pads_set, const_set = sem("table_neg"), sem("pads_set"), sem("const_set")
            gn_stats, gn_mean, gn_mom, gn_avg, gn_copied = (
                sem(n) for n in ("gn_stats", "gn_mean", "gn_mom", "gn_avg", "gn_copied"))
            gn_sq, gn_var, gn_rstd, gn_done = (sem(n) for n in ("gn_sq", "gn_var", "gn_rstd", "gn_done"))
            w_scaled, prep_cols, prep_mat, cols_done = (sem(n) for n in ("w_scaled", "prep_cols", "prep_mat", "cols_done"))
            w1c_done, prep_bv, bpc_done, prep_rows, rows_done, split_done, wpz_done = (
                sem(n) for n in ("w1c_done", "prep_bv", "bpc_done", "prep_rows", "rows_done", "split_done", "wpz_done"))
            r_ready, r_turned, y_stats, y_mv, y_ve, y_rstd, y_ready, y_turned, y_stored, k_made, k_stored = (
                sem(n) for n in ("r_ready", "r_turned", "y_stats", "y_mv", "y_ve", "y_rstd", "y_ready", "y_turned",
                                 "y_stored", "k_made", "k_stored"))

            block = mem.enter_context(nc.Block())

            @block.sync
            def _(sp):
                for b in range(B):
                    sp.dma_start(X[:, b, :], x[b]).then_inc(x_in[b], 16)
                sp.wait_ge(far_set, 1)
                sp.dma_start(cdram.rearrange("c h q a k -> (c h q) (a k)"), far[0:96, 0:13 * KC]).then_inc(far_out, 16)
                for part in range(3):
                    sp.dma_start(tdram.rearrange("r c h a b k -> (r c h a b k)").rearrange("(p n) -> p n", p=P)
                                 [:, part * 3 * NK:(part + 1) * 3 * NK], far[:]).then_inc(far_out, 16)
                sp.wait_ge(far_out, 64)
                for cc, c0 in enumerate((0, QC, W - QC)):
                    for qc in range(QC):
                        start = min(max(c0 + qc - R, 0), W - K)
                        at, idx = start - (c0 - R), start - (c0 + qc) + K - 1
                        sp.dma_start(cdram[cc, :, qc, :, at:at + K],
                                     rpb[:, :, idx:idx + K]).then_inc(columns_out, 16)
                sp.wait_ge(columns_out, 16 * 3 * QC)
                for rc, r0 in enumerate((0, QR, H - QR)):
                    for qr in range(QR):
                        start = min(max(r0 + qr - R, 0), H - K)
                        at, idx = start - (r0 - R), start - (r0 + qr) + K - 1
                        sp.dma_start(tdram[rc, :, :, qr, :, at * KC:(at + K) * KC].rearrange("c h q n -> (c h) q n"),
                                     cdram[:, :, :, idx:idx + K, :].rearrange("c h q a k -> (c h) q (a k)")
                                     ).then_inc(table_out, 16)
                sp.wait_ge(table_out, 16 * 3 * QR)
                for cc in range(3):
                    sp.dma_start(tab[:, cc, :, :], tdram[:, cc].rearrange("r h a b k -> (h a b) r k")).then_inc(table_in, 16)

            @block.gpsimd
            def _(pool):
                nc.gpsimd.memset(far[:], FAR).then_inc(far_set, 1)
                nc.gpsimd.memset(halfneg[:], -0.5).then_inc(const_set, 1)
                nc.gpsimd.memset(ones3[:], 1.0).then_inc(const_set, 1)
                nc.gpsimd.memset(bias3[:], 0.0).then_inc(const_set, 1)
                for b in range(B):
                    nc.gpsimd.memset(Y[:, b, 0:PADT, :], 0.0).then_inc(pads_set, 1)
                    nc.gpsimd.memset(Y[:, b, PADT + H:YH, :], 0.0).then_inc(pads_set, 1)
                    nc.gpsimd.memset(Y[:, b, PADT:PADT + H, 0:R], 0.0).then_inc(pads_set, 1)
                    nc.gpsimd.memset(Y[:, b, PADT:PADT + H, R + W:PW], 0.0).then_inc(pads_set, 1)
                    nc.gpsimd.memset(KEY[:, b, 0:R, :], 0.0).then_inc(pads_set, 1)
                    nc.gpsimd.memset(KEY[:, b, R + H:KH, :], 0.0).then_inc(pads_set, 1)
                    nc.gpsimd.memset(KEY[:, b, R:R + H, 0:R], 0.0).then_inc(pads_set, 1)
                    nc.gpsimd.memset(KEY[:, b, R:R + H, R + W:PW], 0.0).then_inc(pads_set, 1)
                pool.wait_ge(const_set, 1)
                pool.wait_ge(gn_var, 2)
                nc.gpsimd.tensor_tensor(gn_scale[:], gvar[:], halfneg[:, 0:B], ALU.pow).then_inc(gn_rstd, 1)

                def ln_rstd(i, par):
                    j, b = shift(i, par)
                    if exists(j):
                        m = B * j + b
                        wait(pool, y_ve, m + 1)
                        wait(pool, y_ready, T * (m - 1))
                        nc.gpsimd.tensor_tensor(trs[:, b, :], tve[:, b, :], halfneg[:], ALU.pow).then_inc(y_rstd, 1)

                for i in range(2):
                    for par in range(2):
                        ln_rstd(i, par)
                with pool.Fori(2, NBLK // 2) as i:
                    for par in range(2):
                        ln_rstd(i, par)

            @block.scalar
            def _(act):
                act.dma_start(cst[:], consts).then_inc(const_in, 16)
                act.dma_start(vec[:], vecs).then_inc(const_in, 16)
                act.dma_start(row[:], rows).then_inc(const_in, 16)
                act.dma_start(wqkv_in[:], wqkvT).then_inc(wqkv_sem, 16)
                act.dma_start(wp_in[:], wp).then_inc(wrest_sem, 16)
                act.dma_start(WP[:], wpT).then_inc(wrest_sem, 16)
                act.dma_start(w123_in[:], w123T).then_inc(wrest_sem, 16)
                act.wait_ge(gn_done, 1)

                def normalise(i, par):
                    j, b = shift(i, par)
                    if exists(j):
                        m = B * j + b
                        wait(act, r_turned, m - 1)
                        nc.scalar.activation(rslot[:, b, :], X[:, b, bass.ds(j * BLK, BLK)], ACT.Identity,
                                             bias=gn_bias[:, b:b + 1], scale=gn_scale[:, b:b + 1]).then_inc(r_ready, 1)

                def store_y(i, par):
                    j, b = shift(i, par - 1)
                    if exists(j):
                        m = B * j + b
                        wait(act, y_turned, m + 1)
                        nc.scalar.activation(Y[:, b, bass.ds(j * BROWS + PADT, BROWS), R:R + W],
                                             TB[b][:].rearrange("p (r c) -> p r c", c=W), ACT.Copy).then_inc(y_stored, 1)

                def store_k(i, par):
                    j, b = shift(i, par - 2)
                    if exists(j):
                        m = B * j + b
                        wait(act, k_made, m + 1)
                        nc.scalar.activation(KEY[:, b, bass.ds(j * BROWS + R, BROWS), R:R + W],
                                             KP[b][:].rearrange("p (r c) -> p r c", c=W), ACT.Identity,
                                             bias=bk[:]).then_inc(k_stored, 1)

                def steps(i):
                    for par in range(2):
                        normalise(i, par)
                        store_y(i, par)
                        store_k(i, par)

                act.wait_ge(cols_done, 3)
                act.wait_ge(pads_set, 16)
                steps(0)
                steps(1)
                with act.Fori(2, NBLK // 2) as i:
                    steps(i)
                steps(NBLK // 2)

            @block.vector
            def _(dve):
                for b in range(B):
                    dve.wait_ge(x_in[b], 16)
                    for c in range(8):
                        nc.vector.bn_stats(stat[:, b, c, :], X[:, b, c * 512:(c + 1) * 512]).then_inc(gn_stats, 1)
                for b in range(B):
                    dve.wait_ge(gn_stats, 8 * (b + 1))
                    nc.vector.bn_aggr(mv[:, b, :], stat[:, b, :, :].rearrange("p c s -> p (c s)")).then_inc(gn_mean, 1)
                dve.wait_ge(gn_mean, 2)
                nc.vector.tensor_copy(mom[:, :, 0], mv[:, :, 0]).then_inc(gn_mom, 1)
                nc.vector.tensor_tensor(gsq[:], mv[:, :, 0], mv[:, :, 0], ALU.mult).then_inc(gn_sq, 1)
                dve.wait_ge(gn_sq, 1)
                nc.vector.tensor_tensor(mom[:, :, 1], gsq[:], mv[:, :, 1], ALU.add).then_inc(gn_mom, 1)
                dve.wait_ge(gn_avg, 1)
                nc.vector.tensor_copy(gmom[:].rearrange("p b s -> p (b s)"), gsum).then_inc(gn_copied, 1)
                dve.wait_ge(gn_copied, 1)
                dve.wait_ge(gn_mom, 2)
                nc.vector.tensor_tensor(gsq[:], gmom[:, :, 0], gmom[:, :, 0], ALU.mult).then_inc(gn_sq, 1)
                dve.wait_ge(gn_sq, 2)
                nc.vector.scalar_tensor_tensor(gvar[:], gmom[:, :, 1], 1e-5, gsq[:], ALU.add, ALU.subtract).then_inc(gn_var, 2)
                dve.wait_ge(gn_rstd, 1)
                nc.vector.scalar_tensor_tensor(gn_bias[:], gmom[:, :, 0], -1.0, gn_scale[:], ALU.mult, ALU.mult).then_inc(gn_done, 1)

                dve.wait_ge(const_in, 48)
                dve.wait_ge(wqkv_sem, 16)
                dve.wait_ge(wrest_sem, 48)

                def gain(dst, src, g, scale=None):
                    a = (scale, ALU.mult) if scale is not None else (None, ALU.bypass)
                    nc.vector.tensor_scalar(dst, src, vec[:, VI[g]:VI[g] + 1], a[0], ALU.mult, a[1]).then_inc(w_scaled, 1)

                gain(WQ[:], wqkv_in[:, 0, :], "g1", -DH ** -0.5)
                gain(WK[:], wqkv_in[:, 1, :], "g1")
                gain(WV[:], wqkv_in[:, 2, :], "g1")
                gain(w1g[:], w123_in[:, 0, :], "g2")
                gain(W2[:], w123_in[:, 1, :], "g3")
                gain(w3g[:], w123_in[:, 2, :], "g4")
                dve.wait_ge(prep_cols, 1)

                def plus(dst, a, v):
                    nc.vector.tensor_tensor(dst, a, vec[:, VI[v]:VI[v] + 1], ALU.add).then_inc(cols_done, 1)

                nc.vector.tensor_scalar(bq[:], wq_be, vec[:, VI["bq"]:VI["bq"] + 1], -DH ** -0.5, ALU.add,
                                        ALU.mult).then_inc(cols_done, 1)
                plus(bk[:], wk_be, "bk")
                plus(bvc[:], wv_be, "bv")
                plus(b3[:], w3_be, "bl3")
                dve.wait_ge(gn_done, 1)
                for b in range(B):
                    nc.vector.scalar_tensor_tensor(res_bias[:, b:b + 1], w1_be, vec[:, VI["bl1"]:VI["bl1"] + 1],
                                                   gn_bias[:, b:b + 1], ALU.add, ALU.add).then_inc(cols_done, 1)
                dve.wait_ge(prep_mat, 1)
                nc.vector.tensor_copy(w1c[:], w1c_ps).then_inc(w1c_done, 1)
                nc.vector.tensor_copy(W3[:], w3c_ps).then_inc(w1c_done, 1)
                dve.wait_ge(prep_bv, 1)
                nc.vector.tensor_tensor(bpc[:], wp_bv, vec[:, VI["bp"]:VI["bp"] + 1], ALU.add).then_inc(bpc_done, 1)
                dve.wait_ge(prep_mat, 2)
                nc.vector.tensor_copy(WPZ[:], wpz_ps).then_inc(wpz_done, 1)
                dve.wait_ge(prep_rows, 1)
                rp = row_ps.rearrange("p (k c) -> p k c", k=3)
                nc.vector.tensor_tensor(brow[:, 0, :], rp[:, 0, :], row[:, 0, :], ALU.add).then_inc(rows_done, 1)
                nc.vector.tensor_copy(brow[:, 1, :], rp[:, 1, :]).then_inc(rows_done, 1)
                nc.vector.tensor_tensor(brow[:, 2, :], rp[:, 2, :], row[:, 1, :], ALU.add).then_inc(rows_done, 1)
                nc.vector.tensor_copy(brow[:, 3, :], row[:, 2, :]).then_inc(rows_done, 1)
                dve.wait_ge(rows_done, 4)
                nc.vector.tensor_copy(bhi[:, 0], brow[:]).then_inc(split_done, 1)
                dve.wait_ge(split_done, 1)
                nc.vector.tensor_tensor(bres[:, 0], brow[:], bhi[:, 0], ALU.subtract).then_inc(split_done, 1)
                dve.wait_ge(split_done, 2)
                nc.vector.tensor_copy(bhi[:, 1], bres[:, 0]).then_inc(split_done, 1)
                dve.wait_ge(split_done, 3)
                nc.vector.tensor_tensor(bres[:, 1], bres[:, 0], bhi[:, 1], ALU.subtract).then_inc(split_done, 1)
                dve.wait_ge(split_done, 4)
                nc.vector.tensor_copy(bhi[:, 2], bres[:, 1]).then_inc(split_done, 1)
                dve.wait_ge(split_done, 5)
                dve.wait_ge(const_set, 3)
                for part in range(3):
                    for k in range(len(BIAS)):
                        nc.vector.tensor_copy(bias3[32 * part:32 * part + 1, k, :, :],
                                              bhi[:, part, k:k + 1, :].broadcast_to([1, T, P])).then_inc(split_done, 1)

                def stats(i, par):
                    j, b = shift(i, par)
                    if exists(j):
                        m = B * j + b
                        wait(dve, r_turned, m + 1)
                        wait(dve, y_mv, T * (m - 1))
                        for t in range(T):
                            nc.vector.bn_stats(tstat[:, b, t, :], TA[b][:, t * P:(t + 1) * P]).then_inc(y_stats, 1)
                        wait(dve, y_ready, T * (m - 1))
                        wait(dve, y_stats, T * (m + 1))
                        settle(dve, passed["dve"])
                        for t in range(T):
                            nc.vector.bn_aggr(tmv[:, b, t, :], tstat[:, b, t, :]).then_inc(y_mv, 1)
                        wait(dve, y_mv, T * m + T)
                        wait(dve, y_rstd, m - 1)
                        nc.vector.tensor_scalar_add(tve[:, b, :], tmv[:, b, :, 1], 1e-5).then_inc(y_ve, 1)

                def apply(i, par):
                    j, b = shift(i, par - 1)
                    if exists(j):
                        m = B * j + b
                        wait(dve, y_rstd, m + 1)
                        wait(dve, y_turned, m - 1)
                        for t in range(T):
                            nc.vector.tensor_scalar(yn[:, b, t * P:(t + 1) * P], TA[b][:, t * P:(t + 1) * P],
                                                    tmv[:, b, t, 0:1], trs[:, b, t:t + 1], ALU.subtract,
                                                    ALU.mult).then_inc(y_ready, 1)

                def steps(i):
                    for par in range(2):
                        stats(i, par)
                        apply(i, par)

                steps(0)
                steps(1)
                with dve.Fori(2, NBLK // 2) as i:
                    steps(i)
                steps(NBLK // 2)
                dve.wait_ge(table_in, 48)
                nc.vector.tensor_scalar(tab[:], tab[:], -1.0, None, ALU.mult).then_inc(table_neg, 1)

            @block.tensor
            def _(pe):
                mm = nc.tensor.matmul
                pe.wait_ge(const_in, 48)
                pe.wait_ge(wqkv_sem, 16)
                pe.wait_ge(wrest_sem, 48)
                v = lambda n: vec[:, VI[n]:VI[n] + 1]
                mm(wq_be, wqkv_in[:, 0, :], v("be1"), start=True, stop=True)
                mm(wk_be, wqkv_in[:, 1, :], v("be1"), start=True, stop=True)
                mm(wv_be, wqkv_in[:, 2, :], v("be1"), start=True, stop=True)
                mm(w1_be, w123_in[:, 0, :], v("be2"), start=True, stop=True)
                mm(w3_be, w123_in[:, 2, :], v("be4"), start=True, stop=True).then_inc(prep_cols, 1)
                pe.wait_ge(gn_mom, 2)
                mm(gsum, groupavg, mom[:].rearrange("p b s -> p (b s)"), start=True, stop=True).then_inc(gn_avg, 1)
                pe.wait_ge(w_scaled, 6)
                mm(w1c_ps, center, w1g[:], start=True, stop=True)
                mm(w3c_ps, center, w3g[:], start=True, stop=True).then_inc(prep_mat, 1)
                pe.wait_ge(cols_done, 6)
                pe.wait_ge(gn_copied, 1)
                mm(wp_bv, WP[:], bvc[:], start=True, stop=True).then_inc(prep_bv, 1)
                pe.wait_ge(w1c_done, 2)
                mm(wpz_ps, wp_in[:], w1c[:], start=True, stop=True).then_inc(prep_mat, 1)
                pe.wait_ge(bpc_done, 1)
                rp = row_ps.rearrange("p (k c) -> p k c", k=3)
                mm(rp[:, 0, :], bvc[:], WP[:], start=True, stop=True)
                mm(rp[:, 1, :], bpc[:], w1c[:], start=True, stop=True)
                mm(rp[:, 2, :], v("be3"), w123_in[:, 1, :], start=True, stop=True).then_inc(prep_rows, 1)

                def turn_r(i, par):
                    j, b = shift(i, par)
                    if exists(j):
                        m = B * j + b
                        wait(pe, r_ready, m + 1)
                        wait(pe, y_ready, T * (m - 1))
                        for t in range(T):
                            ins = nc.tensor.transpose(TA[b][:, t * P:(t + 1) * P], rslot[:, b, t * P:(t + 1) * P], ident)
                        ins.then_inc(r_turned, 1)

                def turn_y(i, par):
                    j, b = shift(i, par - 1)
                    if exists(j):
                        m = B * j + b
                        wait(pe, y_ready, T * (m + 1))
                        wait(pe, y_stored, m - 1)
                        for t in range(T):
                            ins = nc.tensor.transpose(TB[b][:, t * P:(t + 1) * P], yn[:, b, t * P:(t + 1) * P], ident)
                        ins.then_inc(y_turned, 1)

                def keys(i, par):
                    j, b = shift(i, par - 2)
                    if exists(j):
                        m = B * j + b
                        wait(pe, y_stored, m + 1)
                        wait(pe, k_stored, m - 1)
                        mm(KP[b][:], WK[:], Y[:, b, bass.ds(j * BROWS + PADT, BROWS), R:R + W],
                           start=True, stop=True).then_inc(k_made, 1)

                def steps(i):
                    for par in range(2):
                        turn_r(i, par)
                        turn_y(i, par)
                        keys(i, par)

                steps(0)
                steps(1)
                with pe.Fori(2, NBLK // 2) as i:
                    steps(i)
                steps(NBLK // 2)

        with ExitStack() as mem:
            ystrip = sb(mem, "ystrip", [P, B, YH, KC])
            tcur = sb(mem, "tcur", [P, B, 3, NK])
            Q = sb(mem, "Q", [P, B, TILES, HEADS, NQ])
            V = sb(mem, "V", [CHK, B, NCH, P])
            S = sb(mem, "S", [P, 2, 2, NK])
            smin = sb(mem, "smin", [P, 2, 2])
            E = sb(mem, "E", [P, 2, 2, NK])
            esum = sb(mem, "esum", [P, 2, 2])
            erec = sb(mem, "erec", [P, 2, 2])
            skip = 2 * CHK + QR * KC
            FR = sb(mem, "FR", [P, 2, KC + 2 * skip])
            frames = FR[:, :, KC:].rearrange("p s (t n) -> p s t n", n=skip)[:, :, :, 0:NK]
            PT = sb(mem, "PT", [CHK, 2, 2, 2, P])
            SP = [ps(mem, f"SP{i}") for i in range(2)]
            PP = [ps(mem, f"PP{i}") for i in range(2)]
            OP = [ps(mem, f"OP{i}") for i in range(2)]
            QV = [ps(mem, f"QV{i}") for i in range(2)]
            VG = 3
            frames_zero, q_zero = sem("frames_zero"), sem("q_zero")
            strip_ready, table_ready, qv_made, q_ready, v_ready = (
                sem(n) for n in ("strip_ready", "table_ready", "qv_made", "q_ready", "v_ready"))
            s_made, scored, exp_done, rec_done, normed, p_turned, pt_ready, pv_done, attn_stored = (
                sem(n) for n in ("s_made", "scored", "exp_done", "rec_done", "normed", "p_turned", "pt_ready",
                                 "pv_done", "attn_stored"))
            block = mem.enter_context(nc.Block())

            def strip_at(i, par, d):
                j, b = shift(i, par + d)
                return j, b, B * j + b

            def pair_at(i, par, p, d):
                j, b, m = strip_at(i, par, (p + d) // PAIRS)
                pp = (p + d) % PAIRS
                return j, b, m, pp, PAIRS * m + pp

            def over_strips(eng, steps):
                steps(0)
                with eng.Fori(1, STRIPS - 1) as i:
                    steps(i)
                steps(STRIPS - 1)

            @block.gpsimd
            def _(pool):
                nc.gpsimd.memset(FR[:], 0.0).then_inc(frames_zero, 1)

                def table(i, par, d):
                    s, b, m = strip_at(i, par, d)
                    if exists(s):
                        cls = (s > 0) + (s > STRIPS - 2) if isinstance(s, int) else (s + 7) // 8 + (s + 1) // 8
                        wait(pool, scored, 2 * PAIRS * (m - 1))
                        settle(pool, passed["pool"])
                        nc.gpsimd.tensor_copy(tcur[:, b, :, :], tab[:, bass.ds(cls, 1), :, :].rearrange(
                            "p c r k -> p (c r) k")).then_inc(table_ready, 1)

                def norm(i, par, p, d):
                    s, b, m, pp, g = pair_at(i, par, p, d)
                    if exists(s):
                        wait(pool, rec_done, g + 1)
                        wait(pool, p_turned, g - 1)
                        nc.gpsimd.tensor_tensor(frames[:, pp % 2], E[:, pp % 2],
                                                erec[:, pp % 2, :].unsqueeze(2).broadcast_to([P, 2, NK]),
                                                ALU.mult).then_inc(normed, 1)

                def steps(i):
                    for par in range(2):
                        for p in range(PAIRS):
                            norm(i, par, p, 1)
                            if p == 1:
                                table(i, par, 1)

                pool.wait_ge(frames_zero, 1)
                table(0, 0, 0)
                norm(0, 0, 0, 0)
                over_strips(pool, steps)

            @block.vector
            def _(dve):
                nc.vector.memset(Q[:], 0.0).then_inc(q_zero, 1)
                dve.wait_ge(q_zero, 1)

                def strip(i, par, d):
                    s, b, m = strip_at(i, par, d)
                    if exists(s):
                        wait(dve, qv_made, 4 * (m - 1))
                        nc.vector.tensor_copy(ystrip[:, b], Y[:, b, :, bass.ds(s * QC, KC)]).then_inc(strip_ready, 1)

                def store_q(i, par, d, heads):
                    s, b, m = strip_at(i, par, d)
                    if exists(s):
                        wait(dve, qv_made, 4 * m + 1)
                        wait(dve, s_made, PAIRS * (m - 1))
                        for h in heads:
                            hs = slice(h * DH, (h + 1) * DH)
                            nc.vector.tensor_scalar(Q[hs, b, :, h, :], QV[0][hs, :].rearrange("p (t q) -> p t q", q=NQ),
                                                    bq[hs, :], None, ALU.add).then_inc(q_ready, 1)

                def score(i, par, p, d):
                    s, b, m, pp, g = pair_at(i, par, p, d)
                    if exists(s):
                        wait(dve, s_made, g + 1)
                        wait(dve, exp_done, 2 * (g - 1))
                        wait(dve, table_ready, m + 1)
                        settle(dve, passed["dve"])
                        for t in range(2):
                            tile = 2 * pp + t
                            rc = 0 if tile == 0 else 2 if tile == TILES - 1 else 1
                            nc.vector.tensor_tensor_reduce(
                                S[:, pp % 2, t, :], SP[pp % 2][:, t * NK:(t + 1) * NK], tcur[:, b, rc, :], 1.0, 3.0e38,
                                ALU.add, ALU.min, smin[:, pp % 2, t:t + 1]).then_inc(scored, 1)

                def recip(i, par, p, d):
                    s, b, m, pp, g = pair_at(i, par, p, d)
                    if exists(s):
                        wait(dve, exp_done, 2 * (g + 1))
                        wait(dve, normed, g - 1)
                        nc.vector.reciprocal(erec[:, pp % 2, :], esum[:, pp % 2, :]).then_inc(rec_done, 1)

                def steps(i):
                    for par in range(2):
                        for p in range(PAIRS):
                            recip(i, par, p, 1)
                            score(i, par, p, 2)
                            if p == 0:
                                strip(i, par, 1)
                            if p == 2:
                                store_q(i, par, 1, range(HEADS))

                strip(0, 0, 0)
                store_q(0, 0, 0, range(HEADS))
                score(0, 0, 0, 0)
                score(0, 0, 1, 0)
                recip(0, 0, 0, 0)
                over_strips(dve, steps)

            @block.scalar
            def _(act):
                def store_v(i, par, d, group):
                    s, b, m = strip_at(i, par, d)
                    if exists(s):
                        wait(act, qv_made, 4 * m + 2 + group)
                        wait(act, pv_done, PAIRS * (m - 1))
                        nc.scalar.activation(V[:, b, VG * group:VG * group + VG, :],
                                             QV[(group + 1) % 2][0:CHK, 0:VG * P].rearrange("p (c n) -> p c n", c=VG),
                                             ACT.Copy).then_inc(v_ready, 1)

                def exps(i, par, p, d):
                    s, b, m, pp, g = pair_at(i, par, p, d)
                    if exists(s):
                        wait(act, scored, 2 * (g + 1))
                        wait(act, normed, g - 1)
                        wait(act, rec_done, g - 1)
                        for t in range(2):
                            nc.scalar.activation(E[:, pp % 2, t, :], S[:, pp % 2, t, :], ACT.Exp,
                                                 bias=smin[:, pp % 2, t:t + 1], scale=-1.0,
                                                 accum_out=esum[:, pp % 2, t:t + 1]).then_inc(exp_done, 1)

                def store_pt(i, par, p, d):
                    s, b, m, pp, g = pair_at(i, par, p, d)
                    if exists(s):
                        wait(act, p_turned, g + 1)
                        wait(act, pv_done, g - 1)
                        nc.scalar.activation(PT[:, pp % 2].rearrange("p c t n -> p (c t n)"), PP[pp % 2][0:CHK, :],
                                             ACT.Copy).then_inc(pt_ready, 1)

                def store_attn(i, par, d):
                    s, b, m = strip_at(i, par, d)
                    if exists(s):
                        wait(act, pv_done, PAIRS * (m + 1))
                        wait(act, strip_ready, m + 3 if not isinstance(m, int) else min(m + 3, NSTRIP))
                        nc.scalar.activation(Y[:, b, PADT:PADT + H, bass.ds(s * QC + R, QC)],
                                             OP[b][:].rearrange("p (r c) -> p r c", c=QC), ACT.Copy).then_inc(attn_stored, 1)

                def steps(i):
                    for par in range(2):
                        for p in range(PAIRS):
                            exps(i, par, p, 1)
                            store_pt(i, par, p, 0)
                            if p in (3, 4, 5):
                                store_v(i, par, 1, p - 3)
                            if p == 1:
                                store_attn(i, par, -1)

                for group in range(3):
                    store_v(0, 0, 0, group)
                exps(0, 0, 0, 0)
                over_strips(act, steps)
                store_attn(STRIPS - 1, 1, 0)

            @block.tensor
            def _(pe):
                mm = nc.tensor.matmul

                def queries(i, par, d):
                    s, b, m = strip_at(i, par, d)
                    if exists(s):
                        wait(pe, strip_ready, m + 1)
                        wait(pe, v_ready, 3 * m - 1)
                        mm(QV[0][:], WQ[:], ystrip[:, b, PADT:PADT + H, R:R + QC], start=True, stop=True).then_inc(qv_made, 1)

                def values(i, par, d, group):
                    s, b, m = strip_at(i, par, d)
                    if exists(s):
                        if group == 1:
                            wait(pe, q_ready, HEADS * (m + 1))
                        else:
                            wait(pe, v_ready, 3 * m + group - 1 if group else 3 * m)
                        for c in range(VG):
                            ch = VG * group + c
                            ins = mm(QV[(group + 1) % 2][0:CHK, c * P:(c + 1) * P],
                                     ystrip[:, b, CHR * ch:CHR * (ch + 1), :].rearrange("p r c -> p (r c)"), WV[:],
                                     start=True, stop=True)
                        ins.then_inc(qv_made, 1)

                def scores(i, par, p, d):
                    s, b, m, pp, g = pair_at(i, par, p, d)
                    if exists(s):
                        wait(pe, q_ready, HEADS * (m + 1))
                        wait(pe, scored, 2 * (g - 1))
                        for t in range(2):
                            tile = 2 * pp + t
                            ins = mm(SP[pp % 2][:, t * NK:(t + 1) * NK],
                                     Q[:, b, tile].rearrange("p h q -> p (h q)"),
                                     KEY[:, b, QR * tile:QR * tile + KR, bass.ds(s * QC, KC)], start=True, stop=True)
                        ins.then_inc(s_made, 1)

                def turn(i, par, p, d):
                    s, b, m, pp, g = pair_at(i, par, p, d)
                    if exists(s):
                        wait(pe, normed, g + 1)
                        wait(pe, pt_ready, g - 1)
                        for c in range(2):
                            for t in range(2):
                                at = (2 * c + t) * P
                                ins = nc.tensor.transpose(PP[pp % 2][0:CHK, at:at + P],
                                                          FR[:, pp % 2, (2 * t + c) * CHK:(2 * t + c + 1) * CHK], ident)
                        ins.then_inc(p_turned, 1)

                def weigh(i, par, p, d):
                    s, b, m, pp, g = pair_at(i, par, p, d)
                    if exists(s):
                        wait(pe, pt_ready, g + 1)
                        wait(pe, v_ready, 3 * (m + 1))
                        wait(pe, attn_stored, m - 1)
                        for h in range(HEADS):
                            hs = slice(h * DH, (h + 1) * DH)
                            for c in range(2):
                                ins = mm(OP[b][hs, 2 * NQ * pp:2 * NQ * (pp + 1)], V[:, b, pp + c, hs],
                                         PT[:, pp % 2, c, :, hs], start=c == 0, stop=c == 1, tile_position=(0, h * DH))
                        ins.then_inc(pv_done, 1)

                def steps(i):
                    for par in range(2):
                        for p in range(PAIRS):
                            turn(i, par, p, 0)
                            scores(i, par, p, 2)
                            weigh(i, par, p, -1)
                            if p == 1:
                                queries(i, par, 1)
                            if p in (2, 3, 4):
                                values(i, par, 1, p - 2)

                queries(0, 0, 0)
                for group in range(3):
                    values(0, 0, 0, group)
                scores(0, 0, 0, 0)
                scores(0, 0, 1, 0)
                over_strips(pe, steps)
                weigh(STRIPS - 1, 1, PAIRS - 1, 0)

        attn_mem.close()
        with ExitStack() as mem:
            per = {}

            def counter(name, n=1):
                s = sem(name)
                per[name] = (s, n)
                return s

            def done(eng, name, m, n=None):
                s, each = per[name]
                m = min(m, NBLK - 1) if isinstance(m, int) else m
                wait(eng, s, each * m + (each if n is None else n))

            LW = sb(mem, "LW", [P, 3, P])
            EW = sb(mem, "EW", [P, NE * P])
            RW = sb(mem, "RW", [P, NE])
            RB = sb(mem, "RB", [P, NE])
            EBX = sb(mem, "EBX", [T * NE, T, P])
            rank = sb(mem, "rank", [P, T, NE])
            zero3 = sb(mem, "zero3", [96, B * (P + 1)], BF16)

            def two(name, shape=(BLK,)):
                return sb(mem, name, [P, B, *shape])

            def one(name):
                return sb(mem, name, [P, 1, BLK])[:].broadcast_to([P, B, BLK])

            aslot, rslot2, xslot = two("aslot"), two("rslot2"), two("xslot")
            x1, x1b, xn, xnT, u, t0 = (two(n) for n in ("x1", "x1b", "xn", "xnT", "u", "t0"))
            tn, tnT, qf, kf, t1 = (two(n) for n in ("tn", "tnT", "qf", "kf", "t1"))
            eq, ek, rq, rk, kt, am, uT = (one(n) for n in ("eq", "ek", "rq", "rk", "kt", "am", "uT"))
            va = two("va", (T, P + 1))
            state = two("state", (2, P + 1))
            den, rden = two("den", (T,)), two("rden", (T,))
            td, tdT, acc, osum, oT = (two(n) for n in ("td", "tdT", "acc", "osum", "oT"))
            acce, rT = one("acce"), one("rT")
            prod = sb(mem, "prod", [P, 2, 4, P])
            half = sb(mem, "half", [P, 2, 2, P])
            psum4 = two("psum4")
            gate = two("gate", (T, NE))
            gateT = sb(mem, "gateT", [T * NE, B, P])
            lg, is1, w1_, first, lg2, is2, w2_, second, ga, gb = (
                two(n, (T, NE)) for n in ("lg", "is1", "wt1", "first", "lg2", "is2", "wt2", "second", "ga", "gb"))
            top1, best1, top2, best2, gap, e2, dn, g1, g2 = (
                two(n, (T,)) for n in ("top1", "best1", "top2", "best2", "gap", "e2", "dn", "gt1", "gt2"))
            NORMS = {2: "p", 3: "x1", 4: "u", 5: "t0", 6: "t1"}
            bn = {k: two(f"bn{k}", (T, 6)) for k in NORMS}
            mvs = {k: two(f"mvs{k}", (T, 2)) for k in NORMS}
            ve = {k: two(f"ve{k}", (T,)) for k in NORMS}
            nmu = {k: two(f"nmu{k}", (T,)) for k in NORMS}
            rs = {k: two(f"rs{k}", (T,)) for k in NORMS}
            nb = {k: two(f"nb{k}", (T,)) for k in NORMS}
            G = [ps(mem, f"G{i}") for i in range(5)]
            M = [ps(mem, f"M{i}") for i in range(2)]
            SPS = ps(mem, "SPS")

            lw_in, ebx_zero, ebx_in, preset = sem("lw_in"), sem("ebx_zero"), sem("ebx_in"), sem("preset")
            state_zero = sem("state_zero")
            stored = [sem(f"stored{b}") for b in range(B)]
            for name, n in dict(a_copied=1, r_made=1, x_made=1, rt_made=1, rT_ready=1, z1_made=1, xt_made=1, x1_ready=T, x1b_ready=1,
                                xn_ready=T, xn_turned=1, xnT_ready=1, z2_made=1, u_ready=1, u_turned=1, uT_ready=1,
                                z3_made=1, t0_ready=T, p_made=1, tn_ready=T, tn_turned=1, tnT_ready=1, q_made=1,
                                k_made3=1, v_made=1, e_ready=2, v_stored=1, relu_qk=2, f_ready=2, k_turned=1, kt_ready=1,
                                a_made=1, a_masked=1, num_made=T, state_made=T, state_ready=T, den_ready=2, rden_ready=1,
                                t1_ready=T, td_ready=T, td_turned=1, tdT_ready=1, logits_made=1, gated=1, e2_ready=1,
                                gate_steps=18, g_turned=1, gT_ready=1, eb_made=1, moe_made=2 * T, prods=4 * T, sums=2 * T,
                                chain=4 * T, acce_ready=1, osum_ready=1, o_turned=1, oT_ready=1).items():
                counter(name, n)
            for k in NORMS:
                counter(f"stats{k}", T)
                counter(f"mv{k}", T)
                counter(f"ve{k}", 2)
                counter(f"rs{k}", 1)
                counter(f"nb{k}", 1)

            inc = lambda ins, name: ins.then_inc(per[name][0], 1)
            tile = lambda t: slice(t * P, (t + 1) * P)
            NPAIR = NBLK // B
            LAG = dict(pre=0, a=1, b=2, c=3, d=4)

            def over_blocks(eng, steps):
                for i in range(3):
                    steps(i)
                with eng.Fori(3, NPAIR) as i:
                    steps(i)
                for i in range(NPAIR, NPAIR + 2):
                    steps(i)

            def stream(i, par, name):
                j, b = shift(i, par - LAG[name])
                return (j, b, B * j + b) if exists(j) else None

            block = mem.enter_context(nc.Block())

            @block.sync
            def _(sp):
                sp.dma_start(LW[:], laT).then_inc(lw_in, 16)
                sp.dma_start(EW[:], expw).then_inc(lw_in, 16)
                sp.dma_start(RW[:], rw).then_inc(lw_in, 16)
                sp.dma_start(RB[:], rb.broadcast_to([P, NE])).then_inc(lw_in, 16)
                sp.wait_ge(ebx_zero, 1)
                for t in range(T):
                    sp.dma_start(EBX[t * NE:(t + 1) * NE, t, :], expb).then_inc(ebx_in, 16)

                def steps(i):
                    for par in range(2):
                        if s := stream(i, par, "d"):
                            j, b, m = s
                            done(sp, "oT_ready", m)
                            sp.dma_start(out[b][:, bass.ds(j * BLK, BLK)], oT[:, b, :]).then_inc(stored[b], 16)

                over_blocks(sp, steps)
                for b in range(B):
                    sp.wait_ge(stored[b], 16 * NPAIR)

            @block.gpsimd
            def _(pool):
                tt = nc.gpsimd.tensor_tensor
                nc.gpsimd.memset(EBX[:], 0.0).then_inc(ebx_zero, 1)
                nc.gpsimd.memset(zero3[:], 0.0).then_inc(preset, 1)
                nc.gpsimd.memset(va[:, :, :, P:P + 1], 1.0).then_inc(preset, 1)
                nc.gpsimd.memset(state[:], 0.0).then_inc(preset, 1)
                for e in range(NE):
                    nc.gpsimd.memset(rank[:, :, e:e + 1], float(NE - e)).then_inc(preset, 1)

                def rstd(k, s, readers):
                    if s:
                        j, b, m = s
                        done(pool, f"ve{k}", m)
                        done(pool, readers, m - 2)
                        inc(tt(rs[k][:, b, :], ve[k][:, b, :], halfneg[:], ALU.pow), f"rs{k}")
                        if k in (3, 5, 6):
                            done(pool, f"rs{k}", m)
                            inc(tt(nb[k][:, b, :], nmu[k][:, b, :], rs[k][:, b, :], ALU.mult), f"nb{k}")

                def sums(s, t):
                    if s:
                        j, b, m = s
                        done(pool, "prods", m, 4 * t + 4)
                        inc(tt(half[:, t % 2], prod[:, t % 2, 0:2, :], prod[:, t % 2, 2:4, :], ALU.add), "sums")
                        done(pool, "sums", m, 2 * t + 1)
                        done(pool, "osum_ready", m - 2)
                        inc(tt(psum4[:, b, tile(t)], half[:, t % 2, 0, :], half[:, t % 2, 1, :], ALU.add), "sums")

                def steps(i):
                    for par in range(2):
                        pre, a, b_, c, d = (stream(i, par, n) for n in LAG)
                        rstd(3, b_, "xn_ready")
                        rstd(2, a, "x1_ready")
                        sums(d, 0)
                        sums(d, 1)
                        rstd(4, b_, "t0_ready")
                        sums(d, 2)
                        rstd(6, c, "td_ready")
                        sums(d, 3)
                        if d:
                            j, b, m = d
                            done(pool, "acce_ready", m)
                            done(pool, "sums", m)
                            done(pool, "o_turned", m - 2)
                            inc(tt(osum[:, b, :], acce[:, b, :], psum4[:, b, :], ALU.add), "osum_ready")
                        rstd(5, b_, "tn_ready")
                        if pre:
                            j, b, m = pre
                            done(pool, "xt_made", m - 2)
                            inc(nc.gpsimd.tensor_tensor(xslot[:, b, :], X[:, b, bass.ds(j * BLK, BLK)],
                                                        b3[:].broadcast_to([P, BLK]), ALU.add), "x_made")

                over_blocks(pool, steps)

            @block.scalar
            def _(act):
                copy = lambda dst, src: nc.scalar.activation(dst, src, ACT.Copy)

                def apply(k, s, dst, src, name, reader):
                    if s:
                        j, b, m = s
                        done(act, f"nb{k}", m)
                        done(act, reader, m - 2)
                        for t in range(T):
                            inc(nc.scalar.activation(dst[:, b, tile(t)], src[:, b, tile(t)], ACT.Identity,
                                                     bias=nb[k][:, b, t:t + 1], scale=rs[k][:, b, t:t + 1]), name)

                def evacuate(s, dst, src, made, name, reader, depth=2):
                    if s:
                        j, b, m = s
                        done(act, made, m)
                        done(act, reader, m - depth)
                        inc(copy(dst[:, b, :], src[:]), name)

                def experts(s, t):
                    if s:
                        j, b, m = s
                        done(act, "gated", m)
                        done(act, "moe_made", m, 2 * t + 1)
                        if t >= 2:
                            done(act, "sums", m, 2 * (t - 2) + 1)
                        else:
                            done(act, "sums", m - 1, 2 * (t + 2) + 1)
                        for e in range(4):
                            inc(nc.scalar.activation(prod[:, t % 2, e, :], M[0][:, tile(e)], ACT.Copy,
                                                     scale=gate[:, b, t, e:e + 1]), "prods")

                def steps(i):
                    for par in range(2):
                        pre, a, b_, c, d = (stream(i, par, n) for n in LAG)
                        evacuate(b_, rT, G[0], "rt_made", "rT_ready", "x1_ready", depth=1)
                        apply(5, c, tn, t0, "tn_ready", "tn_turned")
                        evacuate(d, tdT, G[3], "td_turned", "tdT_ready", "moe_made")
                        evacuate(c, tnT, G[2], "tn_turned", "tnT_ready", "v_made")
                        if d:
                            j, b, m = d
                            done(act, "gate_steps", m, 13)
                            done(act, "gated", m - 2)
                            inc(nc.scalar.activation(e2[:, b, :], gap[:, b, :], ACT.Exp), "e2_ready")
                        if c:
                            j, b, m = c
                            done(act, "q_made", m)
                            done(act, "f_ready", m - 1)
                            inc(nc.scalar.activation(eq[:, b, :], G[2][:], ACT.Exp,
                                                     bias=vec[:, VI["lbq"]:VI["lbq"] + 1]), "e_ready")
                            done(act, "k_made3", m)
                            inc(nc.scalar.activation(ek[:, b, :], G[0][:], ACT.Exp,
                                                     bias=vec[:, VI["lbk"]:VI["lbk"] + 1]), "e_ready")
                            done(act, "v_made", m)
                            done(act, "num_made", m - 2)
                            inc(copy(va[:, b, :, 0:P], G[1][:].rearrange("p (t n) -> p t n", t=T)), "v_stored")
                        apply(3, b_, xn, x1, "xn_ready", "xn_turned")
                        experts(d, 0)
                        evacuate(b_, xnT, G[3], "xn_turned", "xnT_ready", "z2_made")
                        evacuate(c, kt, G[2], "k_turned", "kt_ready", "state_made", depth=1)
                        if d:
                            j, b, m = d
                            done(act, "g_turned", m)
                            done(act, "eb_made", m - 2)
                            inc(copy(gateT[:, b, :], G[0][0:T * NE, 0:P]), "gT_ready")
                        experts(d, 1)
                        if b_:
                            j, b, m = b_
                            done(act, "z2_made", m)
                            done(act, "u_turned", m - 2)
                            done(act, "stats4", m - 2)
                            inc(nc.scalar.activation(u[:, b, :], G[4][:], ACT.Relu), "u_ready")
                        experts(d, 2)
                        if c:
                            j, b, m = c
                            for t in range(T):
                                done(act, "state_made", m, t + 1)
                                done(act, "num_made", m, t)
                                inc(copy(state[:, b, (t + 1) % 2, :], SPS[:, b * (P + 1):(b + 1) * (P + 1)]), "state_ready")
                        experts(d, 3)
                        evacuate(b_, uT, G[0], "u_turned", "uT_ready", "z3_made", depth=1)
                        if d:
                            j, b, m = d
                            done(act, "o_turned", m)
                            wait(act, stored[b], 16 * j)
                            inc(copy(oT[:, b, :], G[3][:]), "oT_ready")
                        apply(6, c, td, t1, "td_ready", "td_turned")

                act.wait_ge(preset, 3)
                over_blocks(act, steps)

            @block.vector
            def _(dve):
                tt, stt, ts = nc.vector.tensor_tensor, nc.vector.scalar_tensor_tensor, nc.vector.tensor_scalar

                def stats(k, s, src, made, n=None):
                    if s:
                        j, b, m = s
                        done(dve, made, m)
                        done(dve, f"mv{k}", m - 2)
                        for t in range(T):
                            inc(nc.vector.bn_stats(bn[k][:, b, t, :], src(b, t)), f"stats{k}")
                        done(dve, f"ve{k}", m - 2)
                        done(dve, f"stats{k}", m)
                        settle(dve, passed["dve"])
                        for t in range(T):
                            inc(nc.vector.bn_aggr(mvs[k][:, b, t, :], bn[k][:, b, t, :]), f"mv{k}")
                        done(dve, f"mv{k}", m)
                        done(dve, f"nb{k}" if k in (3, 5, 6) else f"rs{k}", m - 2)
                        inc(nc.vector.tensor_scalar_add(ve[k][:, b, :], mvs[k][:, b, :, 1], 1e-5), f"ve{k}")
                        inc(ts(nmu[k][:, b, :], mvs[k][:, b, :, 0], -1.0, None, ALU.mult), f"ve{k}")

                def experts(s, t):
                    if s:
                        j, b, m = s
                        done(dve, "moe_made", m, 2 * t + 2)
                        done(dve, "gated", m)
                        done(dve, "acce_ready", m - 2)
                        for e in range(4):
                            if e:
                                done(dve, "chain", m, 4 * t + e)
                            inc(stt(acc[:, b, tile(t)], M[1][:, tile(e)], gate[:, b, t, 4 + e:5 + e],
                                    (acc if e else t1)[:, b, tile(t)], ALU.mult, ALU.add), "chain")

                def gating(s):
                    if not s:
                        return
                    j, b, m = s
                    wide = lambda v: v[:, b, :].unsqueeze(2).broadcast_to([P, T, NE])
                    n = 0

                    def step(ins):
                        nonlocal n
                        inc(ins, "gate_steps")
                        n += 1
                        done(dve, "gate_steps", m, n)

                    def pick(logits, top, same, weight, best, chosen):
                        step(nc.vector.tensor_reduce(top[:, b, :], logits[:, b], AX_X, ALU.max))
                        step(tt(same[:, b], logits[:, b], wide(top), ALU.is_equal))
                        step(tt(weight[:, b], same[:, b], rank[:], ALU.mult))
                        step(nc.vector.tensor_reduce(best[:, b, :], weight[:, b], AX_X, ALU.max))
                        step(tt(chosen[:, b], weight[:, b], wide(best), ALU.is_equal))

                    done(dve, "logits_made", m)
                    done(dve, "gated", m - 2)
                    done(dve, "e2_ready", m - 2)
                    step(tt(lg[:, b], G[3][:, 0:T * NE].rearrange("p (t e) -> p t e", t=T),
                            RB[:].unsqueeze(1).broadcast_to([P, T, NE]), ALU.add))
                    pick(lg, top1, is1, w1_, best1, first)
                    step(stt(lg2[:, b], first[:, b], -3.0e38, lg[:, b], ALU.mult, ALU.add))
                    pick(lg2, top2, is2, w2_, best2, second)
                    step(tt(gap[:, b, :], top2[:, b, :], top1[:, b, :], ALU.subtract))
                    done(dve, "e2_ready", m)
                    step(nc.vector.tensor_scalar_add(dn[:, b, :], e2[:, b, :], 1.0))
                    step(nc.vector.reciprocal(g1[:, b, :], dn[:, b, :]))
                    step(tt(g2[:, b, :], g1[:, b, :], e2[:, b, :], ALU.mult))
                    step(tt(ga[:, b], first[:, b], wide(g1), ALU.mult))
                    step(tt(gb[:, b], second[:, b], wide(g2), ALU.mult))
                    done(dve, "prods", m - 2)
                    done(dve, "g_turned", m - 2)
                    done(dve, "chain", m - 2)
                    inc(tt(gate[:, b], ga[:, b], gb[:, b], ALU.add), "gated")
                    assert n == per["gate_steps"][1]

                def steps(i):
                    for par in range(2):
                        pre, a, b_, c, d = (stream(i, par, n) for n in LAG)
                        if b_:
                            j, b, m = b_
                            done(dve, "rT_ready", m)
                            done(dve, "z1_made", m)
                            done(dve, "rs2", m)
                            done(dve, "xn_ready", m - 2)
                            done(dve, "x1b_ready", m - 2)
                            for t in range(T):
                                inc(stt(x1[:, b, tile(t)], G[1][:, tile(t)], rs[2][:, b, t:t + 1], rT[:, b, tile(t)],
                                        ALU.mult, ALU.add), "x1_ready")
                        stats(3, b_, lambda b, t: x1[:, b, tile(t)], "x1_ready")
                        stats(2, a, lambda b, t: G[4][:, tile(t)], "p_made")
                        gating(d)
                        if c:
                            j, b, m = c
                            for n, (bank, made, bias, r, e, f) in enumerate(
                                    ((G[2], "q_made", "lbq", rq, eq, qf), (G[0], "k_made3", "lbk", rk, ek, kf))):
                                done(dve, made, m)
                                done(dve, "e_ready", m, n + 1)
                                done(dve, "f_ready", m - 1)
                                inc(ts(r[:, b, :], bank[:], vec[:, VI[bias]:VI[bias] + 1], 0.0, ALU.add, ALU.max),
                                    "relu_qk")
                                done(dve, "relu_qk", m, n + 1)
                                done(dve, "a_made", m - 2)
                                done(dve, "num_made", m - 2)
                                inc(stt(f[:, b, :], e[:, b, :], 1.0, r[:, b, :], ALU.min, ALU.add), "f_ready")
                        if b_:
                            j, b, m = b_
                            done(dve, "xt_made", m)
                            done(dve, "t0_ready", m - 2)
                            inc(tt(x1b[:, b, :], x1[:, b, :], G[4][:], ALU.add), "x1b_ready")
                        experts(d, 0)
                        if c:
                            j, b, m = c
                            done(dve, "a_made", m)
                            done(dve, "num_made", m - 1)
                            inc(tt(am[:, b, :].rearrange("p (t n) -> p t n", t=T),
                                   G[1][:].rearrange("p (t n) -> p t n", t=T),
                                   causal.unsqueeze(1).broadcast_to([P, T, P]), ALU.mult), "a_masked")
                        experts(d, 1)
                        stats(4, b_, lambda b, t: u[:, b, tile(t)], "u_ready")
                        experts(d, 2)
                        if c:
                            j, b, m = c
                            done(dve, "num_made", m)
                            done(dve, "rden_ready", m - 2)
                            for n, bank in enumerate((G[2], G[1])):
                                inc(nc.vector.tensor_scalar_add(
                                    den[:, b, 2 * n:2 * n + 2],
                                    bank[:, 0:2 * (P + 1)].rearrange("p (t n) -> p t n", t=2)[:, :, P], 1e-6), "den_ready")
                            done(dve, "den_ready", m)
                            done(dve, "t1_ready", m - 2)
                            inc(nc.vector.reciprocal(rden[:, b, :], den[:, b, :]), "rden_ready")
                            done(dve, "rden_ready", m)
                            done(dve, "chain", m - 2)
                            for t in range(T):
                                bank, at = (G[2], G[1])[t // 2], (t % 2) * (P + 1)
                                inc(stt(t1[:, b, tile(t)], bank[:, at:at + P], rden[:, b, t:t + 1], t0[:, b, tile(t)],
                                        ALU.mult, ALU.add), "t1_ready")
                        stats(6, c, lambda b, t: t1[:, b, tile(t)], "t1_ready")
                        experts(d, 3)
                        if d:
                            j, b, m = d
                            done(dve, "eb_made", m)
                            done(dve, "chain", m)
                            done(dve, "osum_ready", m - 1)
                            inc(tt(acce[:, b, :], acc[:, b, :], G[3][:], ALU.add), "acce_ready")
                        if b_:
                            j, b, m = b_
                            done(dve, "z3_made", m)
                            done(dve, "rs4", m)
                            done(dve, "x1b_ready", m)
                            done(dve, "t1_ready", m - 2)
                            for t in range(T):
                                inc(stt(t0[:, b, tile(t)], G[4][:, tile(t)], rs[4][:, b, t:t + 1], x1b[:, b, tile(t)],
                                        ALU.mult, ALU.add), "t0_ready")
                        stats(5, b_, lambda b, t: t0[:, b, tile(t)], "t0_ready")
                        if pre:
                            j, b, m = pre
                            done(dve, "z1_made", m - 2)
                            inc(nc.vector.tensor_copy(aslot[:, b, :].rearrange("p (r c) -> p r c", c=W),
                                                      Y[:, b, bass.ds(j * BROWS + PADT, BROWS), R:R + W]), "a_copied")
                            done(dve, "rt_made", m - 2)
                            inc(ts(rslot2[:, b, :], X[:, b, bass.ds(j * BLK, BLK)], gn_scale[:, b:b + 1],
                                   res_bias[:, b:b + 1], ALU.mult, ALU.add), "r_made")

                dve.wait_ge(lw_in, 64)
                dve.wait_ge(preset, 3 + NE)
                over_blocks(dve, steps)

            @block.tensor
            def _(pe):
                mm, turn = nc.tensor.matmul, nc.tensor.transpose

                def bias(bank, name):
                    mm(bank[:], ones3[:], bias3[:, BIAS.index(name)].rearrange("p t n -> p (t n)"), start=True, stop=False,
                       skip_group_check=True)

                def linear(bank, src, b, w, last=True):
                    for t in range(T):
                        ins = mm(bank[:, tile(t)], src[:, b, tile(t)], w, start=False, stop=True, skip_group_check=True)
                    return ins

                def turned(s, bank, src, ready, released, name):
                    if s:
                        j, b, m = s
                        done(pe, ready, m)
                        released(m)
                        for t in range(T):
                            ins = turn(bank[:, tile(t)], src[:, b, tile(t)], ident)
                        inc(ins, name)

                def experts(s, t):
                    if s:
                        j, b, m = s
                        done(pe, "tdT_ready", m)
                        done(pe, "prods", m, 4 * t)
                        inc(mm(M[0][:], tdT[:, b, tile(t)], EW[:, 0:BLK], start=True, stop=True), "moe_made")
                        done(pe, "chain", m, 4 * t)
                        inc(mm(M[1][:], tdT[:, b, tile(t)], EW[:, BLK:], start=True, stop=True), "moe_made")

                def steps(i):
                    for par in range(2):
                        pre, a, b_, c, d = (stream(i, par, n) for n in LAG)
                        turned(b_, G[0], rslot2, "r_made", lambda m: done(pe, "uT_ready", m - 1), "rt_made")
                        if b_:
                            j, b, m = b_
                            done(pe, "a_copied", m)
                            done(pe, "t1_ready", m - 2)
                            bias(G[1], "z1")
                            inc(linear(G[1], aslot, b, WPZ[:]), "z1_made")
                        turned(d, G[3], td, "td_ready", lambda m: done(pe, "oT_ready", m - 1), "td_turned")
                        if a:
                            j, b, m = a
                            done(pe, "a_copied", m)
                            done(pe, "t0_ready", m - 2)
                            bias(G[4], "p")
                            inc(linear(G[4], aslot, b, WP[:]), "p_made")
                        turned(c, G[2], tn, "tn_ready", lambda m: done(pe, "t1_ready", m - 1), "tn_turned")
                        if d:
                            j, b, m = d
                            done(pe, "tdT_ready", m)
                            for t in range(T):
                                ins = mm(G[3][:, t * NE:(t + 1) * NE], tdT[:, b, tile(t)], RW[:], start=True, stop=True)
                            inc(ins, "logits_made")
                        experts(d, 0)
                        if c:
                            j, b, m = c
                            done(pe, "tnT_ready", m)
                            inc(mm(G[2][:], LW[:, 0, :], tnT[:, b, :], start=True, stop=True), "q_made")
                            done(pe, "x1_ready", m + 1)
                            inc(mm(G[0][:], LW[:, 1, :], tnT[:, b, :], start=True, stop=True), "k_made3")
                            bias(G[1], "v")
                            inc(linear(G[1], tnT, b, LW[:, 2, :]), "v_made")
                        turned(b_, G[4], xslot, "x_made", lambda m: done(pe, "stats2", m + 1), "xt_made")
                        experts(d, 1)
                        turned(b_, G[3], xn, "xn_ready", lambda m: done(pe, "gate_steps", m - 2, 1), "xn_turned")
                        turned(c, G[2], kf, "f_ready", lambda m: None, "k_turned")
                        if c:
                            j, b, m = c
                            done(pe, "v_stored", m)
                            for t in range(T):
                                ins = mm(G[1][:, tile(t)], kf[:, b, tile(t)], qf[:, b, tile(t)], start=True, stop=True)
                            inc(ins, "a_made")
                        if d:
                            j, b, m = d
                            done(pe, "gated", m)
                            done(pe, "f_ready", m + 1)
                            inc(turn(G[0][0:T * NE, 0:P], gate[:, b].rearrange("p t e -> p (t e)"), ident), "g_turned")
                        experts(d, 2)
                        if b_:
                            j, b, m = b_
                            done(pe, "xnT_ready", m)
                            done(pe, "x1b_ready", m)
                            bias(G[4], "z2")
                            inc(linear(G[4], xnT, b, W2[:]), "z2_made")
                        if d:
                            j, b, m = d
                            done(pe, "gT_ready", m)
                            done(pe, "xnT_ready", m + 2)
                            inc(mm(G[3][:], gateT[:, b, :], EBX[:].rearrange("p t n -> p (t n)"), start=True, stop=True),
                                "eb_made")
                        if c:
                            j, b, m = c
                            done(pe, "kt_ready", m)
                            done(pe, "a_masked", m)

                            def num(t, first):
                                bank, at = (G[2], G[1])[t // 2], (t % 2) * (P + 1)
                                if first:
                                    mm(bank[:, at:at + P + 1], am[:, b, tile(t)], va[:, b, t, :], start=True, stop=False)
                                else:
                                    inc(mm(bank[:, at:at + P + 1], qf[:, b, tile(t)], state[:, b, t % 2, :], start=False,
                                           stop=True), "num_made")

                            num(0, True)
                            for t in range(T):
                                done(pe, "state_ready", m - 2 if t == 0 else m, None if t == 0 else t)
                                done(pe, "state_ready", m - 1 if t == 0 else m, None if t == 0 else t)
                                inc(mm(SPS[:, b * (P + 1):(b + 1) * (P + 1)], kt[:, b, tile(t)], va[:, b, t, :],
                                       start=False, stop=True, skip_group_check=True), "state_made")
                                num(t, False)
                                if t < T - 1:
                                    num(t + 1, True)
                        experts(d, 3)
                        turned(b_, G[0], u, "u_ready", lambda m: done(pe, "gT_ready", m - 2), "u_turned")
                        if b_:
                            j, b, m = b_
                            done(pe, "uT_ready", m)
                            done(pe, "u_ready", m)
                            for t in range(T):
                                ins = mm(G[4][:, tile(t)], uT[:, b, tile(t)], W3[:], start=True, stop=True)
                            inc(ins, "z3_made")
                        turned(d, G[3], osum, "osum_ready", lambda m: None, "o_turned")

                pe.wait_ge(lw_in, 64)
                pe.wait_ge(ebx_in, 64)
                pe.wait_ge(preset, 3)
                mm(SPS[:, 0:B * (P + 1)], ones3[:], zero3[:], start=True, stop=True).then_inc(state_zero, 1)
                pe.wait_ge(state_zero, 1)
                over_blocks(pe, steps)


def constants():
    eye = np.eye(P, dtype=np.float32)
    group = np.kron(np.eye(GROUPS), np.full((C // GROUPS, C // GROUPS), GROUPS / C)).astype(np.float32)
    center = (np.eye(P) - np.full((P, P), 1.0 / P)).astype(np.float32)
    causal = np.triu(np.ones((P, P), np.float32))
    return np.concatenate([eye, group, center, causal], axis=1)


def kernel(**inputs):
    import concourse.bacc as bacc
    from concourse.bass_utils import run_bass_kernel_spmd as run

    g = {k: np.asarray(v) for k, v in inputs.items()}
    L0, L1 = "L0_conv_", "L1_"
    qkvb, lab = g[L0 + "qkv_b"], g[L1 + "attn_b"]
    col = {**{n: g[L0 + n] for n in ("g1", "be1", "g2", "be2", "g3", "be3", "g4", "be4", "bl1", "bl3")},
           "bq": qkvb[0:C], "bk": qkvb[C:2 * C], "bv": qkvb[2 * C:], "bp": g[L0 + "proj_b"],
           "lbq": lab[0:C], "lbk": lab[C:2 * C]}
    side = lambda ws: np.stack([w.T for w in ws], axis=1)
    arrays = {
        "x": g["x"].reshape(B, C, TOK),
        "wqkvT": side(np.split(g[L0 + "qkv_w"], 3)),
        "wp": g[L0 + "proj_w"],
        "wpT": g[L0 + "proj_w"].T,
        "w123T": side([g[L0 + "w1"], g[L0 + "w2"], g[L0 + "w3"]]),
        "vecs": np.stack([col[n] for n in VEC], axis=1),
        "rows": np.stack([g[L0 + "proj_b"], g[L0 + "bl2"], lab[2 * C:]])[None],
        "rpb": g[L0 + "rpb"],
        "laT": side(np.split(g[L1 + "attn_W"], 3)),
        "expw": g[L1 + "ffn_expert_w"].transpose(1, 0, 2).reshape(C, NE * C),
        "rw": g[L1 + "ffn_router_w"],
        "rb": g[L1 + "ffn_router_b"].reshape(1, NE),
        "expb": g[L1 + "ffn_expert_b"],
        "consts": constants(),
    }
    arrays = {k: np.ascontiguousarray(v) for k, v in arrays.items()}
    nc = bacc.Bacc("TRN2", target_bir_lowering=False, num_devices=1)
    args = {k: nc.dram_tensor("in_" + k, v.shape, mybir.dt.from_np(v.dtype), kind="ExternalInput").ap()
            for k, v in arrays.items()}
    out = nc.dram_tensor("out", (B, C, TOK), F32, kind="ExternalOutput").ap()
    build(nc, out=out, **args)
    r = run(nc, [{"in_" + k: v for k, v in arrays.items()}], core_ids=[0])
    return r.results[0]["out"].reshape(B, C, H, W)
```

```python
from contextlib import ExitStack

import numpy as np

import concourse.bass as bass
from concourse import mybir

F32 = mybir.dt.float32
BF16 = mybir.dt.bfloat16
ALU = mybir.AluOpType
ACT = mybir.ActivationFunctionType
AX_X = mybir.AxisListType.X

B, C, H, W = 2, 128, 64, 64
TOK = H * W
HEADS, DH, K = 4, 32, 7
GROUPS = 32
NE = 8
P = 128

R = K // 2
QR, QC = 4, 8
KR, KC = QR + 2 * R, QC + 2 * R
NK = KR * KC
PW = W + 2 * R
PADT = 4
YH = H + 2 * PADT
KH = H + 2 * R
CHR = 8
CHK = CHR * KC
NCH = YH // CHR
STRIPS = W // QC
NSTRIP = B * STRIPS
TILES = H // QR
PAIRS = TILES // 2
NQ = QR * QC
BLK = 512
BROWS = BLK // W
NBLK = B * TOK // BLK
T = BLK // P
FAR = -1.0e30

VEC = ["g1", "be1", "g2", "be2", "g3", "be3", "g4", "be4", "bq", "bk", "bv", "bp", "bl1", "bl3", "lbq", "lbk"]
VI = {n: i for i, n in enumerate(VEC)}
ROWS = ["bp", "bl2", "lbv"]
BIAS = ["p", "z1", "z2", "v"]


def shift(i, d):
    return i + d // 2, d % 2


def exists(j):
    return not isinstance(j, int) or 0 <= j < NBLK // 2


def wait(eng, sem, value):
    if isinstance(value, int) and value <= 0:
        return
    eng.wait_ge(sem, value)


def settle(eng, passed):
    eng.sem_inc(passed, 1)


def build(nc, x, kept, prep, rows, rpb, laT, expw, rw, rb, expb, out):
    ctx = ExitStack()
    with ctx:
        names = {}

        def sb(stack, name, shape, dt=F32):
            return stack.enter_context(nc.sbuf_tensor(name, shape, dt))

        def ps(stack, name, shape=(P, 512), dt=F32):
            return stack.enter_context(nc.psum_tensor(name, list(shape), dt))

        def sem(name):
            assert name not in names
            names[name] = ctx.enter_context(nc.semaphore(name))
            return names[name]

        passed = {n: sem(f"passed_{n}") for n in ("dve", "pool")}

        X = sb(ctx, "X", [P, B, TOK])
        keep = sb(ctx, "keep", [P, len(VEC) + 5 * P])
        vec = keep[:, 0:len(VEC)]
        WP, ident, groupavg, center, causal = (keep[:, len(VEC) + k * P:len(VEC) + (k + 1) * P] for k in range(5))
        halfneg = sb(ctx, "halfneg", [P, 4])
        row = sb(ctx, "row", [1, len(ROWS), P])
        gn_scale = sb(ctx, "gn_scale", [P, B])
        gn_bias = sb(ctx, "gn_bias", [P, B])
        res_bias = sb(ctx, "res_bias", [P, B])
        b3 = sb(ctx, "b3", [P, 1])
        WPZ = sb(ctx, "WPZ", [P, P])
        W2 = sb(ctx, "W2", [P, P])
        W3 = sb(ctx, "W3", [P, P])
        bias3 = sb(ctx, "bias3", [96, len(BIAS), P], BF16)
        ones3 = sb(ctx, "ones3", [96, P], BF16)
        LW = sb(ctx, "LW", [P, 3, P])
        EW = sb(ctx, "EW", [P, NE * P])
        RW = sb(ctx, "RW", [P, NE])
        RB = sb(ctx, "RB", [P, NE])
        EBX = sb(ctx, "EBX", [T * NE, T, P])
        rank = sb(ctx, "rank", [P, T, NE])
        zero3 = sb(ctx, "zero3", [96, B * (P + 1)], BF16)
        va = sb(ctx, "va", [P, B, T, P + 1])
        state = sb(ctx, "state", [P, B, 2, P + 1])
        eps, minus = sb(ctx, "eps", [P, T]), sb(ctx, "minus", [P, T])
        lw_in, ebx_zero, ebx_in, preset = sem("lw_in"), sem("ebx_zero"), sem("ebx_in"), sem("preset")
        Y = sb(ctx, "Y", [P, B, YH, PW])

        attn_mem = ctx.enter_context(ExitStack())
        KEY = sb(attn_mem, "KEY", [P, B, KH, PW])
        WQ = sb(attn_mem, "WQ", [P, P])
        WK = sb(attn_mem, "WK", [P, P])
        WV = sb(attn_mem, "WV", [P, P])
        bq = sb(attn_mem, "bq", [P, 1])
        bk = sb(attn_mem, "bk", [P, 1])
        Q = sb(attn_mem, "Q", [P, B, TILES, HEADS, NQ])
        tab = sb(attn_mem, "tab", [P, 3, 3, NK])

        with ExitStack() as mem:
            prep_in = sb(mem, "prep_in", [P, 7, P])
            wqkv_in, w123_in, wp_in = prep_in[:, 0:3, :], prep_in[:, 3:6, :], prep_in[:, 6, :]
            w1g = sb(mem, "w1g", [P, P])
            w1c = sb(mem, "w1c", [P, P])
            w3g = sb(mem, "w3g", [P, P])
            far = sb(mem, "far", [P, 3 * NK])
            bvc = sb(mem, "bvc", [P, 1])
            b1 = sb(mem, "b1", [P, 1])
            bpc = sb(mem, "bpc", [P, 1])
            XPARTS = 2
            brow = sb(mem, "brow", [1, len(BIAS), P])
            bhi = sb(mem, "bhi", [1, 2, len(BIAS), P], BF16)
            bres = sb(mem, "bres", [1, 2, len(BIAS), P])
            stat = sb(mem, "stat", [P, B, 8, 6])
            mv = sb(mem, "mv", [P, B, 2])
            mom = sb(mem, "mom", [P, B, 2])
            gmom = sb(mem, "gmom", [P, B, 2])
            gvar = sb(mem, "gvar", [P, B])
            gsq = sb(mem, "gsq", [P, B])
            rslot = sb(mem, "rslot", [P, B, BLK])
            tstat = sb(mem, "tstat", [P, B, T, 6])
            tmv = sb(mem, "tmv", [P, B, T, 2])
            tve = sb(mem, "tve", [P, B, T])
            trs = sb(mem, "trs", [P, B, T])
            tnb = sb(mem, "tnb", [P, B, T])
            yn = sb(mem, "yn", [P, B, BLK])
            TA = [ps(mem, f"TA{i}") for i in range(4)]
            TB = [ps(mem, f"TB{i}") for i in range(B)]
            KP = [ps(mem, f"KP{i}") for i in range(B)]
            PREP = KP
            wq_be, wk_be, wv_be, w1_be, w3_be, wp_bv = (PREP[0][:, a:a + 1] for a in range(6))
            gsum = PREP[0][:, 8:8 + 2 * B]
            w1c_ps, w3c_ps, wpz_ps = (PREP[1][:, k * P:(k + 1) * P] for k in range(3))
            row_ps = PREP[0][0:1, P:4 * P]
            cdram = nc.dram_tensor("column_bias", [3, HEADS, QC, 2 * K - 1, KC], F32, kind="Internal").ap()
            tdram = nc.dram_tensor("bias_table", [3, 3, HEADS, QR, QC, NK], F32, kind="Internal").ap()

            x_in = [[sem(f"x_in{b}{c}") for c in range(XPARTS)] for b in range(B)]
            kept_in, prep_ready, row_in = sem("kept_in"), sem("prep_ready"), sem("row_in")
            far_set, far_out = sem("far_set"), sem("far_out")
            columns_out, table_out, table_in = sem("columns_out"), sem("table_out"), sem("table_in")
            table_neg, pads_set, const_set = sem("table_neg"), sem("pads_set"), sem("const_set")
            gn_stats, gn_mean, gn_mom, gn_avg, gn_copied = (
                sem(n) for n in ("gn_stats", "gn_mean", "gn_mom", "gn_avg", "gn_copied"))
            gn_sq, gn_var, gn_rstd, gn_done = (sem(n) for n in ("gn_sq", "gn_var", "gn_rstd", "gn_done"))
            w_scaled, prep_cols, prep_mat, cols_done = (sem(n) for n in ("w_scaled", "prep_cols", "prep_mat", "cols_done"))
            w1c_done, prep_bv, bpc_done, prep_rows, rows_done, split_done, wpz_done = (
                sem(n) for n in ("w1c_done", "prep_bv", "bpc_done", "prep_rows", "rows_done", "split_done", "wpz_done"))
            r_ready, r_turned, y_stats, y_mv, y_ve, y_rstd, y_ready, y_turned, y_stored, k_made, k_stored = (
                sem(n) for n in ("r_ready", "r_turned", "y_stats", "y_mv", "y_ve", "y_rstd", "y_ready", "y_turned",
                                 "y_stored", "k_made", "k_stored"))

            y_nb, y_ready2, rest_done, res_done = (sem(n) for n in ("y_nb", "y_ready2", "rest_done", "res_done"))
            block = mem.enter_context(nc.Block())

            def over_quads(eng, steps, first, last, end):
                for k in range(first):
                    steps(2 * k)
                with eng.Fori(first, last) as k:
                    steps(2 * k)
                for k in range(last, end):
                    steps(2 * k)

            @block.sync
            def _(sp):
                sp.dma_start(keep[:], kept).then_inc(kept_in, 16)
                sp.dma_start(prep_in[:], prep).then_inc(prep_ready, 16)
                for b in range(B):
                    for c in range(XPARTS):
                        part = slice(c * TOK // XPARTS, (c + 1) * TOK // XPARTS)
                        sp.dma_start(X[:, b, part], x[b][:, part]).then_inc(x_in[b][c], 16)
                sp.wait_ge(far_set, 1)
                sp.dma_start(cdram.rearrange("c h q a k -> (c h q) (a k)"), far[0:96, 0:13 * KC]).then_inc(far_out, 16)
                for part in range(3):
                    sp.dma_start(tdram.rearrange("r c h a b k -> (r c h a b k)").rearrange("(p n) -> p n", p=P)
                                 [:, part * 3 * NK:(part + 1) * 3 * NK], far[:]).then_inc(far_out, 16)
                sp.wait_ge(far_out, 64)
                for cc, c0 in enumerate((0, QC, W - QC)):
                    for qc in range(QC):
                        start = min(max(c0 + qc - R, 0), W - K)
                        at, idx = start - (c0 - R), start - (c0 + qc) + K - 1
                        sp.dma_start(cdram[cc, :, qc, :, at:at + K],
                                     rpb[:, :, idx:idx + K]).then_inc(columns_out, 16)
                sp.wait_ge(columns_out, 16 * 3 * QC)
                for rc, r0 in enumerate((0, QR, H - QR)):
                    for qr in range(QR):
                        start = min(max(r0 + qr - R, 0), H - K)
                        at, idx = start - (r0 - R), start - (r0 + qr) + K - 1
                        sp.dma_start(tdram[rc, :, :, qr, :, at * KC:(at + K) * KC].rearrange("c h q n -> (c h) q n"),
                                     cdram[:, :, :, idx:idx + K, :].rearrange("c h q a k -> (c h) q (a k)")
                                     ).then_inc(table_out, 16)
                sp.wait_ge(table_out, 16 * 3 * QR)
                for cc in range(3):
                    sp.dma_start(tab[:, cc, :, :], tdram[:, cc].rearrange("r h a b k -> (h a b) r k")).then_inc(table_in, 16)

            @block.gpsimd
            def _(pool):
                nc.gpsimd.memset(far[:], FAR).then_inc(far_set, 1)
                nc.gpsimd.memset(halfneg[:], -0.5).then_inc(const_set, 1)
                nc.gpsimd.memset(ones3[:], 1.0).then_inc(const_set, 1)
                nc.gpsimd.memset(bias3[:], 0.0).then_inc(const_set, 1)
                for b in range(B):
                    nc.gpsimd.memset(Y[:, b, 0:PADT, :], 0.0).then_inc(pads_set, 1)
                    nc.gpsimd.memset(Y[:, b, PADT + H:YH, :], 0.0).then_inc(pads_set, 1)
                    nc.gpsimd.memset(Y[:, b, PADT:PADT + H, 0:R], 0.0).then_inc(pads_set, 1)
                    nc.gpsimd.memset(Y[:, b, PADT:PADT + H, R + W:PW], 0.0).then_inc(pads_set, 1)
                    nc.gpsimd.memset(KEY[:, b, 0:R, :], 0.0).then_inc(pads_set, 1)
                    nc.gpsimd.memset(KEY[:, b, R + H:KH, :], 0.0).then_inc(pads_set, 1)
                    nc.gpsimd.memset(KEY[:, b, R:R + H, 0:R], 0.0).then_inc(pads_set, 1)
                    nc.gpsimd.memset(KEY[:, b, R:R + H, R + W:PW], 0.0).then_inc(pads_set, 1)
                nc.gpsimd.memset(Q[:], 0.0).then_inc(pads_set, 1)
                pool.wait_ge(rows_done, 4)
                pool.wait_ge(split_done, 1)
                nc.gpsimd.tensor_tensor(bres[:, 0], brow[:], bhi[:, 0], ALU.subtract).then_inc(rest_done, 1)
                pool.wait_ge(rest_done, 1)
                pool.wait_ge(split_done, 2)
                nc.gpsimd.tensor_tensor(bres[:, 1], bres[:, 0], bhi[:, 1], ALU.subtract).then_inc(rest_done, 1)
                pool.wait_ge(const_set, 1)
                pool.wait_ge(gn_var, 2)
                nc.gpsimd.tensor_tensor(gn_scale[:], gvar[:], halfneg[:, 0:B], ALU.pow).then_inc(gn_rstd, 1)

                def ln_rstd(i, par):
                    j, b = shift(i, par)
                    if exists(j):
                        m = B * j + b
                        wait(pool, y_ve, m + 1)
                        wait(pool, y_ready, T // 2 * (m - 1))
                        wait(pool, y_ready2, T // 2 * (m - 1))
                        nc.gpsimd.tensor_tensor(trs[:, b, :], tve[:, b, :], halfneg[:], ALU.pow).then_inc(y_rstd, 1)

                def steps(i):
                    for par in range(4):
                        ln_rstd(i, par)
                
                over_quads(pool, steps, 1, 3, 4)
                nc.gpsimd.memset(EBX[:], 0.0).then_inc(ebx_zero, 1)
                nc.gpsimd.memset(zero3[:], 0.0).then_inc(preset, 1)
                nc.gpsimd.memset(eps[:], 1e-5).then_inc(preset, 1)
                nc.gpsimd.memset(minus[:], -1.0).then_inc(preset, 1)
                nc.gpsimd.memset(va[:, :, :, P:P + 1], 1.0).then_inc(preset, 1)
                nc.gpsimd.memset(state[:], 0.0).then_inc(preset, 1)
                for e in range(NE):
                    nc.gpsimd.memset(rank[:, :, e:e + 1], float(NE - e)).then_inc(preset, 1)

            @block.scalar
            def _(act):
                act.dma_start(row[:], rows).then_inc(row_in, 16)

                act.wait_ge(const_set, 3)
                act.wait_ge(rows_done, 4)
                nc.scalar.activation(bhi[:, 0], brow[:], ACT.Copy).then_inc(split_done, 1)
                act.wait_ge(rest_done, 1)
                nc.scalar.activation(bhi[:, 1], bres[:, 0], ACT.Copy).then_inc(split_done, 1)
                act.wait_ge(split_done, 2)
                for part in range(2):
                    nc.scalar.activation(bias3[32 * part:32 * part + 1, :, :], bhi[:, part], ACT.Copy).then_inc(split_done, 1)
                act.wait_ge(rest_done, 2)
                nc.scalar.activation(bias3[64:65, :, :], bres[:, 1], ACT.Copy).then_inc(split_done, 1)

                def normalise(i, par, d):
                    j, b = shift(i, par + d)
                    if exists(j):
                        m = B * j + b
                        wait(act, r_turned, m - 1)
                        nc.scalar.activation(rslot[:, b, :], X[:, b, bass.ds(j * BLK, BLK)], ACT.Identity,
                                             bias=gn_bias[:, b:b + 1], scale=gn_scale[:, b:b + 1]).then_inc(r_ready, 1)

                def half_apply(i, par):
                    j, b = shift(i, par - 2)
                    if exists(j):
                        m = B * j + b
                        wait(act, y_nb, m + 1)
                        wait(act, y_ready, T // 2 * (m + 1))
                        wait(act, y_turned, m - 1)
                        for t in range(T // 2, T):
                            nc.scalar.activation(yn[:, b, t * P:(t + 1) * P], TA[(par - 2) % 4][:, t * P:(t + 1) * P], ACT.Identity,
                                                 bias=tnb[:, b, t:t + 1], scale=trs[:, b, t:t + 1]).then_inc(y_ready2, 1)

                def store_y(i, par):
                    j, b = shift(i, par - 3)
                    if exists(j):
                        m = B * j + b
                        wait(act, y_turned, m + 1)
                        nc.scalar.activation(Y[:, b, bass.ds(j * BROWS + PADT, BROWS), R:R + W],
                                             TB[b][:].rearrange("p (r c) -> p r c", c=W), ACT.Copy).then_inc(y_stored, 1)

                def store_k(i, par):
                    j, b = shift(i, par - 4)
                    if exists(j):
                        m = B * j + b
                        wait(act, k_made, m + 1)
                        nc.scalar.activation(KEY[:, b, bass.ds(j * BROWS + R, BROWS), R:R + W],
                                             KP[b][:].rearrange("p (r c) -> p r c", c=W), ACT.Identity,
                                             bias=bk[:]).then_inc(k_stored, 1)

                def steps(i):
                    for par in range(4):
                        half_apply(i, par)
                        store_y(i, par)
                        store_k(i, par)
                        normalise(i, par, 2)

                act.wait_ge(cols_done, 3)
                act.wait_ge(pads_set, 16)
                act.wait_ge(gn_done, 1)
                normalise(0, 0, 0)
                normalise(0, 0, 1)
                over_quads(act, steps, 2, 3, 5)

            @block.vector
            def _(dve):
                dve.wait_ge(kept_in, 16)
                dve.wait_ge(prep_ready, 16)

                def gain(dst, src, g, scale=None):
                    a = (scale, ALU.mult) if scale is not None else (None, ALU.bypass)
                    nc.vector.tensor_scalar(dst, src, vec[:, VI[g]:VI[g] + 1], a[0], ALU.mult, a[1]).then_inc(w_scaled, 1)

                gain(w1g[:], w123_in[:, 0, :], "g2")
                gain(w3g[:], w123_in[:, 2, :], "g4")
                gain(WQ[:], wqkv_in[:, 0, :], "g1", -DH ** -0.5)
                gain(WK[:], wqkv_in[:, 1, :], "g1")
                gain(WV[:], wqkv_in[:, 2, :], "g1")
                gain(W2[:], w123_in[:, 1, :], "g3")
                dve.wait_ge(prep_cols, 1)

                def plus(dst, a, v):
                    nc.vector.tensor_tensor(dst, a, vec[:, VI[v]:VI[v] + 1], ALU.add).then_inc(cols_done, 1)

                nc.vector.tensor_scalar(bq[:], wq_be, vec[:, VI["bq"]:VI["bq"] + 1], -DH ** -0.5, ALU.add,
                                        ALU.mult).then_inc(cols_done, 1)
                plus(bk[:], wk_be, "bk")
                plus(bvc[:], wv_be, "bv")
                plus(b3[:], w3_be, "bl3")
                plus(b1[:], w1_be, "bl1")
                dve.wait_ge(prep_mat, 1)
                nc.vector.tensor_copy(w1c[:], w1c_ps).then_inc(w1c_done, 1)
                nc.vector.tensor_copy(W3[:], w3c_ps).then_inc(w1c_done, 1)
                dve.wait_ge(prep_bv, 1)
                nc.vector.tensor_tensor(bpc[:], wp_bv, vec[:, VI["bp"]:VI["bp"] + 1], ALU.add).then_inc(bpc_done, 1)
                dve.wait_ge(prep_mat, 2)
                nc.vector.tensor_copy(WPZ[:], wpz_ps).then_inc(wpz_done, 1)

                def moments(b, parts):
                    for part in parts:
                        dve.wait_ge(x_in[b][part], 16)
                        for c in range(part * 8 // XPARTS, (part + 1) * 8 // XPARTS):
                            nc.vector.bn_stats(stat[:, b, c, :], X[:, b, c * 512:(c + 1) * 512]).then_inc(gn_stats, 1)

                moments(0, range(XPARTS))
                dve.wait_ge(row_in, 16)
                dve.wait_ge(prep_rows, 1)
                rp = row_ps.rearrange("p (k c) -> p k c", k=3)
                nc.vector.tensor_tensor(brow[:, 0, :], rp[:, 0, :], row[:, 0, :], ALU.add).then_inc(rows_done, 1)
                nc.vector.tensor_copy(brow[:, 1, :], rp[:, 1, :]).then_inc(rows_done, 1)
                nc.vector.tensor_tensor(brow[:, 2, :], rp[:, 2, :], row[:, 1, :], ALU.add).then_inc(rows_done, 1)
                nc.vector.tensor_copy(brow[:, 3, :], row[:, 2, :]).then_inc(rows_done, 1)
                moments(1, range(XPARTS))
                for b in range(B):
                    dve.wait_ge(gn_stats, 8 * (b + 1))
                    nc.vector.bn_aggr(mv[:, b, :], stat[:, b, :, :].rearrange("p c s -> p (c s)")).then_inc(gn_mean, 1)
                dve.wait_ge(gn_mean, 2)
                nc.vector.tensor_copy(mom[:, :, 0], mv[:, :, 0]).then_inc(gn_mom, 1)
                nc.vector.tensor_tensor(gsq[:], mv[:, :, 0], mv[:, :, 0], ALU.mult).then_inc(gn_sq, 1)
                dve.wait_ge(gn_sq, 1)
                nc.vector.tensor_tensor(mom[:, :, 1], gsq[:], mv[:, :, 1], ALU.add).then_inc(gn_mom, 1)
                dve.wait_ge(gn_avg, 1)
                nc.vector.tensor_copy(gmom[:].rearrange("p b s -> p (b s)"), gsum).then_inc(gn_copied, 1)
                dve.wait_ge(gn_copied, 1)
                dve.wait_ge(gn_mom, 2)
                nc.vector.tensor_tensor(gsq[:], gmom[:, :, 0], gmom[:, :, 0], ALU.mult).then_inc(gn_sq, 1)
                dve.wait_ge(gn_sq, 2)
                nc.vector.scalar_tensor_tensor(gvar[:], gmom[:, :, 1], 1e-5, gsq[:], ALU.add, ALU.subtract).then_inc(gn_var, 2)
                dve.wait_ge(gn_rstd, 1)
                nc.vector.scalar_tensor_tensor(gn_bias[:], gmom[:, :, 0], -1.0, gn_scale[:], ALU.mult, ALU.mult).then_inc(gn_done, 1)
                dve.wait_ge(gn_done, 1)
                dve.wait_ge(cols_done, 5)
                nc.vector.tensor_tensor(res_bias[:], gn_bias[:], b1[:].broadcast_to([P, B]), ALU.add).then_inc(res_done, 1)

                def stats(i, par):
                    j, b = shift(i, par)
                    if exists(j):
                        m = B * j + b
                        wait(dve, r_turned, m + 1)
                        wait(dve, y_mv, T * (m - 1))
                        for t in range(T):
                            nc.vector.bn_stats(tstat[:, b, t, :], TA[par][:, t * P:(t + 1) * P]).then_inc(y_stats, 1)
                        wait(dve, y_ready, T // 2 * (m - 1))
                        wait(dve, y_nb, m - 1)
                        wait(dve, y_stats, T * (m + 1))
                        settle(dve, passed["dve"])
                        for t in range(T):
                            nc.vector.bn_aggr(tmv[:, b, t, :], tstat[:, b, t, :]).then_inc(y_mv, 1)
                        wait(dve, y_mv, T * m + T)
                        wait(dve, y_rstd, m - 1)
                        nc.vector.tensor_scalar_add(tve[:, b, :], tmv[:, b, :, 1], 1e-5).then_inc(y_ve, 1)

                def apply(i, par):
                    j, b = shift(i, par - 2)
                    if exists(j):
                        m = B * j + b
                        wait(dve, y_rstd, m + 1)
                        wait(dve, y_ready2, T // 2 * (m - 1))
                        nc.vector.scalar_tensor_tensor(tnb[:, b, :], tmv[:, b, :, 0], -1.0, trs[:, b, :], ALU.mult,
                                                       ALU.mult).then_inc(y_nb, 1)
                        wait(dve, y_turned, m - 1)
                        for t in range(T // 2):
                            nc.vector.tensor_scalar(yn[:, b, t * P:(t + 1) * P], TA[(par - 2) % 4][:, t * P:(t + 1) * P],
                                                    tmv[:, b, t, 0:1], trs[:, b, t:t + 1], ALU.subtract,
                                                    ALU.mult).then_inc(y_ready, 1)

                def steps(i):
                    for par in range(4):
                        apply(i, par)
                        stats(i, par)

                over_quads(dve, steps, 2, 4, 5)
                dve.wait_ge(table_in, 48)
                nc.vector.tensor_scalar(tab[:], tab[:], -1.0, None, ALU.mult).then_inc(table_neg, 1)

            @block.tensor
            def _(pe):
                mm = nc.tensor.matmul
                pe.wait_ge(kept_in, 16)
                pe.wait_ge(prep_ready, 16)
                v = lambda n: vec[:, VI[n]:VI[n] + 1]
                mm(wq_be, wqkv_in[:, 0, :], v("be1"), start=True, stop=True)
                mm(wk_be, wqkv_in[:, 1, :], v("be1"), start=True, stop=True)
                mm(wv_be, wqkv_in[:, 2, :], v("be1"), start=True, stop=True)
                mm(w1_be, w123_in[:, 0, :], v("be2"), start=True, stop=True)
                mm(w3_be, w123_in[:, 2, :], v("be4"), start=True, stop=True).then_inc(prep_cols, 1)
                pe.wait_ge(w_scaled, 2)
                mm(w1c_ps, center, w1g[:], start=True, stop=True)
                mm(w3c_ps, center, w3g[:], start=True, stop=True).then_inc(prep_mat, 1)
                pe.wait_ge(cols_done, 5)
                mm(wp_bv, WP, bvc[:], start=True, stop=True).then_inc(prep_bv, 1)
                pe.wait_ge(w1c_done, 2)
                mm(wpz_ps, wp_in, w1c[:], start=True, stop=True).then_inc(prep_mat, 1)
                pe.wait_ge(bpc_done, 1)
                rp = row_ps.rearrange("p (k c) -> p k c", k=3)
                mm(rp[:, 0, :], bvc[:], WP, start=True, stop=True)
                mm(rp[:, 1, :], bpc[:], w1c[:], start=True, stop=True)
                mm(rp[:, 2, :], v("be3"), w123_in[:, 1, :], start=True, stop=True).then_inc(prep_rows, 1)
                pe.wait_ge(gn_mom, 2)
                pe.wait_ge(rows_done, 3)
                mm(gsum, groupavg, mom[:].rearrange("p b s -> p (b s)"), start=True, stop=True).then_inc(gn_avg, 1)
                pe.wait_ge(wpz_done, 1)
                pe.wait_ge(gn_copied, 1)
                pe.wait_ge(w_scaled, 6)

                def turn_r(i, par):
                    j, b = shift(i, par)
                    if exists(j):
                        m = B * j + b
                        wait(pe, r_ready, m + 1)
                        wait(pe, y_ready, T // 2 * (m - 3))
                        wait(pe, y_ready2, T // 2 * (m - 3))
                        for t in range(T):
                            ins = nc.tensor.transpose(TA[par][:, t * P:(t + 1) * P], rslot[:, b, t * P:(t + 1) * P], ident)
                        ins.then_inc(r_turned, 1)

                def turn_y(i, par):
                    j, b = shift(i, par - 2)
                    if exists(j):
                        m = B * j + b
                        wait(pe, y_ready, T // 2 * (m + 1))
                        wait(pe, y_ready2, T // 2 * (m + 1))
                        wait(pe, y_stored, m - 1)
                        for t in range(T):
                            ins = nc.tensor.transpose(TB[b][:, t * P:(t + 1) * P], yn[:, b, t * P:(t + 1) * P], ident)
                        ins.then_inc(y_turned, 1)

                def keys(i, par):
                    j, b = shift(i, par - 4)
                    if exists(j):
                        m = B * j + b
                        wait(pe, y_stored, m + 1)
                        wait(pe, k_stored, m - 1)
                        mm(KP[b][:], WK[:], Y[:, b, bass.ds(j * BROWS + PADT, BROWS), R:R + W],
                           start=True, stop=True).then_inc(k_made, 1)

                def steps(i):
                    for par in range(4):
                        turn_r(i, par)
                        keys(i, par)
                        turn_y(i, par)

                over_quads(pe, steps, 2, 4, 5)

        with ExitStack() as mem:
            ystrip = sb(mem, "ystrip", [P, B, YH, KC])
            tcur = sb(mem, "tcur", [P, B, 3, NK])
            V = sb(mem, "V", [CHK, B, NCH, P])
            S = sb(mem, "S", [P, 2, 2, NK])
            smin = sb(mem, "smin", [P, 2, 2])
            E = sb(mem, "E", [P, 2, 2, NK])
            esum = sb(mem, "esum", [P, 2, 2])
            erec = sb(mem, "erec", [P, 2, 2])
            skip = 2 * CHK + QR * KC
            FR = sb(mem, "FR", [P, 2, KC + 2 * skip])
            frames = FR[:, :, KC:].rearrange("p s (t n) -> p s t n", n=skip)[:, :, :, 0:NK]
            PT = sb(mem, "PT", [CHK, 2, 2, 2, P])
            SP = [ps(mem, f"SP{i}") for i in range(2)]
            PP = [ps(mem, f"PP{i}") for i in range(2)]
            OP = [ps(mem, f"OP{i}") for i in range(2)]
            QV = [ps(mem, f"QV{i}") for i in range(2)]
            VG = 3
            VBANK = (1, 1, 0)
            frames_zero = sem("frames_zero")
            strip_ready, table_ready, qv_made, q_ready, v_ready = (
                sem(n) for n in ("strip_ready", "table_ready", "qv_made", "q_ready", "v_ready"))
            s_made, scored, exp_done, rec_done, normed, p_turned, pt_ready, pv_done, attn_stored = (
                sem(n) for n in ("s_made", "scored", "exp_done", "rec_done", "normed", "p_turned", "pt_ready",
                                 "pv_done", "attn_stored"))
            block = mem.enter_context(nc.Block())

            def strip_at(i, par, d):
                j, b = shift(i, par + d)
                return j, b, B * j + b

            def pair_at(i, par, p, d):
                j, b, m = strip_at(i, par, (p + d) // PAIRS)
                pp = (p + d) % PAIRS
                return j, b, m, pp, PAIRS * m + pp

            def over_strips(eng, steps):
                steps(0)
                with eng.Fori(1, STRIPS - 1) as i:
                    steps(i)
                steps(STRIPS - 1)

            @block.sync
            def _(sp):
                sp.dma_start(LW[:], laT).then_inc(lw_in, 16)
                sp.dma_start(EW[:], expw).then_inc(lw_in, 16)
                sp.dma_start(RW[:], rw).then_inc(lw_in, 16)
                sp.dma_start(RB[:], rb.broadcast_to([P, NE])).then_inc(lw_in, 16)
                sp.wait_ge(ebx_zero, 1)
                for t in range(T):
                    sp.dma_start(EBX[t * NE:(t + 1) * NE, t, :], expb).then_inc(ebx_in, 16)

            @block.gpsimd
            def _(pool):
                nc.gpsimd.memset(FR[:], 0.0).then_inc(frames_zero, 1)

                def table(i, par, d, rc):
                    s, b, m = strip_at(i, par, d)
                    if exists(s):
                        cls = (s > 0) + (s > STRIPS - 2) if isinstance(s, int) else (s + 7) // 8 + (s + 1) // 8
                        wait(pool, scored, 2 * PAIRS * (m - 1))
                        settle(pool, passed["pool"])
                        nc.gpsimd.tensor_copy(tcur[:, b, rc:rc + 1, :], tab[:, bass.ds(cls, 1), rc, :]).then_inc(table_ready, 1)

                def norm(i, par, p, d):
                    s, b, m, pp, g = pair_at(i, par, p, d)
                    if exists(s):
                        wait(pool, rec_done, g + 1)
                        wait(pool, p_turned, g - 1)
                        nc.gpsimd.tensor_tensor(frames[:, pp % 2], E[:, pp % 2],
                                                erec[:, pp % 2, :].unsqueeze(2).broadcast_to([P, 2, NK]),
                                                ALU.mult).then_inc(normed, 1)

                def steps(i):
                    for par in range(2):
                        for p in range(PAIRS):
                            norm(i, par, p, 1)
                            if p < 3:
                                table(i, par, 1, p)

                pool.wait_ge(frames_zero, 1)
                for rc in range(3):
                    table(0, 0, 0, rc)
                norm(0, 0, 0, 0)
                over_strips(pool, steps)

            @block.vector
            def _(dve):
                def strip(i, par, d):
                    s, b, m = strip_at(i, par, d)
                    if exists(s):
                        wait(dve, qv_made, 4 * (m - 1))
                        nc.vector.tensor_copy(ystrip[:, b], Y[:, b, :, bass.ds(s * QC, KC)]).then_inc(strip_ready, 1)

                def store_q(i, par, d, h):
                    s, b, m = strip_at(i, par, d)
                    if exists(s):
                        wait(dve, qv_made, 4 * m + 1)
                        wait(dve, s_made, PAIRS * (m - 1))
                        hs = slice(h * DH, (h + 1) * DH)
                        nc.vector.tensor_scalar(Q[hs, b, :, h, :], QV[0][hs, :].rearrange("p (t q) -> p t q", q=NQ),
                                                bq[hs, :], None, ALU.add).then_inc(q_ready, 1)

                def score(i, par, p, d):
                    s, b, m, pp, g = pair_at(i, par, p, d)
                    if exists(s):
                        wait(dve, s_made, g + 1)
                        wait(dve, exp_done, 2 * (g - 1))
                        wait(dve, table_ready, 3 * (m + 1))
                        settle(dve, passed["dve"])
                        for t in range(2):
                            tile = 2 * pp + t
                            rc = 0 if tile == 0 else 2 if tile == TILES - 1 else 1
                            nc.vector.tensor_tensor_reduce(
                                S[:, pp % 2, t, :], SP[pp % 2][:, t * NK:(t + 1) * NK], tcur[:, b, rc, :], 1.0, 3.0e38,
                                ALU.add, ALU.min, smin[:, pp % 2, t:t + 1]).then_inc(scored, 1)

                def recip(i, par, p, d):
                    s, b, m, pp, g = pair_at(i, par, p, d)
                    if exists(s):
                        wait(dve, exp_done, 2 * (g + 1))
                        wait(dve, normed, g - 1)
                        nc.vector.reciprocal(erec[:, pp % 2, :], esum[:, pp % 2, :]).then_inc(rec_done, 1)

                def steps(i):
                    for par in range(2):
                        for p in range(PAIRS):
                            recip(i, par, p, 1)
                            score(i, par, p, 3)
                            if 1 <= p <= HEADS:
                                store_q(i, par, 1, p - 1)
                            if p == 6:
                                strip(i, par, 2)

                strip(0, 0, 0)
                strip(0, 0, 1)
                for h in range(HEADS):
                    store_q(0, 0, 0, h)
                for p in range(3):
                    score(0, 0, p, 0)
                recip(0, 0, 0, 0)
                over_strips(dve, steps)

            @block.scalar
            def _(act):
                def store_v(i, par, d, group):
                    s, b, m = strip_at(i, par, d)
                    if exists(s):
                        wait(act, qv_made, 4 * m + 2 + group)
                        wait(act, pv_done, PAIRS * (m - 1))
                        nc.scalar.activation(V[:, b, VG * group:VG * group + VG, :],
                                             QV[VBANK[group]][0:CHK, 0:VG * P].rearrange("p (c n) -> p c n", c=VG),
                                             ACT.Copy).then_inc(v_ready, 1)

                def exps(i, par, p, d):
                    s, b, m, pp, g = pair_at(i, par, p, d)
                    if exists(s):
                        wait(act, scored, 2 * (g + 1))
                        wait(act, normed, g - 1)
                        wait(act, rec_done, g - 1)
                        for t in range(2):
                            nc.scalar.activation(E[:, pp % 2, t, :], S[:, pp % 2, t, :], ACT.Exp,
                                                 bias=smin[:, pp % 2, t:t + 1], scale=-1.0,
                                                 accum_out=esum[:, pp % 2, t:t + 1]).then_inc(exp_done, 1)

                def store_pt(i, par, p, d):
                    s, b, m, pp, g = pair_at(i, par, p, d)
                    if exists(s):
                        wait(act, p_turned, g + 1)
                        wait(act, pv_done, g - 1)
                        nc.scalar.activation(PT[:, pp % 2].rearrange("p c t n -> p (c t n)"), PP[pp % 2][0:CHK, :],
                                             ACT.Copy).then_inc(pt_ready, 1)

                def store_attn(i, par, d):
                    s, b, m = strip_at(i, par, d)
                    if exists(s):
                        wait(act, pv_done, PAIRS * (m + 1))
                        wait(act, strip_ready, m + 3 if not isinstance(m, int) else min(m + 3, NSTRIP))
                        nc.scalar.activation(Y[:, b, PADT:PADT + H, bass.ds(s * QC + R, QC)],
                                             OP[b][:].rearrange("p (r c) -> p r c", c=QC), ACT.Copy).then_inc(attn_stored, 1)

                def steps(i):
                    for par in range(2):
                        for p in range(PAIRS):
                            exps(i, par, p, 2)
                            store_pt(i, par, p, 0)
                            if p in (3, 5, 7):
                                store_v(i, par, 1, (p - 3) // 2)
                            if p == 1:
                                store_attn(i, par, -1)

                for group in range(3):
                    store_v(0, 0, 0, group)
                exps(0, 0, 0, 0)
                exps(0, 0, 1, 0)
                over_strips(act, steps)
                store_attn(STRIPS - 1, 1, 0)

            @block.tensor
            def _(pe):
                mm = nc.tensor.matmul

                def queries(i, par, d):
                    s, b, m = strip_at(i, par, d)
                    if exists(s):
                        wait(pe, strip_ready, m + 1)
                        wait(pe, v_ready, 3 * m)
                        mm(QV[0][:], WQ[:], ystrip[:, b, PADT:PADT + H, R:R + QC], start=True, stop=True).then_inc(qv_made, 1)

                def values(i, par, d, group):
                    s, b, m = strip_at(i, par, d)
                    if exists(s):
                        if group == 2:
                            wait(pe, q_ready, HEADS * (m + 1))
                        else:
                            wait(pe, v_ready, 3 * m + group)
                        for c in range(VG):
                            ch = VG * group + c
                            ins = mm(QV[VBANK[group]][0:CHK, c * P:(c + 1) * P],
                                     ystrip[:, b, CHR * ch:CHR * (ch + 1), :].rearrange("p r c -> p (r c)"), WV[:],
                                     start=True, stop=True)
                        ins.then_inc(qv_made, 1)

                def scores(i, par, p, d):
                    s, b, m, pp, g = pair_at(i, par, p, d)
                    if exists(s):
                        wait(pe, q_ready, HEADS * (m + 1))
                        wait(pe, scored, 2 * (g - 1))
                        for t in range(2):
                            tile = 2 * pp + t
                            ins = mm(SP[pp % 2][:, t * NK:(t + 1) * NK],
                                     Q[:, b, tile].rearrange("p h q -> p (h q)"),
                                     KEY[:, b, QR * tile:QR * tile + KR, bass.ds(s * QC, KC)], start=True, stop=True)
                        ins.then_inc(s_made, 1)

                def turn(i, par, p, d):
                    s, b, m, pp, g = pair_at(i, par, p, d)
                    if exists(s):
                        wait(pe, normed, g + 1)
                        wait(pe, pt_ready, g - 1)
                        for c in range(2):
                            for t in range(2):
                                at = (2 * c + t) * P
                                ins = nc.tensor.transpose(PP[pp % 2][0:CHK, at:at + P],
                                                          FR[:, pp % 2, (2 * t + c) * CHK:(2 * t + c + 1) * CHK], ident)
                        ins.then_inc(p_turned, 1)

                def weigh(i, par, p, d):
                    s, b, m, pp, g = pair_at(i, par, p, d)
                    if exists(s):
                        wait(pe, pt_ready, g + 1)
                        wait(pe, v_ready, 3 * (m + 1))
                        if pp == 0:
                            wait(pe, attn_stored, m - 1)
                        for h in range(HEADS):
                            hs = slice(h * DH, (h + 1) * DH)
                            for c in range(2):
                                ins = mm(OP[b][hs, 2 * NQ * pp:2 * NQ * (pp + 1)], V[:, b, pp + c, hs],
                                         PT[:, pp % 2, c, :, hs], start=c == 0, stop=c == 1, tile_position=(0, h * DH))
                        ins.then_inc(pv_done, 1)

                def steps(i):
                    for par in range(2):
                        for p in range(PAIRS):
                            turn(i, par, p, 0)
                            scores(i, par, p, 3)
                            weigh(i, par, p, -1)
                            if p == 0:
                                queries(i, par, 1)
                            if p in (2, 4, 6):
                                values(i, par, 1, (p - 2) // 2)

                queries(0, 0, 0)
                for group in range(3):
                    values(0, 0, 0, group)
                for p in range(3):
                    scores(0, 0, p, 0)
                over_strips(pe, steps)
                weigh(STRIPS - 1, 1, PAIRS - 1, 0)

        attn_mem.close()
        with ExitStack() as mem:
            per = {}

            def counter(name, n=1):
                s = sem(name)
                per[name] = (s, n)
                return s

            def done(eng, name, m, n=None):
                s, each = per[name]
                m = min(m, NBLK - 1) if isinstance(m, int) else m
                wait(eng, s, each * m + (each if n is None else n))

            def two(name, shape=(BLK,)):
                return sb(mem, name, [P, B, *shape])

            def one(name):
                return sb(mem, name, [P, 1, BLK])[:].broadcast_to([P, B, BLK])

            aslot = two("aslot")
            rslot2, xslot, rT, xn, xnT, u, uT, x1b = (
                one(n) for n in ("rslot2", "xslot", "rT", "xn", "xnT", "u", "uT", "x1b"))
            x1, t0, t1 = two("x1"), two("t0"), two("t1")
            tn, tnT, eq, ek, rq, rk, qf, kf, kt, am = (
                one(n) for n in ("tn", "tnT", "eq", "ek", "rq", "rk", "qf", "kf", "kt", "am"))
            den, rden = two("den", (T,)), two("rden", (T,))
            td, osum = one("td"), one("osum")
            tdT, base, acc, oT = (two(n) for n in ("tdT", "base", "acc", "oT"))
            prod = sb(mem, "prod", [P, 2, 4, P])
            half = sb(mem, "half", [P, 2, 2, P])
            psum4 = two("psum4")
            gate = two("gate", (T, NE))
            gateT = sb(mem, "gateT", [T * NE, B, P])
            lg, is1, w1_, first, lg2, is2, w2_, second, ga, gb = (
                two(n, (T, NE)) for n in ("lg", "is1", "wt1", "first", "lg2", "is2", "wt2", "second", "ga", "gb"))
            top1, best1, top2, best2, gap, e2, dn, g1, g2 = (
                two(n, (T,)) for n in ("top1", "best1", "top2", "best2", "gap", "e2", "dn", "gt1", "gt2"))
            NORMS = {2: "p", 3: "x1", 4: "u", 5: "t0", 6: "t1"}
            bn = {k: two(f"bn{k}", (T, 6)) for k in NORMS}
            mvs = {k: two(f"mvs{k}", (T, 2)) for k in NORMS}
            ve = {k: two(f"ve{k}", (T,)) for k in NORMS}
            rs = {k: two(f"rs{k}", (T,)) for k in NORMS}
            nb = {k: two(f"nb{k}", (T,)) for k in (3, 5, 6)}
            nm = {k: two(f"nm{k}", (T,)) for k in nb}
            G = [ps(mem, f"G{i}") for i in range(5)]
            M = [ps(mem, f"M{i}") for i in range(2)]
            SPS = ps(mem, "SPS")

            state_zero = sem("state_zero")
            stored = [sem(f"stored{b}") for b in range(B)]
            for name, n in dict(a_copied=1, r_made=1, x_made=1, rt_made=1, rT_ready=1, z1_made=1, xt_made=1, x1_ready=T, x1b_ready=1,
                                xn_ready=T, xn_turned=1, xnT_ready=1, z2_made=1, u_ready=1, u_turned=1, uT_ready=1,
                                z3_made=1, t0_ready=T, p_made=1, tn_ready=T, tn_turned=1, tnT_ready=1, q_made=1,
                                k_made3=1, v_made=1, e_ready=4, v_stored=1, f_ready=2, k_turned=1, kt_ready=1,
                                a_made=1, a_masked=1, num_made=T, state_made=T, state_ready=T, den_ready=2, rden_ready=1,
                                t1_ready=T, td_ready=T, td_turned=1, tdT_ready=1, logits_made=1, gated=1, e2_ready=1,
                                gate_steps=18, g_turned=1, gT_ready=1, eb_made=1, moe_made=2 * T, prods=4 * T, sums=2 * T,
                                chain=4 * T, base_ready=1, osum_ready=1, o_turned=1, oT_ready=1).items():
                counter(name, n)
            for k in NORMS:
                counter(f"stats{k}", T)
                counter(f"mv{k}", T)
                counter(f"ve{k}", 2 if k in nb else 1)
                counter(f"rs{k}", 1)
            for k in nb:
                counter(f"nb{k}", 1)

            inc = lambda ins, name: ins.then_inc(per[name][0], 1)
            tile = lambda t: slice(t * P, (t + 1) * P)
            NPAIR = NBLK // B
            LAG = dict(pre=0, a=1, b=2, e=3, c=4, g=5, d=6, h=7, o=8)
            PEEL = 5

            def over_blocks(eng, steps):
                for i in range(PEEL):
                    steps(i)
                with eng.Fori(PEEL, NPAIR) as i:
                    steps(i)
                for i in range(NPAIR, NPAIR + LAG["o"] // 2):
                    steps(i)

            def stream(i, par, name):
                j, b = shift(i, par - LAG[name])
                return (j, b, B * j + b) if exists(j) else None

            block = mem.enter_context(nc.Block())

            @block.sync
            def _(sp):
                def steps(i):
                    for par in range(2):
                        if s := stream(i, par, "o"):
                            j, b, m = s
                            done(sp, "oT_ready", m)
                            sp.dma_start(out[b][:, bass.ds(j * BLK, BLK)], oT[:, b, :]).then_inc(stored[b], 16)

                over_blocks(sp, steps)
                for b in range(B):
                    sp.wait_ge(stored[b], 16 * NPAIR)

            @block.gpsimd
            def _(pool):
                tt = nc.gpsimd.tensor_tensor
                def rstd(k, s, readers):
                    if s:
                        j, b, m = s
                        done(pool, f"mv{k}", m)
                        done(pool, f"rs{k}", m - 2)
                        inc(tt(ve[k][:, b, :], mvs[k][:, b, :, 1], eps[:], ALU.add), f"ve{k}")
                        if k in nb:
                            done(pool, f"nb{k}", m - 2)
                            inc(tt(nm[k][:, b, :], mvs[k][:, b, :, 0], minus[:], ALU.mult), f"ve{k}")
                        done(pool, f"ve{k}", m, 1)
                        done(pool, readers, m - 2)
                        inc(tt(rs[k][:, b, :], ve[k][:, b, :], halfneg[:], ALU.pow), f"rs{k}")
                        if k in nb:
                            done(pool, f"rs{k}", m)
                            done(pool, f"ve{k}", m)
                            inc(tt(nb[k][:, b, :], nm[k][:, b, :], rs[k][:, b, :], ALU.mult), f"nb{k}")

                def sums(s, t):
                    if s:
                        j, b, m = s
                        done(pool, "prods", m, 4 * t + 4)
                        inc(tt(half[:, t % 2], prod[:, t % 2, 0:2, :], prod[:, t % 2, 2:4, :], ALU.add), "sums")
                        done(pool, "sums", m, 2 * t + 1)
                        done(pool, "osum_ready", m - 2)
                        inc(tt(psum4[:, b, tile(t)], half[:, t % 2, 0, :], half[:, t % 2, 1, :], ALU.add), "sums")

                def steps(i):
                    for par in range(2):
                        pre, a, b_, e, c, g, d, h, o = (stream(i, par, n) for n in LAG)
                        rstd(3, b_, "xn_ready")
                        rstd(4, e, "t0_ready")
                        rstd(6, g, "td_ready")
                        sums(h, 0)
                        rstd(5, e, "tn_ready")
                        sums(h, 1)
                        if b_:
                            j, b, m = b_
                            done(pool, "xt_made", m - 1)
                            inc(tt(xslot[:, b, :], X[:, b, bass.ds(j * BLK, BLK)], b3[:].broadcast_to([P, BLK]), ALU.add),
                                "x_made")
                        sums(h, 2)
                        rstd(2, a, "x1_ready")
                        sums(h, 3)
                        if h:
                            j, b, m = h
                            done(pool, "chain", m)
                            done(pool, "sums", m)
                            done(pool, "o_turned", m - 1)
                            inc(tt(osum[:, b, :], acc[:, b, :], psum4[:, b, :], ALU.add), "osum_ready")

                pool.wait_ge(preset, 5)
                over_blocks(pool, steps)

            @block.scalar
            def _(act):
                copy = lambda dst, src: nc.scalar.activation(dst, src, ACT.Copy)

                def apply(k, s, dst, src, name, reader, tiles=range(T)):
                    if s:
                        j, b, m = s
                        done(act, f"nb{k}", m)
                        done(act, reader, m - 1)
                        for t in tiles:
                            inc(nc.scalar.activation(dst[:, b, tile(t)], src[:, b, tile(t)], ACT.Identity,
                                                     bias=nb[k][:, b, t:t + 1], scale=rs[k][:, b, t:t + 1]), name)

                def evacuate(s, dst, src, made, name, reader, depth=1):
                    if s:
                        j, b, m = s
                        done(act, made, m)
                        done(act, reader, m - depth)
                        inc(copy(dst[:, b, :], src[:]), name)

                def experts(s, t):
                    if s:
                        j, b, m = s
                        done(act, "gated", m)
                        done(act, "moe_made", m, 2 * t + 1)
                        if t >= 2:
                            done(act, "sums", m, 2 * (t - 2) + 1)
                        else:
                            done(act, "sums", m - 1, 2 * (t + 2) + 1)
                        for e in range(4):
                            inc(nc.scalar.activation(prod[:, t % 2, e, :], M[0][:, tile(e)], ACT.Copy,
                                                     scale=gate[:, b, t, e:e + 1]), "prods")

                def features(s, n, bank, made, bias, e, r):
                    if s:
                        j, b, m = s
                        bias = vec[:, VI[bias]:VI[bias] + 1]
                        done(act, made, m)
                        done(act, "f_ready", m - 1)
                        inc(nc.scalar.activation(e[:, b, :], bank[:], ACT.Exp, bias=bias), "e_ready")
                        inc(nc.scalar.activation(r[:, b, :], bank[:], ACT.Relu, bias=bias), "e_ready")

                def running(s, tiles):
                    if s:
                        j, b, m = s
                        for t in tiles:
                            done(act, "state_made", m, t + 1)
                            done(act, "num_made", m, t)
                            inc(copy(state[:, b, (t + 1) % 2, :], SPS[:, b * (P + 1):(b + 1) * (P + 1)]), "state_ready")

                def steps(i):
                    for par in range(2):
                        pre, a, b_, e, c, g, d, h, o = (stream(i, par, n) for n in LAG)
                        evacuate(b_, rT, G[0], "rt_made", "rT_ready", "x1_ready")
                        if h:
                            j, b, m = h
                            done(act, "gate_steps", m, 13)
                            done(act, "gated", m - 2)
                            inc(nc.scalar.activation(e2[:, b, :], gap[:, b, :], ACT.Exp), "e2_ready")
                        running(g, (0,))
                        evacuate(e, xnT, G[2], "xn_turned", "xnT_ready", "z2_made")
                        running(g, (1,))
                        apply(5, c, tn, t0, "tn_ready", "tn_turned", (0, 1))
                        if e:
                            j, b, m = e
                            done(act, "z2_made", m)
                            done(act, "u_turned", m - 1)
                            done(act, "stats4", m - 1)
                            inc(nc.scalar.activation(u[:, b, :], G[2][:], ACT.Relu), "u_ready")
                        if h:
                            j, b, m = h
                            done(act, "g_turned", m)
                            done(act, "eb_made", m - 2)
                            inc(copy(gateT[:, b, :], M[1][0:T * NE, 0:P]), "gT_ready")
                        if o:
                            j, b, m = o
                            done(act, "o_turned", m)
                            wait(act, stored[b], 16 * j)
                            inc(copy(oT[:, b, :], G[4][:]), "oT_ready")
                        apply(5, c, tn, t0, "tn_ready", "tn_turned", (2, 3))
                        running(g, (2, 3))
                        experts(h, 0)
                        evacuate(e, uT, G[2], "u_turned", "uT_ready", "z3_made")
                        evacuate(c, tnT, G[0], "tn_turned", "tnT_ready", "v_made")
                        apply(3, b_, xn, x1, "xn_ready", "xn_turned")
                        experts(h, 1)
                        features(c, 0, G[0], "q_made", "lbq", eq, rq)
                        evacuate(d, tdT, G[3], "td_turned", "tdT_ready", "moe_made", depth=2)
                        features(c, 1, G[1], "k_made3", "lbk", ek, rk)
                        apply(6, g, td, t1, "td_ready", "td_turned")
                        experts(h, 2)
                        if c:
                            j, b, m = c
                            done(act, "v_made", m)
                            done(act, "num_made", m - 2)
                            inc(copy(va[:, b, :, 0:P], G[4][:].rearrange("p (t n) -> p t n", t=T)), "v_stored")
                        evacuate(c, kt, G[0], "k_turned", "kt_ready", "state_made")
                        experts(h, 3)

                act.wait_ge(preset, 5)
                over_blocks(act, steps)

            @block.vector
            def _(dve):
                tt, stt, ts = nc.vector.tensor_tensor, nc.vector.scalar_tensor_tensor, nc.vector.tensor_scalar

                def stats(k, s, src, made, between=lambda: None):
                    if s:
                        j, b, m = s
                        done(dve, made, m)
                        done(dve, f"mv{k}", m - 2)
                        for t in range(T):
                            inc(nc.vector.bn_stats(bn[k][:, b, t, :], src(b, t)), f"stats{k}")
                            between()
                        done(dve, f"nb{k}" if k in nb else f"rs{k}", m - 2)
                        done(dve, f"stats{k}", m)
                        settle(dve, passed["dve"])
                        for t in range(T):
                            inc(nc.vector.bn_aggr(mvs[k][:, b, t, :], bn[k][:, b, t, :]), f"mv{k}")

                def experts(s, t, between=lambda: None):
                    if s:
                        j, b, m = s
                        done(dve, "moe_made", m, 2 * t + 2)
                        done(dve, "gated", m)
                        done(dve, "base_ready", m)
                        done(dve, "osum_ready", m - 2)
                    for e in range(4):
                        if s:
                            if e:
                                done(dve, "chain", m, 4 * t + e)
                            inc(stt(acc[:, b, tile(t)], M[1][:, tile(e)], gate[:, b, t, 4 + e:5 + e],
                                    (acc if e else base)[:, b, tile(t)], ALU.mult, ALU.add), "chain")
                        between()

                def gating(s, n):
                    if not s:
                        return
                    j, b, m = s
                    wide = lambda v: v[:, b, :].unsqueeze(2).broadcast_to([P, T, NE])

                    def pick(n, logits, top, same, weight, best, chosen):
                        if n == 0:
                            return nc.vector.tensor_reduce(top[:, b, :], logits[:, b], AX_X, ALU.max)
                        if n == 1:
                            return tt(same[:, b], logits[:, b], wide(top), ALU.is_equal)
                        if n == 2:
                            return tt(weight[:, b], same[:, b], rank[:], ALU.mult)
                        if n == 3:
                            return nc.vector.tensor_reduce(best[:, b, :], weight[:, b], AX_X, ALU.max)
                        return tt(chosen[:, b], weight[:, b], wide(best), ALU.is_equal)

                    if n == 0:
                        done(dve, "logits_made", m)
                        done(dve, "gated", m - 2)
                        done(dve, "e2_ready", m - 2)
                        ins = tt(lg[:, b], G[3][:, 0:T * NE].rearrange("p (t e) -> p t e", t=T),
                                 RB[:].unsqueeze(1).broadcast_to([P, T, NE]), ALU.add)
                    else:
                        done(dve, "gate_steps", m, n)
                    if 1 <= n <= 5:
                        ins = pick(n - 1, lg, top1, is1, w1_, best1, first)
                    elif n == 6:
                        ins = stt(lg2[:, b], first[:, b], -3.0e38, lg[:, b], ALU.mult, ALU.add)
                    elif 7 <= n <= 11:
                        ins = pick(n - 7, lg2, top2, is2, w2_, best2, second)
                    elif n == 12:
                        ins = tt(gap[:, b, :], top2[:, b, :], top1[:, b, :], ALU.subtract)
                    elif n == 13:
                        done(dve, "e2_ready", m)
                        ins = nc.vector.tensor_scalar_add(dn[:, b, :], e2[:, b, :], 1.0)
                    elif n == 14:
                        ins = nc.vector.reciprocal(g1[:, b, :], dn[:, b, :])
                    elif n == 15:
                        ins = tt(g2[:, b, :], g1[:, b, :], e2[:, b, :], ALU.mult)
                    elif n == 16:
                        ins = tt(ga[:, b], first[:, b], wide(g1), ALU.mult)
                    elif n == 17:
                        ins = tt(gb[:, b], second[:, b], wide(g2), ALU.mult)
                    elif n == 18:
                        done(dve, "prods", m - 2)
                        done(dve, "g_turned", m - 2)
                        done(dve, "chain", m - 2)
                        inc(tt(gate[:, b], ga[:, b], gb[:, b], ALU.add), "gated")
                        return
                    inc(ins, "gate_steps")

                LATE = 13

                def features(s, n, e, r, f):
                    if s:
                        j, b, m = s
                        done(dve, "e_ready", m, 2 * n + 2)
                        done(dve, "a_made", m - 1)
                        done(dve, "num_made", m - 1)
                        inc(stt(f[:, b, :], e[:, b, :], 1.0, r[:, b, :], ALU.min, ALU.add), "f_ready")

                def steps(i):
                    for par in range(2):
                        pre, a, b_, e, c, g, d, h, o = (stream(i, par, n) for n in LAG)
                        late = list(range(LATE, per["gate_steps"][1] + 1))

                        def late_gate_step():
                            if late:
                                gating(h, late.pop(0))

                        if b_:
                            j, b, m = b_
                            done(dve, "rT_ready", m)
                            done(dve, "z1_made", m)
                            done(dve, "rs2", m)
                            done(dve, "xn_ready", m - 2)
                            done(dve, "x1b_ready", m - 2)
                        for t in range(T):
                            if b_:
                                inc(stt(x1[:, b, tile(t)], G[1][:, tile(t)], rs[2][:, b, t:t + 1], rT[:, b, tile(t)],
                                        ALU.mult, ALU.add), "x1_ready")
                            late_gate_step()
                        stats(3, b_, lambda b, t: x1[:, b, tile(t)], "x1_ready", late_gate_step)
                        while late:
                            late_gate_step()
                        if a:
                            j, b, m = a
                            done(dve, "rt_made", m - 1)
                            inc(ts(rslot2[:, b, :], X[:, b, bass.ds(j * BLK, BLK)], gn_scale[:, b:b + 1],
                                   res_bias[:, b:b + 1], ALU.mult, ALU.add), "r_made")
                        if pre:
                            j, b, m = pre
                            done(dve, "z1_made", m - 2)
                            inc(nc.vector.tensor_copy(aslot[:, b, :].rearrange("p (r c) -> p r c", c=W),
                                                      Y[:, b, bass.ds(j * BROWS + PADT, BROWS), R:R + W]), "a_copied")
                        if h:
                            j, b, m = h
                            done(dve, "eb_made", m)
                            done(dve, "chain", m - 2)
                            inc(tt(base[:, b, :], t1[:, b, :], M[1][:], ALU.add), "base_ready")
                        stats(4, e, lambda b, t: u[:, b, tile(t)], "u_ready")
                        if g:
                            j, b, m = g
                            done(dve, "num_made", m)
                            done(dve, "rden_ready", m - 2)
                            for n, bank in enumerate((G[3], G[4])):
                                inc(nc.vector.tensor_scalar_add(
                                    den[:, b, 2 * n:2 * n + 2],
                                    bank[:, 0:2 * (P + 1)].rearrange("p (t n) -> p t n", t=2)[:, :, P], 1e-6), "den_ready")
                            done(dve, "den_ready", m)
                            done(dve, "t1_ready", m - 2)
                            inc(nc.vector.reciprocal(rden[:, b, :], den[:, b, :]), "rden_ready")
                            done(dve, "rden_ready", m)
                            done(dve, "base_ready", m - 2)
                            done(dve, "td_ready", m - 2)
                            for t in range(T):
                                bank, at = (G[3], G[4])[t // 2], (t % 2) * (P + 1)
                                inc(stt(t1[:, b, tile(t)], bank[:, at:at + P], rden[:, b, t:t + 1], t0[:, b, tile(t)],
                                        ALU.mult, ALU.add), "t1_ready")
                        experts(h, 0)
                        stats(6, g, lambda b, t: t1[:, b, tile(t)], "t1_ready")
                        if e:
                            j, b, m = e
                            done(dve, "xt_made", m)
                            done(dve, "t0_ready", m - 1)
                            inc(tt(x1b[:, b, :], x1[:, b, :], G[1][:], ALU.add), "x1b_ready")
                            done(dve, "z3_made", m)
                            done(dve, "rs4", m)
                            done(dve, "x1b_ready", m)
                            done(dve, "t1_ready", m - 2)
                            for t in range(T):
                                inc(stt(t0[:, b, tile(t)], G[2][:, tile(t)], rs[4][:, b, t:t + 1], x1b[:, b, tile(t)],
                                        ALU.mult, ALU.add), "t0_ready")
                        experts(h, 1)
                        stats(5, e, lambda b, t: t0[:, b, tile(t)], "t0_ready")
                        features(c, 0, eq, rq, qf)
                        features(c, 1, ek, rk, kf)
                        n = 0

                        def gate_step():
                            nonlocal n
                            if n < LATE:
                                gating(d, n)
                                n += 1

                        experts(h, 2, gate_step)
                        stats(2, a, lambda b, t: G[2][:, tile(t)], "p_made", gate_step)
                        while n < 8:
                            gate_step()
                        if c:
                            j, b, m = c
                            done(dve, "a_made", m)
                            done(dve, "num_made", m - 1)
                            inc(tt(am[:, b, :].rearrange("p (t n) -> p t n", t=T),
                                   G[1][:].rearrange("p (t n) -> p t n", t=T),
                                   causal.unsqueeze(1).broadcast_to([P, T, P]), ALU.mult), "a_masked")
                        experts(h, 3, gate_step)
                        gate_step()
                        gate_step()
                        gate_step()
                        while n < LATE:
                            gate_step()

                dve.wait_ge(lw_in, 64)
                dve.wait_ge(preset, 5 + NE)
                over_blocks(dve, steps)

            @block.tensor
            def _(pe):
                mm, turn = nc.tensor.matmul, nc.tensor.transpose

                def bias(bank, name):
                    mm(bank[:].rearrange("p (t n) -> p t n", t=T), ones3[:],
                       bias3[:, BIAS.index(name)].unsqueeze(1).broadcast_to([96, T, P]), start=True, stop=False,
                       skip_group_check=True)

                def linear(bank, src, b, w, last=True):
                    for t in range(T):
                        ins = mm(bank[:, tile(t)], src[:, b, tile(t)], w, start=False, stop=True, skip_group_check=True)
                    return ins

                def turned(s, bank, src, ready, released, name):
                    if s:
                        j, b, m = s
                        done(pe, ready, m)
                        released(m)
                        for t in range(T):
                            ins = turn(bank[:, tile(t)], src[:, b, tile(t)], ident)
                        inc(ins, name)

                def experts(s, t):
                    if s:
                        j, b, m = s
                        done(pe, "tdT_ready", m)
                        done(pe, "prods", m, 4 * t)
                        inc(mm(M[0][:], tdT[:, b, tile(t)], EW[:, 0:BLK], start=True, stop=True), "moe_made")
                        done(pe, "chain", m, 4 * t)
                        done(pe, "base_ready", m)
                        inc(mm(M[1][:], tdT[:, b, tile(t)], EW[:, BLK:], start=True, stop=True), "moe_made")

                def num(s, tiles):
                    if s:
                        j, b, m = s
                        mine = slice(b * (P + 1), (b + 1) * (P + 1))
                        for t in tiles:
                            out = (G[3], G[4])[t // 2][:, (t % 2) * (P + 1):(t % 2 + 1) * (P + 1)]
                            mm(out, am[:, b, tile(t)], va[:, b, t, :], start=True, stop=False)
                            if t:
                                done(pe, "state_ready", m, t)
                            else:
                                done(pe, "state_ready", m - 1)
                            inc(mm(SPS[:, mine], kt[:, b, tile(t)], va[:, b, t, :], start=False, stop=True,
                                   skip_group_check=True), "state_made")
                            inc(mm(out, qf[:, b, tile(t)], state[:, b, t % 2, :], start=False, stop=True), "num_made")

                def steps(i):
                    for par in range(2):
                        pre, a, b_, e, c, g, d, h, o = (stream(i, par, n) for n in LAG)
                        turned(b_, G[0], rslot2, "r_made", lambda m: done(pe, "kt_ready", m - 3), "rt_made")
                        turned(e, G[2], xn, "xn_ready", lambda m: done(pe, "stats2", m + 1), "xn_turned")
                        if b_:
                            j, b, m = b_
                            done(pe, "a_copied", m)
                            done(pe, "a_masked", m - 3)
                            bias(G[1], "z1")
                            inc(linear(G[1], aslot, b, WPZ[:]), "z1_made")
                        if g:
                            j, b, m = g
                            done(pe, "kt_ready", m)
                            done(pe, "a_masked", m)
                            done(pe, "v_stored", m)
                            done(pe, "gate_steps", m - 2, 1)
                        num(g, (0, 1))
                        if e:
                            j, b, m = e
                            done(pe, "xnT_ready", m)
                            bias(G[2], "z2")
                            inc(linear(G[2], xnT, b, W2[:]), "z2_made")
                        if h:
                            j, b, m = h
                            done(pe, "gated", m)
                            done(pe, "chain", m - 1)
                            inc(turn(M[1][0:T * NE, 0:P], gate[:, b].rearrange("p t e -> p (t e)"), ident), "g_turned")
                        turned(o, G[4], osum, "osum_ready", lambda m: done(pe, "v_stored", m + 3), "o_turned")
                        if h:
                            j, b, m = h
                            done(pe, "gT_ready", m)
                            inc(mm(M[1][:], gateT[:, b, :], EBX[:].rearrange("p t n -> p (t n)"), start=True, stop=True),
                                "eb_made")
                        if g:
                            done(pe, "oT_ready", g[2] - 3)
                        num(g, (2, 3))
                        experts(h, 0)
                        turned(e, G[2], u, "u_ready", lambda m: None, "u_turned")
                        turned(c, G[0], tn, "tn_ready", lambda m: done(pe, "rT_ready", m + 2), "tn_turned")
                        turned(e, G[1], xslot, "x_made", lambda m: done(pe, "x1_ready", m + 1), "xt_made")
                        if e:
                            j, b, m = e
                            done(pe, "uT_ready", m)
                            for t in range(T):
                                ins = mm(G[2][:, tile(t)], uT[:, b, tile(t)], W3[:], start=True, stop=True)
                            inc(ins, "z3_made")
                        experts(h, 1)
                        if c:
                            j, b, m = c
                            done(pe, "tnT_ready", m)
                            inc(mm(G[0][:], LW[:, 0, :], tnT[:, b, :], start=True, stop=True), "q_made")
                        turned(d, G[3], td, "td_ready", lambda m: done(pe, "t1_ready", m + 1), "td_turned")
                        if c:
                            j, b, m = c
                            done(pe, "x1b_ready", m + 1)
                            inc(mm(G[1][:], LW[:, 1, :], tnT[:, b, :], start=True, stop=True), "k_made3")
                        experts(h, 2)
                        if d:
                            j, b, m = d
                            done(pe, "tdT_ready", m)
                            for t in range(T):
                                ins = mm(G[3][:, t * NE:(t + 1) * NE], tdT[:, b, tile(t)], RW[:], start=True, stop=True)
                            inc(ins, "logits_made")
                        if c:
                            j, b, m = c
                            done(pe, "t1_ready", m - 1)
                            bias(G[4], "v")
                            inc(linear(G[4], tnT, b, LW[:, 2, :]), "v_made")
                        if a:
                            j, b, m = a
                            done(pe, "a_copied", m)
                            done(pe, "t0_ready", m - 2)
                            done(pe, "stats2", m - 1)
                            bias(G[2], "p")
                            inc(linear(G[2], aslot, b, WP), "p_made")
                        turned(c, G[0], kf, "f_ready", lambda m: None, "k_turned")
                        if c:
                            j, b, m = c
                            for t in range(T):
                                ins = mm(G[1][:, tile(t)], kf[:, b, tile(t)], qf[:, b, tile(t)], start=True, stop=True)
                            inc(ins, "a_made")
                        experts(h, 3)

                pe.wait_ge(lw_in, 64)
                pe.wait_ge(ebx_in, 64)
                pe.wait_ge(preset, 5)
                mm(SPS[:, 0:B * (P + 1)], ones3[:], zero3[:], start=True, stop=True).then_inc(state_zero, 1)
                pe.wait_ge(state_zero, 1)
                over_blocks(pe, steps)


def constants():
    eye = np.eye(P, dtype=np.float32)
    group = np.kron(np.eye(GROUPS), np.full((C // GROUPS, C // GROUPS), GROUPS / C)).astype(np.float32)
    center = (np.eye(P) - np.full((P, P), 1.0 / P)).astype(np.float32)
    causal = np.triu(np.ones((P, P), np.float32))
    return np.concatenate([eye, group, center, causal], axis=1)


def kernel(**inputs):
    import concourse.bacc as bacc
    from concourse.bass_utils import run_bass_kernel_spmd as run

    g = {k: np.asarray(v) for k, v in inputs.items()}
    L0, L1 = "L0_conv_", "L1_"
    qkvb, lab = g[L0 + "qkv_b"], g[L1 + "attn_b"]
    col = {**{n: g[L0 + n] for n in ("g1", "be1", "g2", "be2", "g3", "be3", "g4", "be4", "bl1", "bl3")},
           "bq": qkvb[0:C], "bk": qkvb[C:2 * C], "bv": qkvb[2 * C:], "bp": g[L0 + "proj_b"],
           "lbq": lab[0:C], "lbk": lab[C:2 * C]}
    side = lambda ws: np.stack([w.T for w in ws], axis=1)
    arrays = {
        "x": g["x"].reshape(B, C, TOK),
        "kept": np.concatenate([np.stack([col[n] for n in VEC], axis=1), g[L0 + "proj_w"].T, constants()], axis=1),
        "prep": side(np.split(g[L0 + "qkv_w"], 3) + [g[L0 + "w1"], g[L0 + "w2"], g[L0 + "w3"], g[L0 + "proj_w"].T]),
        "rows": np.stack([g[L0 + "proj_b"], g[L0 + "bl2"], lab[2 * C:]])[None],
        "rpb": g[L0 + "rpb"],
        "laT": side(np.split(g[L1 + "attn_W"], 3)),
        "expw": g[L1 + "ffn_expert_w"].transpose(1, 0, 2).reshape(C, NE * C),
        "rw": g[L1 + "ffn_router_w"],
        "rb": g[L1 + "ffn_router_b"].reshape(1, NE),
        "expb": g[L1 + "ffn_expert_b"],
    }
    arrays = {k: np.ascontiguousarray(v) for k, v in arrays.items()}
    nc = bacc.Bacc("TRN2", target_bir_lowering=False, num_devices=1)
    args = {k: nc.dram_tensor("in_" + k, v.shape, mybir.dt.from_np(v.dtype), kind="ExternalInput").ap()
            for k, v in arrays.items()}
    out = nc.dram_tensor("out", (B, C, TOK), F32, kind="ExternalOutput").ap()
    build(nc, out=out, **args)
    r = run(nc, [{"in_" + k: v for k, v in arrays.items()}], core_ids=[0])
    return r.results[0]["out"].reshape(B, C, H, W)
```

```python
from contextlib import ExitStack

import numpy as np

import concourse.bass as bass
from concourse import mybir

F32 = mybir.dt.float32
BF16 = mybir.dt.bfloat16
ALU = mybir.AluOpType
ACT = mybir.ActivationFunctionType
AX_X = mybir.AxisListType.X

B, C, H, W = 2, 128, 64, 64
TOK = H * W
HEADS, DH, K = 4, 32, 7
GROUPS = 32
NE = 8
P = 128

R = K // 2
QR, QC = 4, 8
KR, KC = QR + 2 * R, QC + 2 * R
NK = KR * KC
PW = W + 2 * R
PADT = 4
YH = H + 2 * PADT
KH = H + 2 * R
CHR = 8
CHK = CHR * KC
NCH = YH // CHR
STRIPS = W // QC
NSTRIP = B * STRIPS
TILES = H // QR
PAIRS = TILES // 2
NQ = QR * QC
BLK = 512
BROWS = BLK // W
NBLK = B * TOK // BLK
T = BLK // P
FAR = -1.0e30

VEC = ["g1", "be1", "g2", "be2", "g3", "be3", "g4", "be4", "bq", "bk", "bv", "bp", "bl1", "bl3", "lbq", "lbk", "bl2"]
VI = {n: i for i, n in enumerate(VEC)}
ROWS = ["bp", "lbv"]
BIAS = ["p", "z1", "v"]


def shift(i, d):
    return i + d // 2, d % 2


def exists(j):
    return not isinstance(j, int) or 0 <= j < NBLK // 2


def wait(eng, sem, value):
    if isinstance(value, int) and value <= 0:
        return
    eng.wait_ge(sem, value)


def settle(eng, passed):
    eng.sem_inc(passed, 1)


def build(nc, x, kept, prep, rows, rpb, laT, expw, rw, rb, expb, out):
    ctx = ExitStack()
    with ctx:
        names = {}

        def sb(stack, name, shape, dt=F32):
            return stack.enter_context(nc.sbuf_tensor(name, shape, dt))

        def ps(stack, name, shape=(P, 512), dt=F32):
            return stack.enter_context(nc.psum_tensor(name, list(shape), dt))

        def sem(name):
            assert name not in names
            names[name] = ctx.enter_context(nc.semaphore(name))
            return names[name]

        passed = {n: sem(f"passed_{n}") for n in ("dve", "pool")}

        X = sb(ctx, "X", [P, B, TOK])
        keep = sb(ctx, "keep", [P, len(VEC) + 5 * P])
        vec = keep[:, 0:len(VEC)]
        WP, ident, groupavg, center, causal = (keep[:, len(VEC) + k * P:len(VEC) + (k + 1) * P] for k in range(5))
        halfneg = sb(ctx, "halfneg", [P, 4])
        row = sb(ctx, "row", [1, len(ROWS), P])
        gn_scale = sb(ctx, "gn_scale", [P, B])
        gn_bias = sb(ctx, "gn_bias", [P, B])
        wide_in = sb(ctx, "wide_in", [P, 2, B, P])
        b2 = sb(ctx, "b2", [P, 1])
        b3 = sb(ctx, "b3", [P, 1])
        WPZ = sb(ctx, "WPZ", [P, P])
        W2 = sb(ctx, "W2", [P, P])
        W3 = sb(ctx, "W3", [P, P])
        bias3 = sb(ctx, "bias3", [96, len(BIAS), P], BF16)
        ones3 = sb(ctx, "ones3", [96, P], BF16)
        LW = sb(ctx, "LW", [P, 3, P])
        EW = sb(ctx, "EW", [P, NE * P])
        RW = sb(ctx, "RW", [P, NE])
        RB = sb(ctx, "RB", [P, NE])
        EBX = sb(ctx, "EBX", [T * NE, T, P])
        rank = sb(ctx, "rank", [P, T, NE])
        zero3 = sb(ctx, "zero3", [96, B * (P + 1)], BF16)
        va = sb(ctx, "va", [P, B, T, P + 1])
        state = sb(ctx, "state", [P, B, 2, P + 1])
        eps, minus = sb(ctx, "eps", [P, T]), sb(ctx, "minus", [P, T])
        gn_wide = sem("gn_wide")
        lw_in, ebx_zero, ebx_in, preset = sem("lw_in"), sem("ebx_zero"), sem("ebx_in"), sem("preset")
        Y = sb(ctx, "Y", [P, B, YH, PW])

        attn_mem = ctx.enter_context(ExitStack())
        KEY = sb(attn_mem, "KEY", [P, B, KH, PW])
        WQ = sb(attn_mem, "WQ", [P, P])
        WK = sb(attn_mem, "WK", [P, P])
        WV = sb(attn_mem, "WV", [P, P])
        bq = sb(attn_mem, "bq", [P, 1])
        bk = sb(attn_mem, "bk", [P, 1])
        Q = sb(attn_mem, "Q", [P, B, TILES, HEADS, NQ])
        tab = sb(attn_mem, "tab", [P, 3, 3, NK])

        with ExitStack() as mem:
            prep_in = sb(mem, "prep_in", [P, 7, P])
            wqkv_in, w123_in, wp_in = prep_in[:, 0:3, :], prep_in[:, 3:6, :], prep_in[:, 6, :]
            w1g = sb(mem, "w1g", [P, P])
            w1c = sb(mem, "w1c", [P, P])
            w3g = sb(mem, "w3g", [P, P])
            far = sb(mem, "far", [P, 3 * NK])
            bvc = sb(mem, "bvc", [P, 1])
            b1 = sb(mem, "b1", [P, 1])
            res_bias = sb(mem, "res_bias", [P, B])
            b3s = sb(mem, "b3s", [P, B])
            bpc = sb(mem, "bpc", [P, 1])
            XPARTS = 2
            brow = sb(mem, "brow", [1, len(BIAS), P])
            bhi = sb(mem, "bhi", [1, 2, len(BIAS), P], BF16)
            bres = sb(mem, "bres", [1, 2, len(BIAS), P])
            stat = sb(mem, "stat", [P, B, 8, 6])
            mv = sb(mem, "mv", [P, B, 2])
            mom = sb(mem, "mom", [P, B, 2])
            gmom = sb(mem, "gmom", [P, B, 2])
            gvar = sb(mem, "gvar", [P, B])
            gsq = sb(mem, "gsq", [P, B])
            rslot = sb(mem, "rslot", [P, B, BLK])
            tstat = sb(mem, "tstat", [P, B, T, 6])
            tmv = sb(mem, "tmv", [P, B, T, 2])
            tve = sb(mem, "tve", [P, B, T])
            trs = sb(mem, "trs", [P, B, T])
            tnb = sb(mem, "tnb", [P, B, T])
            yn = sb(mem, "yn", [P, B, BLK])
            TA = [ps(mem, f"TA{i}") for i in range(4)]
            TB = [ps(mem, f"TB{i}") for i in range(B)]
            KP = [ps(mem, f"KP{i}") for i in range(B)]
            PREP = KP
            wq_be, wk_be, wv_be, w1_be, w3_be, wp_bv, w2_be = (PREP[0][:, a:a + 1] for a in range(7))
            gsum = PREP[0][:, 8:8 + 2 * B]
            w1c_ps, w3c_ps, wpz_ps = (PREP[1][:, k * P:(k + 1) * P] for k in range(3))
            row_ps = PREP[0][0:1, P:3 * P]
            cdram = nc.dram_tensor("column_bias", [3, HEADS, QC, 2 * K - 1, KC], F32, kind="Internal").ap()
            tdram = nc.dram_tensor("bias_table", [3, 3, HEADS, QR, QC, NK], F32, kind="Internal").ap()

            x_in = [[sem(f"x_in{b}{c}") for c in range(XPARTS)] for b in range(B)]
            kept_in, prep_ready, row_in = sem("kept_in"), sem("prep_ready"), sem("row_in")
            far_set, far_out = sem("far_set"), sem("far_out")
            columns_out, table_out, table_in = sem("columns_out"), sem("table_out"), sem("table_in")
            table_neg, pads_set, const_set = sem("table_neg"), sem("pads_set"), sem("const_set")
            gn_stats, gn_mean, gn_mom, gn_avg, gn_copied = (
                sem(n) for n in ("gn_stats", "gn_mean", "gn_mom", "gn_avg", "gn_copied"))
            gn_sq, gn_var, gn_rstd, gn_done = (sem(n) for n in ("gn_sq", "gn_var", "gn_rstd", "gn_done"))
            w_scaled, prep_cols, prep_mat, cols_done = (sem(n) for n in ("w_scaled", "prep_cols", "prep_mat", "cols_done"))
            w1c_done, prep_bv, bpc_done, prep_rows, rows_done, split_done, wpz_done = (
                sem(n) for n in ("w1c_done", "prep_bv", "bpc_done", "prep_rows", "rows_done", "split_done", "wpz_done"))
            r_ready, r_turned, y_stats, y_mv, y_ve, y_rstd, y_front_ready, y_turned, y_stored, k_made, k_stored = (
                sem(n) for n in ("r_ready", "r_turned", "y_stats", "y_mv", "y_ve", "y_rstd", "y_front_ready", "y_turned",
                                 "y_stored", "k_made", "k_stored"))

            y_nb, y_back_ready, rest_done, res_done = (sem(n) for n in ("y_nb", "y_back_ready", "rest_done", "res_done"))
            block = mem.enter_context(nc.Block())

            def over_quads(eng, steps, first, last, end):
                for k in range(first):
                    steps(2 * k)
                with eng.Fori(first, last) as k:
                    steps(2 * k)
                for k in range(last, end):
                    steps(2 * k)

            @block.sync
            def _(sp):
                sp.dma_start(keep[:], kept).then_inc(kept_in, 16)
                sp.dma_start(prep_in[:], prep).then_inc(prep_ready, 16)
                for b in range(B):
                    for c in range(XPARTS):
                        part = slice(c * TOK // XPARTS, (c + 1) * TOK // XPARTS)
                        sp.dma_start(X[:, b, part], x[b][:, part]).then_inc(x_in[b][c], 16)
                sp.wait_ge(far_set, 1)
                sp.dma_start(cdram.rearrange("c h q a k -> (c h q) (a k)"), far[0:96, 0:13 * KC]).then_inc(far_out, 16)
                for part in range(3):
                    sp.dma_start(tdram.rearrange("r c h a b k -> (r c h a b k)").rearrange("(p n) -> p n", p=P)
                                 [:, part * 3 * NK:(part + 1) * 3 * NK], far[:]).then_inc(far_out, 16)
                sp.wait_ge(far_out, 64)
                for cc, c0 in enumerate((0, QC, W - QC)):
                    for qc in range(QC):
                        start = min(max(c0 + qc - R, 0), W - K)
                        at, idx = start - (c0 - R), start - (c0 + qc) + K - 1
                        sp.dma_start(cdram[cc, :, qc, :, at:at + K],
                                     rpb[:, :, idx:idx + K]).then_inc(columns_out, 16)
                sp.wait_ge(columns_out, 16 * 3 * QC)
                for rc, r0 in enumerate((0, QR, H - QR)):
                    for qr in range(QR):
                        start = min(max(r0 + qr - R, 0), H - K)
                        at, idx = start - (r0 - R), start - (r0 + qr) + K - 1
                        sp.dma_start(tdram[rc, :, :, qr, :, at * KC:(at + K) * KC].rearrange("c h q n -> (c h) q n"),
                                     cdram[:, :, :, idx:idx + K, :].rearrange("c h q a k -> (c h) q (a k)")
                                     ).then_inc(table_out, 16)
                sp.wait_ge(table_out, 16 * 3 * QR)
                for cc in range(3):
                    sp.dma_start(tab[:, cc, :, :], tdram[:, cc].rearrange("r h a b k -> (h a b) r k")).then_inc(table_in, 16)

            @block.gpsimd
            def _(pool):
                nc.gpsimd.memset(far[:], FAR).then_inc(far_set, 1)
                nc.gpsimd.memset(halfneg[:], -0.5).then_inc(const_set, 1)
                nc.gpsimd.memset(ones3[:], 1.0).then_inc(const_set, 1)
                nc.gpsimd.memset(bias3[:], 0.0).then_inc(const_set, 1)
                for b in range(B):
                    nc.gpsimd.memset(Y[:, b, 0:PADT, :], 0.0).then_inc(pads_set, 1)
                    nc.gpsimd.memset(Y[:, b, PADT + H:YH, :], 0.0).then_inc(pads_set, 1)
                    nc.gpsimd.memset(Y[:, b, PADT:PADT + H, 0:R], 0.0).then_inc(pads_set, 1)
                    nc.gpsimd.memset(Y[:, b, PADT:PADT + H, R + W:PW], 0.0).then_inc(pads_set, 1)
                    nc.gpsimd.memset(KEY[:, b, 0:R, :], 0.0).then_inc(pads_set, 1)
                    nc.gpsimd.memset(KEY[:, b, R + H:KH, :], 0.0).then_inc(pads_set, 1)
                    nc.gpsimd.memset(KEY[:, b, R:R + H, 0:R], 0.0).then_inc(pads_set, 1)
                    nc.gpsimd.memset(KEY[:, b, R:R + H, R + W:PW], 0.0).then_inc(pads_set, 1)
                nc.gpsimd.memset(Q[:], 0.0).then_inc(pads_set, 1)
                pool.wait_ge(rows_done, 3)
                pool.wait_ge(split_done, 1)
                nc.gpsimd.tensor_tensor(bres[:, 0], brow[:], bhi[:, 0], ALU.subtract).then_inc(rest_done, 1)
                pool.wait_ge(rest_done, 1)
                pool.wait_ge(split_done, 2)
                nc.gpsimd.tensor_tensor(bres[:, 1], bres[:, 0], bhi[:, 1], ALU.subtract).then_inc(rest_done, 1)
                pool.wait_ge(const_set, 1)
                pool.wait_ge(gn_var, 2)
                nc.gpsimd.tensor_tensor(gn_scale[:], gvar[:], halfneg[:, 0:B], ALU.pow).then_inc(gn_rstd, 1)

                def ln_rstd(i, par):
                    j, b = shift(i, par)
                    if exists(j):
                        m = B * j + b
                        wait(pool, y_ve, m + 1)
                        wait(pool, y_front_ready, T // 2 * (m - 1))
                        wait(pool, y_back_ready, T // 2 * (m - 1))
                        nc.gpsimd.tensor_tensor(trs[:, b, :], tve[:, b, :], halfneg[:], ALU.pow).then_inc(y_rstd, 1)

                def steps(i):
                    for par in range(4):
                        ln_rstd(i, par)
                
                over_quads(pool, steps, 1, 3, 4)
                pool.wait_ge(res_done, 3)
                for b in range(B):
                    for n, column in enumerate((gn_scale, res_bias)):
                        nc.gpsimd.tensor_copy(wide_in[:, n, b, :], column[:, b:b + 1].broadcast_to([P, P])).then_inc(gn_wide, 1)
                nc.gpsimd.memset(EBX[:], 0.0).then_inc(ebx_zero, 1)
                nc.gpsimd.memset(zero3[:], 0.0).then_inc(preset, 1)
                nc.gpsimd.memset(eps[:], 1e-5).then_inc(preset, 1)
                nc.gpsimd.memset(minus[:], -1.0).then_inc(preset, 1)
                nc.gpsimd.memset(va[:, :, :, P:P + 1], 1.0).then_inc(preset, 1)
                nc.gpsimd.memset(state[:], 0.0).then_inc(preset, 1)
                for e in range(NE):
                    nc.gpsimd.memset(rank[:, :, e:e + 1], float(NE - e)).then_inc(preset, 1)

            @block.scalar
            def _(act):
                act.dma_start(row[:], rows).then_inc(row_in, 16)

                act.wait_ge(const_set, 3)
                act.wait_ge(rows_done, 3)
                nc.scalar.activation(bhi[:, 0], brow[:], ACT.Copy).then_inc(split_done, 1)
                act.wait_ge(rest_done, 1)
                nc.scalar.activation(bhi[:, 1], bres[:, 0], ACT.Copy).then_inc(split_done, 1)
                act.wait_ge(split_done, 2)
                for part in range(2):
                    nc.scalar.activation(bias3[32 * part:32 * part + 1, :, :], bhi[:, part], ACT.Copy).then_inc(split_done, 1)
                act.wait_ge(rest_done, 2)
                nc.scalar.activation(bias3[64:65, :, :], bres[:, 1], ACT.Copy).then_inc(split_done, 1)

                def normalise(i, par, d):
                    j, b = shift(i, par + d)
                    if exists(j):
                        m = B * j + b
                        wait(act, r_turned, m - 1)
                        nc.scalar.activation(rslot[:, b, :], X[:, b, bass.ds(j * BLK, BLK)], ACT.Identity,
                                             bias=gn_bias[:, b:b + 1], scale=gn_scale[:, b:b + 1]).then_inc(r_ready, 1)

                def half_apply(i, par):
                    j, b = shift(i, par - 2)
                    if exists(j):
                        m = B * j + b
                        wait(act, y_nb, m + 1)
                        wait(act, y_front_ready, T // 2 * (m + 1))
                        wait(act, y_turned, m - 1)
                        for t in range(T // 2, T):
                            nc.scalar.activation(yn[:, b, t * P:(t + 1) * P], TA[(par - 2) % 4][:, t * P:(t + 1) * P], ACT.Identity,
                                                 bias=tnb[:, b, t:t + 1], scale=trs[:, b, t:t + 1]).then_inc(y_back_ready, 1)

                def store_y(i, par):
                    j, b = shift(i, par - 3)
                    if exists(j):
                        m = B * j + b
                        wait(act, y_turned, m + 1)
                        nc.scalar.activation(Y[:, b, bass.ds(j * BROWS + PADT, BROWS), R:R + W],
                                             TB[b][:].rearrange("p (r c) -> p r c", c=W), ACT.Copy).then_inc(y_stored, 1)

                def store_k(i, par):
                    j, b = shift(i, par - 4)
                    if exists(j):
                        m = B * j + b
                        wait(act, k_made, m + 1)
                        nc.scalar.activation(KEY[:, b, bass.ds(j * BROWS + R, BROWS), R:R + W],
                                             KP[b][:].rearrange("p (r c) -> p r c", c=W), ACT.Identity,
                                             bias=bk[:]).then_inc(k_stored, 1)

                def steps(i):
                    for par in range(4):
                        half_apply(i, par)
                        store_y(i, par)
                        store_k(i, par)
                        normalise(i, par, 2)

                act.wait_ge(cols_done, 3)
                act.wait_ge(pads_set, 16)
                act.wait_ge(gn_done, 1)
                normalise(0, 0, 0)
                normalise(0, 0, 1)
                over_quads(act, steps, 2, 3, 5)

            @block.vector
            def _(dve):
                dve.wait_ge(kept_in, 16)
                dve.wait_ge(prep_ready, 16)

                def gain(dst, src, g, scale=None):
                    a = (scale, ALU.mult) if scale is not None else (None, ALU.bypass)
                    nc.vector.tensor_scalar(dst, src, vec[:, VI[g]:VI[g] + 1], a[0], ALU.mult, a[1]).then_inc(w_scaled, 1)

                gain(w1g[:], w123_in[:, 0, :], "g2")
                gain(w3g[:], w123_in[:, 2, :], "g4")
                gain(WQ[:], wqkv_in[:, 0, :], "g1", -DH ** -0.5)
                gain(WK[:], wqkv_in[:, 1, :], "g1")
                gain(WV[:], wqkv_in[:, 2, :], "g1")
                gain(W2[:], w123_in[:, 1, :], "g3")
                dve.wait_ge(prep_cols, 1)

                def plus(dst, a, v):
                    nc.vector.tensor_tensor(dst, a, vec[:, VI[v]:VI[v] + 1], ALU.add).then_inc(cols_done, 1)

                nc.vector.tensor_scalar(bq[:], wq_be, vec[:, VI["bq"]:VI["bq"] + 1], -DH ** -0.5, ALU.add,
                                        ALU.mult).then_inc(cols_done, 1)
                plus(bk[:], wk_be, "bk")
                plus(bvc[:], wv_be, "bv")
                plus(b3[:], w3_be, "bl3")
                plus(b1[:], w1_be, "bl1")
                plus(b2[:], w2_be, "bl2")
                dve.wait_ge(prep_mat, 1)
                nc.vector.tensor_copy(w1c[:], w1c_ps).then_inc(w1c_done, 1)
                nc.vector.tensor_copy(W3[:], w3c_ps).then_inc(w1c_done, 1)
                dve.wait_ge(prep_bv, 1)
                nc.vector.tensor_tensor(bpc[:], wp_bv, vec[:, VI["bp"]:VI["bp"] + 1], ALU.add).then_inc(bpc_done, 1)
                dve.wait_ge(prep_mat, 2)
                nc.vector.tensor_copy(WPZ[:], wpz_ps).then_inc(wpz_done, 1)

                def moments(b, parts):
                    for part in parts:
                        dve.wait_ge(x_in[b][part], 16)
                        for c in range(part * 8 // XPARTS, (part + 1) * 8 // XPARTS):
                            nc.vector.bn_stats(stat[:, b, c, :], X[:, b, c * 512:(c + 1) * 512]).then_inc(gn_stats, 1)

                moments(0, range(XPARTS))
                dve.wait_ge(row_in, 16)
                dve.wait_ge(prep_rows, 1)
                rp = row_ps.rearrange("p (k c) -> p k c", k=2)
                nc.vector.tensor_tensor(brow[:, 0, :], rp[:, 0, :], row[:, 0, :], ALU.add).then_inc(rows_done, 1)
                nc.vector.tensor_copy(brow[:, 1, :], rp[:, 1, :]).then_inc(rows_done, 1)
                nc.vector.tensor_copy(brow[:, 2, :], row[:, 1, :]).then_inc(rows_done, 1)
                moments(1, range(XPARTS))
                for b in range(B):
                    dve.wait_ge(gn_stats, 8 * (b + 1))
                    nc.vector.bn_aggr(mv[:, b, :], stat[:, b, :, :].rearrange("p c s -> p (c s)")).then_inc(gn_mean, 1)
                dve.wait_ge(gn_mean, 2)
                nc.vector.tensor_copy(mom[:, :, 0], mv[:, :, 0]).then_inc(gn_mom, 1)
                nc.vector.tensor_tensor(gsq[:], mv[:, :, 0], mv[:, :, 0], ALU.mult).then_inc(gn_sq, 1)
                dve.wait_ge(gn_sq, 1)
                nc.vector.tensor_tensor(mom[:, :, 1], gsq[:], mv[:, :, 1], ALU.add).then_inc(gn_mom, 1)
                dve.wait_ge(gn_avg, 1)
                nc.vector.tensor_copy(gmom[:].rearrange("p b s -> p (b s)"), gsum).then_inc(gn_copied, 1)
                dve.wait_ge(gn_copied, 1)
                dve.wait_ge(gn_mom, 2)
                nc.vector.tensor_tensor(gsq[:], gmom[:, :, 0], gmom[:, :, 0], ALU.mult).then_inc(gn_sq, 1)
                dve.wait_ge(gn_sq, 2)
                nc.vector.scalar_tensor_tensor(gvar[:], gmom[:, :, 1], 1e-5, gsq[:], ALU.add, ALU.subtract).then_inc(gn_var, 2)
                dve.wait_ge(gn_rstd, 1)
                nc.vector.scalar_tensor_tensor(gn_bias[:], gmom[:, :, 0], -1.0, gn_scale[:], ALU.mult, ALU.mult).then_inc(gn_done, 1)
                dve.wait_ge(gn_done, 1)
                dve.wait_ge(cols_done, 6)
                nc.vector.tensor_tensor(res_bias[:], gn_bias[:], b1[:].broadcast_to([P, B]), ALU.add).then_inc(res_done, 1)
                nc.vector.tensor_tensor(b3s[:], gn_scale[:], b3[:].broadcast_to([P, B]), ALU.mult).then_inc(res_done, 1)
                dve.wait_ge(res_done, 2)
                nc.vector.tensor_tensor(res_bias[:], res_bias[:], b3s[:], ALU.subtract).then_inc(res_done, 1)

                def stats(i, par):
                    j, b = shift(i, par)
                    if exists(j):
                        m = B * j + b
                        wait(dve, r_turned, m + 1)
                        wait(dve, y_mv, T * (m - 1))
                        for t in range(T):
                            nc.vector.bn_stats(tstat[:, b, t, :], TA[par][:, t * P:(t + 1) * P]).then_inc(y_stats, 1)
                        wait(dve, y_front_ready, T // 2 * (m - 1))
                        wait(dve, y_nb, m - 1)
                        wait(dve, y_stats, T * (m + 1))
                        settle(dve, passed["dve"])
                        for t in range(T):
                            nc.vector.bn_aggr(tmv[:, b, t, :], tstat[:, b, t, :]).then_inc(y_mv, 1)
                        wait(dve, y_mv, T * m + T)
                        wait(dve, y_rstd, m - 1)
                        nc.vector.tensor_scalar_add(tve[:, b, :], tmv[:, b, :, 1], 1e-5).then_inc(y_ve, 1)

                def apply(i, par):
                    j, b = shift(i, par - 2)
                    if exists(j):
                        m = B * j + b
                        wait(dve, y_rstd, m + 1)
                        wait(dve, y_back_ready, T // 2 * (m - 1))
                        nc.vector.scalar_tensor_tensor(tnb[:, b, :], tmv[:, b, :, 0], -1.0, trs[:, b, :], ALU.mult,
                                                       ALU.mult).then_inc(y_nb, 1)
                        wait(dve, y_turned, m - 1)
                        for t in range(T // 2):
                            nc.vector.tensor_scalar(yn[:, b, t * P:(t + 1) * P], TA[(par - 2) % 4][:, t * P:(t + 1) * P],
                                                    tmv[:, b, t, 0:1], trs[:, b, t:t + 1], ALU.subtract,
                                                    ALU.mult).then_inc(y_front_ready, 1)

                def steps(i):
                    for par in range(4):
                        apply(i, par)
                        stats(i, par)

                over_quads(dve, steps, 2, 4, 5)
                dve.wait_ge(table_in, 48)
                nc.vector.tensor_scalar(tab[:], tab[:], -1.0, None, ALU.mult).then_inc(table_neg, 1)

            @block.tensor
            def _(pe):
                mm = nc.tensor.matmul
                pe.wait_ge(kept_in, 16)
                pe.wait_ge(prep_ready, 16)
                v = lambda n: vec[:, VI[n]:VI[n] + 1]
                mm(wq_be, wqkv_in[:, 0, :], v("be1"), start=True, stop=True)
                mm(wk_be, wqkv_in[:, 1, :], v("be1"), start=True, stop=True)
                mm(wv_be, wqkv_in[:, 2, :], v("be1"), start=True, stop=True)
                mm(w1_be, w123_in[:, 0, :], v("be2"), start=True, stop=True)
                mm(w2_be, w123_in[:, 1, :], v("be3"), start=True, stop=True)
                mm(w3_be, w123_in[:, 2, :], v("be4"), start=True, stop=True).then_inc(prep_cols, 1)
                pe.wait_ge(w_scaled, 2)
                mm(w1c_ps, center, w1g[:], start=True, stop=True)
                mm(w3c_ps, center, w3g[:], start=True, stop=True).then_inc(prep_mat, 1)
                pe.wait_ge(cols_done, 6)
                mm(wp_bv, WP, bvc[:], start=True, stop=True).then_inc(prep_bv, 1)
                pe.wait_ge(w1c_done, 2)
                mm(wpz_ps, wp_in, w1c[:], start=True, stop=True).then_inc(prep_mat, 1)
                pe.wait_ge(bpc_done, 1)
                rp = row_ps.rearrange("p (k c) -> p k c", k=2)
                mm(rp[:, 0, :], bvc[:], WP, start=True, stop=True)
                mm(rp[:, 1, :], bpc[:], w1c[:], start=True, stop=True).then_inc(prep_rows, 1)
                pe.wait_ge(gn_mom, 2)
                pe.wait_ge(rows_done, 2)
                mm(gsum, groupavg, mom[:].rearrange("p b s -> p (b s)"), start=True, stop=True).then_inc(gn_avg, 1)
                pe.wait_ge(wpz_done, 1)
                pe.wait_ge(gn_copied, 1)
                pe.wait_ge(w_scaled, 6)

                def turn_r(i, par):
                    j, b = shift(i, par)
                    if exists(j):
                        m = B * j + b
                        wait(pe, r_ready, m + 1)
                        wait(pe, y_front_ready, T // 2 * (m - 3))
                        wait(pe, y_back_ready, T // 2 * (m - 3))
                        for t in range(T):
                            ins = nc.tensor.transpose(TA[par][:, t * P:(t + 1) * P], rslot[:, b, t * P:(t + 1) * P], ident)
                        ins.then_inc(r_turned, 1)

                def turn_y(i, par):
                    j, b = shift(i, par - 2)
                    if exists(j):
                        m = B * j + b
                        wait(pe, y_front_ready, T // 2 * (m + 1))
                        wait(pe, y_back_ready, T // 2 * (m + 1))
                        wait(pe, y_stored, m - 1)
                        for t in range(T):
                            ins = nc.tensor.transpose(TB[b][:, t * P:(t + 1) * P], yn[:, b, t * P:(t + 1) * P], ident)
                        ins.then_inc(y_turned, 1)

                def keys(i, par):
                    j, b = shift(i, par - 4)
                    if exists(j):
                        m = B * j + b
                        wait(pe, y_stored, m + 1)
                        wait(pe, k_stored, m - 1)
                        mm(KP[b][:], WK[:], Y[:, b, bass.ds(j * BROWS + PADT, BROWS), R:R + W],
                           start=True, stop=True).then_inc(k_made, 1)

                def steps(i):
                    for par in range(4):
                        turn_r(i, par)
                        keys(i, par)
                        turn_y(i, par)

                over_quads(pe, steps, 2, 4, 5)

        with ExitStack() as mem:
            ystrip = sb(mem, "ystrip", [P, B, YH, KC])
            tcur = sb(mem, "tcur", [P, B, 3, NK])
            V = sb(mem, "V", [CHK, B, NCH, P])
            S = sb(mem, "S", [P, 2, 2, NK])
            smin = sb(mem, "smin", [P, 2, 2])
            E = sb(mem, "E", [P, 2, 2, NK])
            esum = sb(mem, "esum", [P, 2, 2])
            erec = sb(mem, "erec", [P, 2, 2])
            skip = 2 * CHK + QR * KC
            FR = sb(mem, "FR", [P, 2, KC + 2 * skip])
            frames = FR[:, :, KC:].rearrange("p s (t n) -> p s t n", n=skip)[:, :, :, 0:NK]
            PT = sb(mem, "PT", [CHK, 2, 2, 2, P])
            SP = [ps(mem, f"SP{i}") for i in range(2)]
            PP = [ps(mem, f"PP{i}") for i in range(2)]
            OP = [ps(mem, f"OP{i}") for i in range(2)]
            QV = [ps(mem, f"QV{i}") for i in range(2)]
            VG = 3
            VBANK = (1, 1, 0)
            frames_zero = sem("frames_zero")
            strip_ready, table_ready, qv_made, q_ready, v_ready = (
                sem(n) for n in ("strip_ready", "table_ready", "qv_made", "q_ready", "v_ready"))
            s_made, scored, exp_done, rec_done, normed, p_turned, pt_ready, pv_done, attn_stored = (
                sem(n) for n in ("s_made", "scored", "exp_done", "rec_done", "normed", "p_turned", "pt_ready",
                                 "pv_done", "attn_stored"))
            block = mem.enter_context(nc.Block())

            def strip_at(i, par, d):
                j, b = shift(i, par + d)
                return j, b, B * j + b

            def pair_at(i, par, p, d):
                j, b, m = strip_at(i, par, (p + d) // PAIRS)
                pp = (p + d) % PAIRS
                return j, b, m, pp, PAIRS * m + pp

            def over_strips(eng, steps):
                steps(0)
                with eng.Fori(1, STRIPS - 1) as i:
                    steps(i)
                steps(STRIPS - 1)

            @block.sync
            def _(sp):
                sp.dma_start(LW[:], laT).then_inc(lw_in, 16)
                sp.dma_start(EW[:], expw).then_inc(lw_in, 16)
                sp.dma_start(RW[:], rw).then_inc(lw_in, 16)
                sp.dma_start(RB[:], rb.broadcast_to([P, NE])).then_inc(lw_in, 16)
                sp.wait_ge(ebx_zero, 1)
                for t in range(T):
                    sp.dma_start(EBX[t * NE:(t + 1) * NE, t, :], expb).then_inc(ebx_in, 16)

            @block.gpsimd
            def _(pool):
                nc.gpsimd.memset(FR[:], 0.0).then_inc(frames_zero, 1)

                def table(i, par, d, rc):
                    s, b, m = strip_at(i, par, d)
                    if exists(s):
                        cls = (s > 0) + (s > STRIPS - 2) if isinstance(s, int) else (s + 7) // 8 + (s + 1) // 8
                        wait(pool, scored, 2 * PAIRS * (m - 1))
                        settle(pool, passed["pool"])
                        nc.gpsimd.tensor_copy(tcur[:, b, rc:rc + 1, :], tab[:, bass.ds(cls, 1), rc, :]).then_inc(table_ready, 1)

                def norm(i, par, p, d):
                    s, b, m, pp, g = pair_at(i, par, p, d)
                    if exists(s):
                        wait(pool, rec_done, g + 1)
                        wait(pool, p_turned, g - 1)
                        nc.gpsimd.tensor_tensor(frames[:, pp % 2], E[:, pp % 2],
                                                erec[:, pp % 2, :].unsqueeze(2).broadcast_to([P, 2, NK]),
                                                ALU.mult).then_inc(normed, 1)

                def steps(i):
                    for par in range(2):
                        for p in range(PAIRS):
                            norm(i, par, p, 1)
                            if p < 3:
                                table(i, par, 1, p)

                pool.wait_ge(frames_zero, 1)
                for rc in range(3):
                    table(0, 0, 0, rc)
                norm(0, 0, 0, 0)
                over_strips(pool, steps)

            @block.vector
            def _(dve):
                def strip(i, par, d):
                    s, b, m = strip_at(i, par, d)
                    if exists(s):
                        wait(dve, qv_made, 4 * (m - 1))
                        nc.vector.tensor_copy(ystrip[:, b], Y[:, b, :, bass.ds(s * QC, KC)]).then_inc(strip_ready, 1)

                def store_q(i, par, d, h):
                    s, b, m = strip_at(i, par, d)
                    if exists(s):
                        wait(dve, qv_made, 4 * m + 1)
                        wait(dve, s_made, PAIRS * (m - 1))
                        hs = slice(h * DH, (h + 1) * DH)
                        nc.vector.tensor_scalar(Q[hs, b, :, h, :], QV[0][hs, :].rearrange("p (t q) -> p t q", q=NQ),
                                                bq[hs, :], None, ALU.add).then_inc(q_ready, 1)

                def score(i, par, p, d):
                    s, b, m, pp, g = pair_at(i, par, p, d)
                    if exists(s):
                        wait(dve, s_made, g + 1)
                        wait(dve, exp_done, 2 * (g - 1))
                        wait(dve, table_ready, 3 * (m + 1))
                        settle(dve, passed["dve"])
                        for t in range(2):
                            tile = 2 * pp + t
                            rc = 0 if tile == 0 else 2 if tile == TILES - 1 else 1
                            nc.vector.tensor_tensor_reduce(
                                S[:, pp % 2, t, :], SP[pp % 2][:, t * NK:(t + 1) * NK], tcur[:, b, rc, :], 1.0, 3.0e38,
                                ALU.add, ALU.min, smin[:, pp % 2, t:t + 1]).then_inc(scored, 1)

                def recip(i, par, p, d):
                    s, b, m, pp, g = pair_at(i, par, p, d)
                    if exists(s):
                        wait(dve, exp_done, 2 * (g + 1))
                        wait(dve, normed, g - 1)
                        nc.vector.reciprocal(erec[:, pp % 2, :], esum[:, pp % 2, :]).then_inc(rec_done, 1)

                def steps(i):
                    for par in range(2):
                        for p in range(PAIRS):
                            recip(i, par, p, 1)
                            score(i, par, p, 3)
                            if 1 <= p <= HEADS:
                                store_q(i, par, 1, p - 1)
                            if p == 6:
                                strip(i, par, 2)

                strip(0, 0, 0)
                strip(0, 0, 1)
                for h in range(HEADS):
                    store_q(0, 0, 0, h)
                for p in range(3):
                    score(0, 0, p, 0)
                recip(0, 0, 0, 0)
                over_strips(dve, steps)

            @block.scalar
            def _(act):
                def store_v(i, par, d, group):
                    s, b, m = strip_at(i, par, d)
                    if exists(s):
                        wait(act, qv_made, 4 * m + 2 + group)
                        wait(act, pv_done, PAIRS * (m - 1))
                        nc.scalar.activation(V[:, b, VG * group:VG * group + VG, :],
                                             QV[VBANK[group]][0:CHK, 0:VG * P].rearrange("p (c n) -> p c n", c=VG),
                                             ACT.Copy).then_inc(v_ready, 1)

                def exps(i, par, p, d):
                    s, b, m, pp, g = pair_at(i, par, p, d)
                    if exists(s):
                        wait(act, scored, 2 * (g + 1))
                        wait(act, normed, g - 1)
                        wait(act, rec_done, g - 1)
                        for t in range(2):
                            nc.scalar.activation(E[:, pp % 2, t, :], S[:, pp % 2, t, :], ACT.Exp,
                                                 bias=smin[:, pp % 2, t:t + 1], scale=-1.0,
                                                 accum_out=esum[:, pp % 2, t:t + 1]).then_inc(exp_done, 1)

                def store_pt(i, par, p, d):
                    s, b, m, pp, g = pair_at(i, par, p, d)
                    if exists(s):
                        wait(act, p_turned, g + 1)
                        wait(act, pv_done, g - 1)
                        nc.scalar.activation(PT[:, pp % 2].rearrange("p c t n -> p (c t n)"), PP[pp % 2][0:CHK, :],
                                             ACT.Copy).then_inc(pt_ready, 1)

                def store_attn(i, par, d):
                    s, b, m = strip_at(i, par, d)
                    if exists(s):
                        wait(act, pv_done, PAIRS * (m + 1))
                        wait(act, strip_ready, m + 3 if not isinstance(m, int) else min(m + 3, NSTRIP))
                        nc.scalar.activation(Y[:, b, PADT:PADT + H, bass.ds(s * QC + R, QC)],
                                             OP[b][:].rearrange("p (r c) -> p r c", c=QC), ACT.Copy).then_inc(attn_stored, 1)

                def steps(i):
                    for par in range(2):
                        for p in range(PAIRS):
                            exps(i, par, p, 2)
                            store_pt(i, par, p, 0)
                            if p in (3, 5, 7):
                                store_v(i, par, 1, (p - 3) // 2)
                            if p == 1:
                                store_attn(i, par, -1)

                for group in range(3):
                    store_v(0, 0, 0, group)
                exps(0, 0, 0, 0)
                exps(0, 0, 1, 0)
                over_strips(act, steps)
                store_attn(STRIPS - 1, 1, 0)

            @block.tensor
            def _(pe):
                mm = nc.tensor.matmul

                def queries(i, par, d):
                    s, b, m = strip_at(i, par, d)
                    if exists(s):
                        wait(pe, strip_ready, m + 1)
                        wait(pe, v_ready, 3 * m)
                        mm(QV[0][:], WQ[:], ystrip[:, b, PADT:PADT + H, R:R + QC], start=True, stop=True).then_inc(qv_made, 1)

                def values(i, par, d, group):
                    s, b, m = strip_at(i, par, d)
                    if exists(s):
                        if group == 2:
                            wait(pe, q_ready, HEADS * (m + 1))
                        else:
                            wait(pe, v_ready, 3 * m + group)
                        for c in range(VG):
                            ch = VG * group + c
                            ins = mm(QV[VBANK[group]][0:CHK, c * P:(c + 1) * P],
                                     ystrip[:, b, CHR * ch:CHR * (ch + 1), :].rearrange("p r c -> p (r c)"), WV[:],
                                     start=True, stop=True)
                        ins.then_inc(qv_made, 1)

                def scores(i, par, p, d):
                    s, b, m, pp, g = pair_at(i, par, p, d)
                    if exists(s):
                        wait(pe, q_ready, HEADS * (m + 1))
                        wait(pe, scored, 2 * (g - 1))
                        for t in range(2):
                            tile = 2 * pp + t
                            ins = mm(SP[pp % 2][:, t * NK:(t + 1) * NK],
                                     Q[:, b, tile].rearrange("p h q -> p (h q)"),
                                     KEY[:, b, QR * tile:QR * tile + KR, bass.ds(s * QC, KC)], start=True, stop=True)
                        ins.then_inc(s_made, 1)

                def turn(i, par, p, d):
                    s, b, m, pp, g = pair_at(i, par, p, d)
                    if exists(s):
                        wait(pe, normed, g + 1)
                        wait(pe, pt_ready, g - 1)
                        for c in range(2):
                            for t in range(2):
                                at = (2 * c + t) * P
                                ins = nc.tensor.transpose(PP[pp % 2][0:CHK, at:at + P],
                                                          FR[:, pp % 2, (2 * t + c) * CHK:(2 * t + c + 1) * CHK], ident)
                        ins.then_inc(p_turned, 1)

                def weigh(i, par, p, d):
                    s, b, m, pp, g = pair_at(i, par, p, d)
                    if exists(s):
                        wait(pe, pt_ready, g + 1)
                        wait(pe, v_ready, 3 * (m + 1))
                        if pp == 0:
                            wait(pe, attn_stored, m - 1)
                        for h in range(HEADS):
                            hs = slice(h * DH, (h + 1) * DH)
                            for c in range(2):
                                ins = mm(OP[b][hs, 2 * NQ * pp:2 * NQ * (pp + 1)], V[:, b, pp + c, hs],
                                         PT[:, pp % 2, c, :, hs], start=c == 0, stop=c == 1, tile_position=(0, h * DH))
                        ins.then_inc(pv_done, 1)

                def steps(i):
                    for par in range(2):
                        for p in range(PAIRS):
                            turn(i, par, p, 0)
                            scores(i, par, p, 3)
                            weigh(i, par, p, -1)
                            if p == 0:
                                queries(i, par, 1)
                            if p in (2, 4, 6):
                                values(i, par, 1, (p - 2) // 2)

                queries(0, 0, 0)
                for group in range(3):
                    values(0, 0, 0, group)
                for p in range(3):
                    scores(0, 0, p, 0)
                over_strips(pe, steps)
                weigh(STRIPS - 1, 1, PAIRS - 1, 0)

        attn_mem.close()
        with ExitStack() as mem:
            per = {}

            def counter(name, n=1):
                s = sem(name)
                per[name] = (s, n)
                return s

            def done(eng, name, m, n=None):
                s, each = per[name]
                m = min(m, NBLK - 1) if isinstance(m, int) else m
                wait(eng, s, each * m + (each if n is None else n))

            def two(name, shape=(BLK,)):
                return sb(mem, name, [P, B, *shape])

            def one(name):
                return sb(mem, name, [P, 1, BLK])[:].broadcast_to([P, B, BLK])

            aslot = two("aslot")
            xslot, xs, rT, xn, xnT, uT = (one(n) for n in ("xslot", "xs", "rT", "xn", "xnT", "uT"))
            xT, x1b = two("xT"), two("x1b")
            x1, t0, t1 = two("x1"), two("t0"), two("t1")
            tn, tnT, eq, ek, rq, rk, qf, kf, kt, am = (
                one(n) for n in ("tn", "tnT", "eq", "ek", "rq", "rk", "qf", "kf", "kt", "am"))
            den, rden = two("den", (T,)), two("rden", (T,))
            td, osum = one("td"), one("osum")
            tdT, base, acc, oT = (two(n) for n in ("tdT", "base", "acc", "oT"))
            prod = sb(mem, "prod", [P, 2, 4, P])
            half = sb(mem, "half", [P, 2, 2, P])
            psum4 = two("psum4")
            gate = two("gate", (T, NE))
            gateT = sb(mem, "gateT", [T * NE, B, P])
            lg, is1, w1_, first, lg2, is2, w2_, second, ga, gb = (
                two(n, (T, NE)) for n in ("lg", "is1", "wt1", "first", "lg2", "is2", "wt2", "second", "ga", "gb"))
            top1, best1, top2, best2, gap, e2, dn, g1, g2 = (
                two(n, (T,)) for n in ("top1", "best1", "top2", "best2", "gap", "e2", "dn", "gt1", "gt2"))
            NORMS = {2: "p", 3: "x1", 4: "u", 5: "t0", 6: "t1"}
            bn = {k: two(f"bn{k}", (T, 6)) for k in NORMS}
            mvs = {k: two(f"mvs{k}", (T, 2)) for k in NORMS}
            ve = {k: two(f"ve{k}", (T,)) for k in NORMS}
            rs = {k: two(f"rs{k}", (T,)) for k in NORMS}
            nb = {k: two(f"nb{k}", (T,)) for k in (3, 5, 6)}
            nm = {k: two(f"nm{k}", (T,)) for k in nb}
            G = [ps(mem, f"G{i}") for i in range(5)]
            M = [ps(mem, f"M{i}") for i in range(2)]
            SPS = ps(mem, "SPS")

            state_zero = sem("state_zero")
            gn_turned, gn_rows_ready = sem("gn_turned"), sem("gn_rows_ready")
            gn_rows = sb(mem, "gn_rows", [P, 2, B, P])
            stored = [sem(f"stored{b}") for b in range(B)]
            for name, n in dict(a_copied=1, x_made=1, xt_made=1, xT_ready=1, xs_ready=1, rT_ready=1, z1_made=1, x1_ready=T, x1b_ready=1,
                                xn_ready=T, xn_turned=1, xnT_ready=1, z2_made=1, u_turned=1, uT_ready=1,
                                z3_made=1, t0_ready=T, p_made=1, tn_ready=T, tn_turned=1, tnT_ready=1, q_made=1,
                                k_made3=1, v_made=1, e_ready=4, v_stored=1, f_ready=2, k_turned=1, kt_ready=1,
                                a_made=1, a_masked=1, num_made=T, state_made=T, state_ready=T, den_ready=2, rden_ready=1,
                                t1_ready=T, td_ready=T, td_turned=1, tdT_ready=1, logits_made=1, gated=1, e2_ready=1,
                                gate_steps=18, g_turned=1, gT_ready=1, eb_made=1, moe_made=2 * T, prods=4 * T, sums=2 * T,
                                chain=4 * T, base_ready=1, osum_ready=1, o_turned=1, oT_ready=1).items():
                counter(name, n)
            for k in NORMS:
                counter(f"stats{k}", T)
                counter(f"mv{k}", T)
                counter(f"ve{k}", 2 if k in nb else 1)
                counter(f"rs{k}", 1)
            for k in nb:
                counter(f"nb{k}", 1)

            inc = lambda ins, name: ins.then_inc(per[name][0], 1)
            tile = lambda t: slice(t * P, (t + 1) * P)
            NPAIR = NBLK // B
            LAG = dict(pre=0, a=1, b=2, e=3, c=4, g=5, d=6, h=7, o=8)
            PEEL = 5

            def over_blocks(eng, steps):
                for i in range(PEEL):
                    steps(i)
                with eng.Fori(PEEL, NPAIR) as i:
                    steps(i)
                for i in range(NPAIR, NPAIR + LAG["o"] // 2):
                    steps(i)

            def stream(i, par, name):
                j, b = shift(i, par - LAG[name])
                return (j, b, B * j + b) if exists(j) else None

            def over(i, par, name="c"):
                return isinstance(i, int) and 2 * i + par - LAG[name] >= NBLK

            def router_bank(i, par):
                return G[0] if over(i, par) else G[3]

            def gate_bank(i, par):
                return G[3] if over(i, par, "g") else M[1]

            def expert_banks(i, par, t):
                return (G[1], G[2]) if over(i, par) and t % 2 else (M[0], M[1])

            block = mem.enter_context(nc.Block())

            @block.sync
            def _(sp):
                def steps(i):
                    for par in range(2):
                        if s := stream(i, par, "o"):
                            j, b, m = s
                            done(sp, "oT_ready", m)
                            sp.dma_start(out[b][:, bass.ds(j * BLK, BLK)], oT[:, b, :]).then_inc(stored[b], 16)

                over_blocks(sp, steps)
                for b in range(B):
                    sp.wait_ge(stored[b], 16 * NPAIR)

            @block.gpsimd
            def _(pool):
                tt = nc.gpsimd.tensor_tensor
                def rstd(k, s, readers):
                    if s:
                        j, b, m = s
                        done(pool, f"mv{k}", m)
                        done(pool, f"rs{k}", m - 2)
                        inc(tt(ve[k][:, b, :], mvs[k][:, b, :, 1], eps[:], ALU.add), f"ve{k}")
                        if k in nb:
                            done(pool, f"nb{k}", m - 2)
                            inc(tt(nm[k][:, b, :], mvs[k][:, b, :, 0], minus[:], ALU.mult), f"ve{k}")
                        done(pool, f"ve{k}", m, 1)
                        done(pool, readers, m - 2)
                        inc(tt(rs[k][:, b, :], ve[k][:, b, :], halfneg[:], ALU.pow), f"rs{k}")
                        if k in nb:
                            done(pool, f"rs{k}", m)
                            done(pool, f"ve{k}", m)
                            inc(tt(nb[k][:, b, :], nm[k][:, b, :], rs[k][:, b, :], ALU.mult), f"nb{k}")

                def sums(s, t):
                    if s:
                        j, b, m = s
                        done(pool, "prods", m, 4 * t + 4)
                        inc(tt(half[:, t % 2], prod[:, t % 2, 0:2, :], prod[:, t % 2, 2:4, :], ALU.add), "sums")
                        done(pool, "sums", m, 2 * t + 1)
                        done(pool, "osum_ready", m - 2)
                        inc(tt(psum4[:, b, tile(t)], half[:, t % 2, 0, :], half[:, t % 2, 1, :], ALU.add), "sums")

                def steps(i):
                    for par in range(2):
                        pre, a, b_, e, c, g, d, h, o = (stream(i, par, n) for n in LAG)
                        if a:
                            j, b, m = a
                            done(pool, "xt_made", m - 1)
                            inc(tt(xslot[:, b, :], X[:, b, bass.ds(j * BLK, BLK)], b3[:].broadcast_to([P, BLK]), ALU.add),
                                "x_made")
                        rstd(3, b_, "xn_ready")
                        rstd(4, e, "t0_ready")
                        rstd(6, g, "td_ready")
                        sums(h, 0)
                        if a:
                            j, b, m = a
                            wide = lambda k: gn_rows[:, k, b:b + 1, :].broadcast_to([P, T, P])
                            tiled = lambda v: v.rearrange("p (t n) -> p t n", t=T)
                            done(pool, "xT_ready", m)
                            done(pool, "rT_ready", m - 1)
                            inc(tt(tiled(xs[:, b, :]), tiled(xT[:, b, :]), wide(0), ALU.mult), "xs_ready")
                            done(pool, "xs_ready", m)
                            done(pool, "x1_ready", m - 1)
                            inc(tt(tiled(rT[:, b, :]), tiled(xs[:, b, :]), wide(1), ALU.add), "rT_ready")
                        rstd(5, e, "tn_ready")
                        sums(h, 1)
                        sums(h, 2)
                        rstd(2, a, "x1_ready")
                        sums(h, 3)
                        if h:
                            j, b, m = h
                            done(pool, "chain", m)
                            done(pool, "sums", m)
                            done(pool, "o_turned", m - 1)
                            inc(tt(osum[:, b, :], acc[:, b, :], psum4[:, b, :], ALU.add), "osum_ready")

                pool.wait_ge(preset, 5)
                pool.wait_ge(gn_rows_ready, 1)
                over_blocks(pool, steps)

            @block.scalar
            def _(act):
                copy = lambda dst, src: nc.scalar.activation(dst, src, ACT.Copy)

                def apply(k, s, dst, src, name, reader, tiles=range(T)):
                    if s:
                        j, b, m = s
                        done(act, f"nb{k}", m)
                        done(act, reader, m - 1)
                        for t in tiles:
                            inc(nc.scalar.activation(dst[:, b, tile(t)], src[:, b, tile(t)], ACT.Identity,
                                                     bias=nb[k][:, b, t:t + 1], scale=rs[k][:, b, t:t + 1]), name)

                def evacuate(s, dst, src, made, name, reader, depth=1):
                    if s:
                        j, b, m = s
                        done(act, made, m)
                        done(act, reader, m - depth)
                        inc(copy(dst[:, b, :], src[:]), name)

                def experts(s, t, bank):
                    if s:
                        j, b, m = s
                        done(act, "gated", m)
                        done(act, "moe_made", m, 2 * t + 1)
                        if t >= 2:
                            done(act, "sums", m, 2 * (t - 2) + 1)
                        else:
                            done(act, "sums", m - 1, 2 * (t + 2) + 1)
                        for e in range(4):
                            inc(nc.scalar.activation(prod[:, t % 2, e, :], bank[:, tile(e)], ACT.Copy,
                                                     scale=gate[:, b, t, e:e + 1]), "prods")

                def features(s, n, bank, made, bias, e, r):
                    if s:
                        j, b, m = s
                        bias = vec[:, VI[bias]:VI[bias] + 1]
                        done(act, made, m)
                        done(act, "f_ready", m - 1)
                        inc(nc.scalar.activation(e[:, b, :], bank[:], ACT.Exp, bias=bias), "e_ready")
                        inc(nc.scalar.activation(r[:, b, :], bank[:], ACT.Relu, bias=bias), "e_ready")

                def store_o(s):
                    if s:
                        j, b, m = s
                        done(act, "o_turned", m)
                        wait(act, stored[b], 16 * j)
                        inc(copy(oT[:, b, :], G[4][:]), "oT_ready")

                def gate_exp(s):
                    if s:
                        j, b, m = s
                        done(act, "gate_steps", m, 13)
                        done(act, "gated", m - 2)
                        inc(nc.scalar.activation(e2[:, b, :], gap[:, b, :], ACT.Exp), "e2_ready")

                def running(s, tiles):
                    if s:
                        j, b, m = s
                        for t in tiles:
                            done(act, "state_made", m, t + 1)
                            done(act, "num_made", m, t)
                            inc(copy(state[:, b, (t + 1) % 2, :], SPS[:, b * (P + 1):(b + 1) * (P + 1)]), "state_ready")

                def steps(i):
                    for par in range(2):
                        pre, a, b_, e, c, g, d, h, o = (stream(i, par, n) for n in LAG)
                        evacuate(e, xnT, G[2], "xn_turned", "xnT_ready", "z2_made")
                        if over(i, par):
                            evacuate(d, tdT, router_bank(i, par), "td_turned", "tdT_ready", "moe_made", depth=2)
                        if not over(i, par, "b"):
                            gate_exp(h)
                        running(g, (0,))
                        if over(i, par, "b") and not over(i, par - 1):
                            gate_exp(h)
                        if e:
                            j, b, m = e
                            done(act, "z2_made", m)
                            done(act, "z3_made", m - 1)
                            done(act, "u_turned", m - 1)
                            inc(nc.scalar.activation(uT[:, b, :], G[2][:], ACT.Relu, bias=b2[:]), "uT_ready")
                        running(g, (1,))
                        if not over(i, par):
                            store_o(o)
                        if h:
                            j, b, m = h
                            done(act, "g_turned", m)
                            done(act, "eb_made", m - 2)
                            inc(copy(gateT[:, b, :], gate_bank(i, par)[0:T * NE, 0:P]), "gT_ready")
                        apply(5, c, tn, t0, "tn_ready", "tn_turned", (0, 1))
                        running(g, (2,))
                        apply(5, c, tn, t0, "tn_ready", "tn_turned", (2, 3))
                        running(g, (3,))
                        experts(h, 0, expert_banks(i, par, 0)[0])
                        if over(i, par):
                            store_o(o)
                        evacuate(c, tnT, G[0], "tn_turned", "tnT_ready", "v_made")
                        apply(3, b_, xn, x1, "xn_ready", "xn_turned")
                        evacuate(a, xT, G[1], "xt_made", "xT_ready", "x1b_ready", depth=2)
                        experts(h, 1, expert_banks(i, par, 1)[0])
                        if over(i, par):
                            apply(6, g, td, t1, "td_ready", "td_turned")
                            gate_exp(d)
                        features(c, 0, G[0], "q_made", "lbq", eq, rq)
                        if not over(i, par):
                            evacuate(d, tdT, router_bank(i, par), "td_turned", "tdT_ready", "moe_made", depth=2)
                        features(c, 1, G[1], "k_made3", "lbk", ek, rk)
                        if not over(i, par):
                            apply(6, g, td, t1, "td_ready", "td_turned")
                        experts(h, 2, expert_banks(i, par, 2)[0])
                        if c:
                            j, b, m = c
                            done(act, "v_made", m)
                            done(act, "num_made", m - 2)
                            inc(copy(va[:, b, :, 0:P], G[4][:].rearrange("p (t n) -> p t n", t=T)), "v_stored")
                        evacuate(c, kt, G[0], "k_turned", "kt_ready", "state_made")
                        experts(h, 3, expert_banks(i, par, 3)[0])

                act.wait_ge(preset, 5)
                act.wait_ge(gn_turned, 1)
                copy(gn_rows[:].rearrange("p k b n -> p (k b n)"), G[4][:]).then_inc(gn_rows_ready, 1)
                over_blocks(act, steps)

            @block.vector
            def _(dve):
                tt, stt, ts = nc.vector.tensor_tensor, nc.vector.scalar_tensor_tensor, nc.vector.tensor_scalar

                def stats(k, s, src, made, between=lambda: None):
                    if s:
                        j, b, m = s
                        done(dve, made, m)
                        done(dve, f"mv{k}", m - 2)
                        for t in range(T):
                            inc(nc.vector.bn_stats(bn[k][:, b, t, :], src(b, t)), f"stats{k}")
                            between()
                        done(dve, f"nb{k}" if k in nb else f"rs{k}", m - 2)
                        done(dve, f"stats{k}", m)
                        settle(dve, passed["dve"])
                        for t in range(T):
                            inc(nc.vector.bn_aggr(mvs[k][:, b, t, :], bn[k][:, b, t, :]), f"mv{k}")

                def experts(s, t, bank, between=lambda: None):
                    if s:
                        j, b, m = s
                        done(dve, "moe_made", m, 2 * t + 2)
                        done(dve, "gated", m)
                        done(dve, "base_ready", m)
                        done(dve, "osum_ready", m - 2)
                    for e in range(4):
                        if s:
                            if e:
                                done(dve, "chain", m, 4 * t + e)
                            inc(stt(acc[:, b, tile(t)], bank[:, tile(e)], gate[:, b, t, 4 + e:5 + e],
                                    (acc if e else base)[:, b, tile(t)], ALU.mult, ALU.add), "chain")
                        between()

                def gating(s, n, bank=None):
                    if not s:
                        return
                    j, b, m = s
                    wide = lambda v: v[:, b, :].unsqueeze(2).broadcast_to([P, T, NE])

                    def pick(n, logits, top, same, weight, best, chosen):
                        if n == 0:
                            return nc.vector.tensor_reduce(top[:, b, :], logits[:, b], AX_X, ALU.max)
                        if n == 1:
                            return tt(same[:, b], logits[:, b], wide(top), ALU.is_equal)
                        if n == 2:
                            return tt(weight[:, b], same[:, b], rank[:], ALU.mult)
                        if n == 3:
                            return nc.vector.tensor_reduce(best[:, b, :], weight[:, b], AX_X, ALU.max)
                        return tt(chosen[:, b], weight[:, b], wide(best), ALU.is_equal)

                    if n == 0:
                        done(dve, "logits_made", m)
                        done(dve, "gated", m - 2)
                        done(dve, "e2_ready", m - 2)
                        ins = tt(lg[:, b], bank[:, 0:T * NE].rearrange("p (t e) -> p t e", t=T),
                                 RB[:].unsqueeze(1).broadcast_to([P, T, NE]), ALU.add)
                    else:
                        done(dve, "gate_steps", m, n)
                    if 1 <= n <= 5:
                        ins = pick(n - 1, lg, top1, is1, w1_, best1, first)
                    elif n == 6:
                        ins = stt(lg2[:, b], first[:, b], -3.0e38, lg[:, b], ALU.mult, ALU.add)
                    elif 7 <= n <= 11:
                        ins = pick(n - 7, lg2, top2, is2, w2_, best2, second)
                    elif n == 12:
                        ins = tt(gap[:, b, :], top2[:, b, :], top1[:, b, :], ALU.subtract)
                    elif n == 13:
                        done(dve, "e2_ready", m)
                        ins = nc.vector.tensor_scalar_add(dn[:, b, :], e2[:, b, :], 1.0)
                    elif n == 14:
                        ins = nc.vector.reciprocal(g1[:, b, :], dn[:, b, :])
                    elif n == 15:
                        ins = tt(g2[:, b, :], g1[:, b, :], e2[:, b, :], ALU.mult)
                    elif n == 16:
                        ins = tt(ga[:, b], first[:, b], wide(g1), ALU.mult)
                    elif n == 17:
                        ins = tt(gb[:, b], second[:, b], wide(g2), ALU.mult)
                    elif n == 18:
                        done(dve, "prods", m - 2)
                        done(dve, "g_turned", m - 2)
                        done(dve, "chain", m - 2)
                        inc(tt(gate[:, b], ga[:, b], gb[:, b], ALU.add), "gated")
                        return
                    inc(ins, "gate_steps")

                LATE = 13

                def features(s, n, e, r, f):
                    if s:
                        j, b, m = s
                        done(dve, "e_ready", m, 2 * n + 2)
                        done(dve, "a_made", m - 1)
                        done(dve, "num_made", m - 1)
                        inc(stt(f[:, b, :], e[:, b, :], 1.0, r[:, b, :], ALU.min, ALU.add), "f_ready")

                def steps(i):
                    for par in range(2):
                        pre, a, b_, e, c, g, d, h, o = (stream(i, par, n) for n in LAG)
                        late = [] if over(i, par - 1) else list(range(LATE, per["gate_steps"][1] + 1))
                        last = per["gate_steps"][1] + 1 if over(i, par) else LATE
                        n = 0

                        def gate_step():
                            nonlocal n
                            if n < last:
                                gating(d, n, router_bank(i, par))
                                n += 1

                        def early_gate_step():
                            if over(i, par):
                                gate_step()
                                gate_step()


                        def late_gate_step():
                            if late:
                                gating(h, late.pop(0))

                        if b_:
                            j, b, m = b_
                            done(dve, "rT_ready", m)
                            done(dve, "z1_made", m)
                            done(dve, "rs2", m)
                            done(dve, "xn_ready", m - 2)
                            done(dve, "x1b_ready", m - 2)
                        for t in range(T):
                            if b_:
                                inc(stt(x1[:, b, tile(t)], G[1][:, tile(t)], rs[2][:, b, t:t + 1], rT[:, b, tile(t)],
                                        ALU.mult, ALU.add), "x1_ready")
                            late_gate_step()
                        stats(3, b_, lambda b, t: x1[:, b, tile(t)], "x1_ready", late_gate_step)
                        while late:
                            late_gate_step()
                        if b_:
                            j, b, m = b_
                            done(dve, "xT_ready", m)
                            done(dve, "t0_ready", m - 2)
                            inc(tt(x1b[:, b, :], x1[:, b, :], xT[:, b, :], ALU.add), "x1b_ready")
                        if pre:
                            j, b, m = pre
                            done(dve, "z1_made", m - 2)
                            inc(nc.vector.tensor_copy(aslot[:, b, :].rearrange("p (r c) -> p r c", c=W),
                                                      Y[:, b, bass.ds(j * BROWS + PADT, BROWS), R:R + W]), "a_copied")
                        stats(4, e, lambda b, t: G[2][:, tile(t)], "u_turned")
                        if h:
                            j, b, m = h
                            done(dve, "eb_made", m)
                            done(dve, "chain", m - 2)
                            inc(tt(base[:, b, :], t1[:, b, :], gate_bank(i, par)[:], ALU.add), "base_ready")
                        if g:
                            j, b, m = g
                            done(dve, "num_made", m)
                            done(dve, "rden_ready", m - 2)
                            for half_of, bank in enumerate((G[3], G[4])):
                                inc(nc.vector.tensor_scalar_add(
                                    den[:, b, 2 * half_of:2 * half_of + 2],
                                    bank[:, 0:2 * (P + 1)].rearrange("p (t n) -> p t n", t=2)[:, :, P], 1e-6), "den_ready")
                            done(dve, "den_ready", m)
                            done(dve, "t1_ready", m - 2)
                            inc(nc.vector.reciprocal(rden[:, b, :], den[:, b, :]), "rden_ready")
                            done(dve, "rden_ready", m)
                            done(dve, "base_ready", m - 2)
                            done(dve, "td_ready", m - 2)
                            for t in range(T):
                                bank, at = (G[3], G[4])[t // 2], (t % 2) * (P + 1)
                                inc(stt(t1[:, b, tile(t)], bank[:, at:at + P], rden[:, b, t:t + 1], t0[:, b, tile(t)],
                                        ALU.mult, ALU.add), "t1_ready")
                        if over(i, par):
                            stats(6, g, lambda b, t: t1[:, b, tile(t)], "t1_ready")
                        experts(h, 0, expert_banks(i, par, 0)[1], early_gate_step)
                        if not over(i, par):
                            stats(6, g, lambda b, t: t1[:, b, tile(t)], "t1_ready")
                        if e:
                            j, b, m = e
                            done(dve, "z3_made", m)
                            done(dve, "rs4", m)
                            done(dve, "x1b_ready", m)
                            done(dve, "t1_ready", m - 2)
                            for t in range(T):
                                inc(stt(t0[:, b, tile(t)], G[2][:, tile(t)], rs[4][:, b, t:t + 1], x1b[:, b, tile(t)],
                                        ALU.mult, ALU.add), "t0_ready")
                        experts(h, 1, expert_banks(i, par, 1)[1], early_gate_step)
                        stats(5, e, lambda b, t: t0[:, b, tile(t)], "t0_ready")
                        features(c, 0, eq, rq, qf)
                        features(c, 1, ek, rk, kf)
                        experts(h, 2, expert_banks(i, par, 2)[1], gate_step)
                        stats(2, a, lambda b, t: G[2][:, tile(t)], "p_made", gate_step)
                        while n < 8:
                            gate_step()
                        if c:
                            j, b, m = c
                            done(dve, "a_made", m)
                            done(dve, "num_made", m - 1)
                            inc(tt(am[:, b, :].rearrange("p (t n) -> p t n", t=T),
                                   G[1][:].rearrange("p (t n) -> p t n", t=T),
                                   causal.unsqueeze(1).broadcast_to([P, T, P]), ALU.mult), "a_masked")
                        experts(h, 3, expert_banks(i, par, 3)[1], gate_step)
                        gate_step()
                        gate_step()
                        gate_step()
                        while n < last:
                            gate_step()

                dve.wait_ge(lw_in, 64)
                dve.wait_ge(preset, 5 + NE)
                over_blocks(dve, steps)

            @block.tensor
            def _(pe):
                mm, turn = nc.tensor.matmul, nc.tensor.transpose

                def bias(bank, name):
                    mm(bank[:].rearrange("p (t n) -> p t n", t=T), ones3[:],
                       bias3[:, BIAS.index(name)].unsqueeze(1).broadcast_to([96, T, P]), start=True, stop=False,
                       skip_group_check=True)

                def linear(bank, src, b, w, last=True):
                    for t in range(T):
                        ins = mm(bank[:, tile(t)], src[:, b, tile(t)], w, start=False, stop=True, skip_group_check=True)
                    return ins

                def turned(s, bank, src, ready, released, name):
                    if s:
                        j, b, m = s
                        done(pe, ready, m)
                        released(m)
                        for t in range(T):
                            ins = turn(bank[:, tile(t)], src[:, b, tile(t)], ident)
                        inc(ins, name)

                def experts(s, t, banks, spare, i, par):
                    if s:
                        j, b, m = s
                        done(pe, "tdT_ready", m)
                        n = 4 * max(t - 1, 0) if spare else 4 * t
                        done(pe, "prods", m, n)
                        inc(mm(banks[0][:], tdT[:, b, tile(t)], EW[:, 0:BLK], start=True, stop=True), "moe_made")
                        done(pe, "chain", m, n)
                        if t or not over(i, par, "g"):
                            done(pe, "base_ready", m)
                        inc(mm(banks[1][:], tdT[:, b, tile(t)], EW[:, BLK:], start=True, stop=True), "moe_made")

                def logits(s, bank):
                    if s:
                        j, b, m = s
                        done(pe, "tdT_ready", m)
                        for t in range(T):
                            ins = mm(bank[:, t * NE:(t + 1) * NE], tdT[:, b, tile(t)], RW[:], start=True, stop=True)
                        inc(ins, "logits_made")

                def num(s, tiles):
                    if s:
                        j, b, m = s
                        mine = slice(b * (P + 1), (b + 1) * (P + 1))
                        for t in tiles:
                            out = (G[3], G[4])[t // 2][:, (t % 2) * (P + 1):(t % 2 + 1) * (P + 1)]
                            mm(out, am[:, b, tile(t)], va[:, b, t, :], start=True, stop=False)
                            if t:
                                done(pe, "state_ready", m, t)
                            else:
                                done(pe, "state_ready", m - 1)
                            inc(mm(SPS[:, mine], kt[:, b, tile(t)], va[:, b, t, :], start=False, stop=True,
                                   skip_group_check=True), "state_made")
                            inc(mm(out, qf[:, b, tile(t)], state[:, b, t % 2, :], start=False, stop=True), "num_made")

                def steps(i):
                    for par in range(2):
                        pre, a, b_, e, c, g, d, h, o = (stream(i, par, n) for n in LAG)
                        turned(e, G[2], xn, "xn_ready", lambda m: done(pe, "stats2", m + 1), "xn_turned")
                        if b_:
                            j, b, m = b_
                            done(pe, "a_copied", m)
                            done(pe, "a_masked", m - 3)
                            done(pe, "xT_ready", m)
                            bias(G[1], "z1")
                            inc(linear(G[1], aslot, b, WPZ[:]), "z1_made")
                        if over(i, par) and d:
                            for name in ("kt_ready", "a_masked", "v_stored", "t0_ready"):
                                done(pe, name, NBLK - 1)
                            done(pe, "gate_steps", d[2] - 1, 1)
                            turned(d, G[0], td, "td_ready", lambda m: None, "td_turned")
                            logits(d, G[0])
                        if g:
                            j, b, m = g
                            done(pe, "kt_ready", m)
                            done(pe, "a_masked", m)
                            done(pe, "v_stored", m)
                            done(pe, "gate_steps", m - 2, 1)
                        num(g, (0,))
                        if e:
                            j, b, m = e
                            done(pe, "xnT_ready", m)
                            inc(mm(G[2][:], W2[:], xnT[:, b, :], start=True, stop=True), "z2_made")
                        num(g, (1,))
                        if not over(i, par):
                            turned(o, G[4], osum, "osum_ready", lambda m: done(pe, "v_stored", m + 3), "o_turned")
                        if h:
                            j, b, m = h
                            done(pe, "gated", m)
                            done(pe, "chain", m - 1)
                            inc(turn(gate_bank(i, par)[0:T * NE, 0:P], gate[:, b].rearrange("p t e -> p (t e)"), ident), "g_turned")
                        if over(i, par, "g"):
                            experts(h, 0, expert_banks(i, par, 0), True, i, par)
                        turned(e, G[2], uT, "uT_ready", lambda m: None, "u_turned")
                        if g:
                            done(pe, "oT_ready", g[2] - (4 if over(i, par) else 3))
                        num(g, (2,))
                        if h:
                            j, b, m = h
                            done(pe, "gT_ready", m)
                            inc(mm(gate_bank(i, par)[:], gateT[:, b, :], EBX[:].rearrange("p t n -> p (t n)"), start=True, stop=True),
                                "eb_made")
                        num(g, (3,))
                        if not over(i, par, "g"):
                            experts(h, 0, expert_banks(i, par, 0), over(i, par), i, par)
                        if over(i, par):
                            turned(o, G[4], osum, "osum_ready", lambda m: done(pe, "t1_ready", NBLK - 1), "o_turned")
                        turned(c, G[0], tn, "tn_ready", lambda m: done(pe, "kt_ready", m - 1), "tn_turned")
                        turned(a, G[1], xslot, "x_made", lambda m: done(pe, "x1_ready", m - 1), "xt_made")
                        if e:
                            j, b, m = e
                            done(pe, "stats4", m)
                            for t in range(T):
                                ins = mm(G[2][:, tile(t)], uT[:, b, tile(t)], W3[:], start=True, stop=True)
                            inc(ins, "z3_made")
                        experts(h, 1, expert_banks(i, par, 1), over(i, par), i, par)
                        if c:
                            j, b, m = c
                            done(pe, "tnT_ready", m)
                            inc(mm(G[0][:], LW[:, 0, :], tnT[:, b, :], start=True, stop=True), "q_made")
                        if not over(i, par):
                            turned(d, G[3], td, "td_ready", lambda m: done(pe, "t1_ready", m + 1), "td_turned")
                        if c:
                            j, b, m = c
                            done(pe, "xT_ready", m + 3)
                            inc(mm(G[1][:], LW[:, 1, :], tnT[:, b, :], start=True, stop=True), "k_made3")
                        experts(h, 2, expert_banks(i, par, 2), over(i, par), i, par)
                        if not over(i, par):
                            logits(d, G[3])
                        if c:
                            j, b, m = c
                            done(pe, "t1_ready", m - 1)
                            bias(G[4], "v")
                            inc(linear(G[4], tnT, b, LW[:, 2, :]), "v_made")
                        if a:
                            j, b, m = a
                            done(pe, "a_copied", m)
                            done(pe, "t0_ready", m - 2)
                            done(pe, "stats2", m - 1)
                            bias(G[2], "p")
                            inc(linear(G[2], aslot, b, WP), "p_made")
                        turned(c, G[0], kf, "f_ready", lambda m: None, "k_turned")
                        if c:
                            j, b, m = c
                            for t in range(T):
                                ins = mm(G[1][:, tile(t)], kf[:, b, tile(t)], qf[:, b, tile(t)], start=True, stop=True)
                            inc(ins, "a_made")
                        experts(h, 3, expert_banks(i, par, 3), over(i, par), i, par)

                pe.wait_ge(lw_in, 64)
                pe.wait_ge(ebx_in, 64)
                pe.wait_ge(gn_wide, 2 * B)
                for n in range(2 * B):
                    ins = turn(G[4][:, tile(n)], wide_in[:, n // B, n % B, :], ident)
                ins.then_inc(gn_turned, 1)
                pe.wait_ge(preset, 5)
                mm(SPS[:, 0:B * (P + 1)], ones3[:], zero3[:], start=True, stop=True).then_inc(state_zero, 1)
                pe.wait_ge(state_zero, 1)
                over_blocks(pe, steps)


def constants():
    eye = np.eye(P, dtype=np.float32)
    group = np.kron(np.eye(GROUPS), np.full((C // GROUPS, C // GROUPS), GROUPS / C)).astype(np.float32)
    center = (np.eye(P) - np.full((P, P), 1.0 / P)).astype(np.float32)
    causal = np.triu(np.ones((P, P), np.float32))
    return np.concatenate([eye, group, center, causal], axis=1)


def kernel(**inputs):
    import concourse.bacc as bacc
    from concourse.bass_utils import run_bass_kernel_spmd as run

    g = {k: np.asarray(v) for k, v in inputs.items()}
    L0, L1 = "L0_conv_", "L1_"
    qkvb, lab = g[L0 + "qkv_b"], g[L1 + "attn_b"]
    col = {**{n: g[L0 + n] for n in ("g1", "be1", "g2", "be2", "g3", "be3", "g4", "be4", "bl1", "bl2", "bl3")},
           "bq": qkvb[0:C], "bk": qkvb[C:2 * C], "bv": qkvb[2 * C:], "bp": g[L0 + "proj_b"],
           "lbq": lab[0:C], "lbk": lab[C:2 * C]}
    side = lambda ws: np.stack([w.T for w in ws], axis=1)
    arrays = {
        "x": g["x"].reshape(B, C, TOK),
        "kept": np.concatenate([np.stack([col[n] for n in VEC], axis=1), g[L0 + "proj_w"].T, constants()], axis=1),
        "prep": side(np.split(g[L0 + "qkv_w"], 3) + [g[L0 + "w1"], g[L0 + "w2"], g[L0 + "w3"], g[L0 + "proj_w"].T]),
        "rows": np.stack([g[L0 + "proj_b"], lab[2 * C:]])[None],
        "rpb": g[L0 + "rpb"],
        "laT": side(np.split(g[L1 + "attn_W"], 3)),
        "expw": g[L1 + "ffn_expert_w"].transpose(1, 0, 2).reshape(C, NE * C),
        "rw": g[L1 + "ffn_router_w"],
        "rb": g[L1 + "ffn_router_b"].reshape(1, NE),
        "expb": g[L1 + "ffn_expert_b"],
    }
    arrays = {k: np.ascontiguousarray(v) for k, v in arrays.items()}
    nc = bacc.Bacc("TRN2", target_bir_lowering=False, num_devices=1)
    args = {k: nc.dram_tensor("in_" + k, v.shape, mybir.dt.from_np(v.dtype), kind="ExternalInput").ap()
            for k, v in arrays.items()}
    out = nc.dram_tensor("out", (B, C, TOK), F32, kind="ExternalOutput").ap()
    build(nc, out=out, **args)
    r = run(nc, [{"in_" + k: v for k, v in arrays.items()}], core_ids=[0])
    return r.results[0]["out"].reshape(B, C, H, W)
```
